# Optimizing a Trainium2 kernel written in Bass

```python
import numpy as np
import jax
import jax.numpy as jnp

def _softmax(x, axis=-1):
    return jax.nn.softmax(x, axis=axis)

def _gelu(x):
    return jax.nn.gelu(x, approximate=True)

def _silu(x):
    return jax.nn.silu(x)

def _sigmoid(x):
    return jax.nn.sigmoid(x)

def _layernorm(x, axis=-1, eps=1e-05):
    m = jnp.mean(x, axis=axis, keepdims=True)
    v = jnp.var(x, axis=axis, keepdims=True)
    return (x - m) / jnp.sqrt(v + eps)

def _scatter_add(tgt, idx, src, axis=0):
    return tgt.at[idx].add(src)

def _segment_sum(src, seg, n):
    return jax.ops.segment_sum(src, seg, n)
kernel_name = 'mk_flamingo_gated_d4_seqx_r8_5a9088'

def setup_inputs(seed: int=0):
    np.random.seed(seed)
    _w = jnp.asarray

    def _rec_inputs():
        import jax
        import jax.numpy as jnp
        _rk = jax.random.key(seed)
        x = 7.22e-05 + 1 * jax.random.normal(jax.random.fold_in(_rk, 1), (4, 512, 128), jnp.float32)
        _lenS = 512 - jax.random.randint(jax.random.fold_in(_rk, 7), (4,), 0, max(1, 512 // 4) + 1, jnp.int32)
        _lenS2 = 77 - jax.random.randint(jax.random.fold_in(_rk, 8), (4,), 0, max(1, 77 // 4) + 1, jnp.int32)
        _ctx_1024P = jax.random.normal(jax.random.fold_in(_rk, 11), (4, 16, 128), jnp.float32)
        _ctx_1024c = jax.random.dirichlet(jax.random.fold_in(_rk, 511), 0.3 * jnp.ones((16,), jnp.float32), (4, 77))
        _ctx_1024t = jnp.einsum('bsk,bkd->bsd', _ctx_1024c, _ctx_1024P)
        _ctx_1024t = _ctx_1024t * jax.lax.rsqrt(jnp.mean(jnp.square(_ctx_1024t)) + 1e-12) * 0.953939
        ctx_1024 = 4.13588e-05 + 0.999923 * (_ctx_1024t + 0.3 * jax.random.normal(jax.random.fold_in(_rk, 611), (4, 77, 128), jnp.float32))
        _validS = jnp.arange(512)[None, :] < _lenS[:, None]
        _validS2 = jnp.arange(77)[None, :] < _lenS2[:, None]
        _causal = jnp.tril(jnp.ones((512, 512), dtype=bool))
        mask_Bx1x1xS2_bk0 = jnp.logical_not(jnp.broadcast_to(_validS2[:, None, None, :], (4, 1, 1, 77)))
        mask_BxSxS2_bf0 = jnp.logical_not(jnp.ones((4, 512, 77), dtype=bool))
        _g = jax.random.normal(jax.random.fold_in(_rk, 9001), (2, 4), jnp.float32)
        _g = jnp.sign(_g) * jnp.maximum(jnp.abs(_g), 1.0) + (_g == 0) * 1.0
        g_xattn = _g[0]
        g_ffn = _g[1]
        return (x, ctx_1024, mask_Bx1x1xS2_bk0, mask_BxSxS2_bf0, g_xattn, g_ffn)
    x, ctx_1024, mask_Bx1x1xS2_bk0, mask_BxSxS2_bf0, g_xattn, g_ffn = _rec_inputs()

    def _L0_xattn_setup():
        import jax, jax.numpy as jnp
        import numpy as np
        EMBED_DIM = 128
        NUM_HEADS = 16
        HEAD_DIM = EMBED_DIM // NUM_HEADS

        def _split_heads(x):
            B, S, D = x.shape
            return x.reshape(B, S, NUM_HEADS, HEAD_DIM).transpose(0, 2, 1, 3)
        key = jax.random.key(seed)
        ks = jax.random.split(key, 11)
        B, S, D = (4, 256, EMBED_DIM)
        s = 1.0 / np.sqrt(D)
        return {'query': jax.random.normal(ks[0], (B, S, D), jnp.float32), 'key': jax.random.normal(ks[1], (B, S, D), jnp.float32), 'value': jax.random.normal(ks[2], (B, S, D), jnp.float32), 'Wq': jax.random.normal(ks[3], (D, D), jnp.float32) * s, 'bq': jnp.zeros((D,), jnp.float32), 'Wk': jax.random.normal(ks[4], (D, D), jnp.float32) * s, 'bk': jnp.zeros((D,), jnp.float32), 'Wv': jax.random.normal(ks[5], (D, D), jnp.float32) * s, 'bv': jnp.zeros((D,), jnp.float32), 'Wo': jax.random.normal(ks[6], (D, D), jnp.float32) * s, 'bo': jnp.zeros((D,), jnp.float32)}
    _L0_xattn_all = _L0_xattn_setup()
    _L0_xattn_in = {k: v for k, v in _L0_xattn_all.items() if k in ('Wq', 'bq', 'Wk', 'bk', 'Wv', 'bv', 'Wo', 'bo')}
    del _L0_xattn_all

    def _L0_ffn_setup():
        import jax, jax.numpy as jnp
        import numpy as np
        HIDDEN = 128
        INTER = 512
        N_EXPERTS = 8

        def geglu(x, w1, w2, w3):
            return jax.nn.gelu(x @ w1, approximate=False) * (x @ w2) @ w3
        key = jax.random.key(seed)
        ks = jax.random.split(key, 8)
        s = 0.02
        x = jax.random.normal(ks[0], (2, 256, HIDDEN), dtype=jnp.float32)
        w1s = jax.random.normal(ks[1], (HIDDEN, INTER), dtype=jnp.float32) * s
        w2s = jax.random.normal(ks[2], (HIDDEN, INTER), dtype=jnp.float32) * s
        w3s = jax.random.normal(ks[3], (INTER, HIDDEN), dtype=jnp.float32) * s
        W1 = jax.random.normal(ks[4], (N_EXPERTS, HIDDEN, INTER), dtype=jnp.float32) * s
        W2 = jax.random.normal(ks[5], (N_EXPERTS, HIDDEN, INTER), dtype=jnp.float32) * s
        W3 = jax.random.normal(ks[6], (N_EXPERTS, INTER, HIDDEN), dtype=jnp.float32) * s
        Wg = jax.random.normal(ks[7], (HIDDEN, N_EXPERTS), dtype=jnp.float32) * s
        return {'x': x, 'w1s': w1s, 'w2s': w2s, 'w3s': w3s, 'W1': W1, 'W2': W2, 'W3': W3, 'Wg': Wg}
    _L0_ffn_all = _L0_ffn_setup()
    _L0_ffn_in = {k: v for k, v in _L0_ffn_all.items() if k in ('w1s', 'w2s', 'w3s', 'W1', 'W2', 'W3', 'Wg')}
    del _L0_ffn_all

    def _L1_xattn_setup():
        import math
        import jax, jax.numpy as jnp
        import numpy as np
        NUM_BUCKETS = 32
        MAX_DISTANCE = 128
        H = 16
        D_MODEL = 128
        D_K = D_MODEL // H

        def _relative_position_bucket(relative_position):
            nb = NUM_BUCKETS // 2
            buckets = (relative_position > 0).astype(jnp.int32) * nb
            rp = jnp.abs(relative_position)
            max_exact = nb // 2
            is_small = rp < max_exact
            rp_large = max_exact + (jnp.log(jnp.maximum(rp, 1).astype(jnp.float32) / max_exact) / math.log(MAX_DISTANCE / max_exact) * (nb - max_exact)).astype(jnp.int32)
            rp_large = jnp.minimum(rp_large, nb - 1)
            return buckets + jnp.where(is_small, rp, rp_large)
        key = jax.random.key(seed)
        ks = jax.random.split(key, 8)
        B, T_k, T_q = (4, 256, 128)
        std = D_MODEL ** (-0.5)
        inp = {'src': jax.random.normal(ks[0], (B, T_k, D_MODEL), dtype=jnp.float32), 'dst': jax.random.normal(ks[1], (B, T_q, D_MODEL), dtype=jnp.float32), 'mask': jax.random.randint(ks[2], (B, 1, 1, T_k), 0, 2).astype(bool), 'Wq': jax.random.normal(ks[3], (D_MODEL, D_MODEL), dtype=jnp.float32) * std, 'Wk': jax.random.normal(ks[4], (D_MODEL, D_MODEL), dtype=jnp.float32) * std, 'Wv': jax.random.normal(ks[5], (D_MODEL, D_MODEL), dtype=jnp.float32) * std, 'Wo': jax.random.normal(ks[6], (D_MODEL, D_MODEL), dtype=jnp.float32) * std, 'rel_bias': jax.random.normal(ks[7], (H, NUM_BUCKETS), dtype=jnp.float32) * NUM_BUCKETS ** (-0.5)}
        return inp
    _L1_xattn_all = _L1_xattn_setup()
    _L1_xattn_in = {k: v for k, v in _L1_xattn_all.items() if k in ('Wq', 'Wk', 'Wv', 'Wo', 'rel_bias')}
    del _L1_xattn_all

    def _L1_ffn_setup():
        import jax, jax.numpy as jnp
        import numpy as np
        B, S, D, E, F, K = (4, 128, 128, 8, 352, 1)
        key = jax.random.key(seed)
        ks = jax.random.split(key, 8)
        sc = 0.02
        return {'x_bsD': jax.random.normal(ks[0], (B, S, D), jnp.float32), 'router_DE': jax.random.normal(ks[1], (D, E), jnp.float32) * sc, 'w1_eDF': jax.random.normal(ks[2], (E, D, F), jnp.float32) * sc, 'w3_eDF': jax.random.normal(ks[3], (E, D, F), jnp.float32) * sc, 'w2_eFD': jax.random.normal(ks[4], (E, F, D), jnp.float32) * sc, 'ws1_DF': jax.random.normal(ks[5], (D, F), jnp.float32) * sc, 'ws3_DF': jax.random.normal(ks[6], (D, F), jnp.float32) * sc, 'ws2_FD': jax.random.normal(ks[7], (F, D), jnp.float32) * sc}
    _L1_ffn_all = _L1_ffn_setup()
    _L1_ffn_in = {k: v for k, v in _L1_ffn_all.items() if k in ('router_DE', 'w1_eDF', 'w3_eDF', 'w2_eFD', 'ws1_DF', 'ws3_DF', 'ws2_FD')}
    del _L1_ffn_all

    def _L2_xattn_setup():
        import jax, jax.numpy as jnp
        import numpy as np
        B, S, D = (4, 256, 128)
        H, DK, DV = (16, 64, 64)
        key = jax.random.key(seed)
        ks = jax.random.split(key, 12)

        def lin(k, out_d, in_d, std):
            kw, kb = jax.random.split(k)
            w = jax.random.normal(kw, (out_d, in_d), dtype=jnp.float32) * std
            b = jax.random.uniform(kb, (out_d,), dtype=jnp.float32, minval=-1, maxval=1) / np.sqrt(in_d)
            return (w, b)
        std_k = np.sqrt(2.0 / (D + DK)).astype(np.float32)
        std_v = np.sqrt(2.0 / (D + DV)).astype(np.float32)
        wQ_w, wQ_b = lin(ks[0], DK * H, D, std_k)
        wK_w, wK_b = lin(ks[1], DK * H, D, std_k)
        wV_w, wV_b = lin(ks[2], DV * H, D, std_v)
        wOut_w, wOut_b = lin(ks[3], D, DV * H, std_v)
        Q = jax.random.normal(ks[4], (B, S, D), dtype=jnp.float32)
        K = jax.random.normal(ks[5], (B, S, D), dtype=jnp.float32)
        V = jax.random.normal(ks[6], (B, S, D), dtype=jnp.float32)
        attnMask = jnp.zeros((B, S, S), dtype=bool)
        return {'Q': Q, 'K': K, 'V': V, 'attnMask': attnMask, 'wQ_w': wQ_w, 'wQ_b': wQ_b, 'wK_w': wK_w, 'wK_b': wK_b, 'wV_w': wV_w, 'wV_b': wV_b, 'wOut_w': wOut_w, 'wOut_b': wOut_b}
    _L2_xattn_all = _L2_xattn_setup()
    _L2_xattn_in = {k: v for k, v in _L2_xattn_all.items() if k in ('wQ_w', 'wQ_b', 'wK_w', 'wK_b', 'wV_w', 'wV_b', 'wOut_w', 'wOut_b')}
    del _L2_xattn_all

    def _L2_ffn_setup():
        import jax, jax.numpy as jnp
        import numpy as np
        D_MODEL = 128
        EXPANSION = 4
        D_HIDDEN = D_MODEL * EXPANSION
        NUM_STAGES = int(np.log2(D_HIDDEN))

        def butterfly(y, weights, dim):
            lead = y.shape[:-1]
            for stage in range(weights.shape[0]):
                s = 2 ** stage
                nb = dim // (2 * s)
                yr = y.reshape(*lead, nb, 2, s)
                a = yr[..., 0, :]
                b = yr[..., 1, :]
                w = weights[stage].reshape(nb, s, 2, 2)
                na = w[..., 0, 0] * a + w[..., 0, 1] * b
                nb2 = w[..., 1, 0] * a + w[..., 1, 1] * b
                y = jnp.stack([na, nb2], axis=-2).reshape(*lead, dim)
            return y
        key = jax.random.key(seed)
        ks = jax.random.split(key, 6)
        B, S = (4, 256)
        x = jax.random.normal(ks[0], (B, S, D_MODEL), jnp.float32)
        W_exp = jax.random.normal(ks[1], (D_MODEL, D_HIDDEN), jnp.float32) * 0.02
        b_exp = jnp.zeros((D_HIDDEN,), jnp.float32)
        up_weights = jax.random.normal(ks[2], (NUM_STAGES, D_HIDDEN // 2, 2, 2), jnp.float32) * 0.02
        up_bias = jnp.zeros((D_HIDDEN,), jnp.float32)
        down_weights = jax.random.normal(ks[3], (NUM_STAGES, D_HIDDEN // 2, 2, 2), jnp.float32) * 0.02
        W_con = jax.random.normal(ks[4], (D_HIDDEN, D_MODEL), jnp.float32) * 0.02
        b_con = jnp.zeros((D_MODEL,), jnp.float32)
        down_bias = jnp.zeros((D_MODEL,), jnp.float32)
        return dict(x=x, W_exp=W_exp, b_exp=b_exp, up_weights=up_weights, up_bias=up_bias, down_weights=down_weights, W_con=W_con, b_con=b_con, down_bias=down_bias)
    _L2_ffn_all = _L2_ffn_setup()
    _L2_ffn_in = {k: v for k, v in _L2_ffn_all.items() if k in ('W_exp', 'b_exp', 'up_weights', 'up_bias', 'down_weights', 'W_con', 'b_con', 'down_bias')}
    del _L2_ffn_all

    def _L3_xattn_setup():
        import jax, jax.numpy as jnp
        import numpy as np
        DIM = 128
        NHEADS = 8
        HEAD_DIM = DIM // NHEADS
        ROPE_BASE = 10000.0

        def _rope(t, positions):
            d = t.shape[-1]
            inv_freq = 1.0 / ROPE_BASE ** (jnp.arange(0, d, 2, dtype=jnp.float32) / d)
            freqs = positions[:, None].astype(jnp.float32) * inv_freq
            emb = jnp.concatenate([freqs, freqs], axis=-1)
            cos = jnp.cos(emb)[None, :, None, :].astype(t.dtype)
            sin = jnp.sin(emb)[None, :, None, :].astype(t.dtype)
            t1, t2 = jnp.split(t, 2, axis=-1)
            rot = jnp.concatenate([-t2, t1], axis=-1)
            return t * cos + rot * sin
        key = jax.random.key(seed)
        k1, k2, k3, k4, k5 = jax.random.split(key, 5)
        B, T, S = (2, 256, 375)
        w_std = 1.0 / np.sqrt(DIM)
        return {'x': jax.random.normal(k1, (B, T, DIM), dtype=jnp.float32), 'xmel': jax.random.normal(k2, (B, S, DIM), dtype=jnp.float32), 'Wq': jax.random.normal(k3, (DIM, DIM), dtype=jnp.float32) * w_std, 'Wkv': jax.random.normal(k4, (2 * DIM, DIM), dtype=jnp.float32) * w_std, 'Wout': jax.random.normal(k5, (DIM, DIM), dtype=jnp.float32) * w_std}
    _L3_xattn_all = _L3_xattn_setup()
    _L3_xattn_in = {k: v for k, v in _L3_xattn_all.items() if k in ('Wq', 'Wkv', 'Wout')}
    del _L3_xattn_all

    def _L3_ffn_setup():
        import math
        import jax, jax.numpy as jnp
        from jax import lax
        import numpy as np
        E = 16
        K = 2
        CF = 1.25
        key = jax.random.key(seed)
        k0, k1, k2, k3, k4 = jax.random.split(key, 5)
        B, S, D, H = (2, 256, 128, 128)
        scale = 0.02
        return {'x': jax.random.normal(k0, (B, S, D), dtype=jnp.float32), 'router_w': jax.random.normal(k1, (D, E), dtype=jnp.float32) * scale, 'gate_w': jax.random.normal(k2, (E, D, H), dtype=jnp.float32) * scale, 'up_w': jax.random.normal(k3, (E, D, H), dtype=jnp.float32) * scale, 'down_w': jax.random.normal(k4, (E, H, D), dtype=jnp.float32) * scale}
    _L3_ffn_all = _L3_ffn_setup()
    _L3_ffn_in = {k: v for k, v in _L3_ffn_all.items() if k in ('router_w', 'gate_w', 'up_w', 'down_w')}
    del _L3_ffn_all
    return {'x': x, 'ctx_1024': ctx_1024, 'mask_Bx1x1xS2_bk0': mask_Bx1x1xS2_bk0, 'mask_BxSxS2_bf0': mask_BxSxS2_bf0, 'g_xattn': g_xattn, 'g_ffn': g_ffn, 'L0_xattn_Wq': _L0_xattn_in['Wq'], 'L0_xattn_bq': _L0_xattn_in['bq'], 'L0_xattn_Wk': _L0_xattn_in['Wk'], 'L0_xattn_bk': _L0_xattn_in['bk'], 'L0_xattn_Wv': _L0_xattn_in['Wv'], 'L0_xattn_bv': _L0_xattn_in['bv'], 'L0_xattn_Wo': _L0_xattn_in['Wo'], 'L0_xattn_bo': _L0_xattn_in['bo'], 'L0_ffn_w1s': _L0_ffn_in['w1s'], 'L0_ffn_w2s': _L0_ffn_in['w2s'], 'L0_ffn_w3s': _L0_ffn_in['w3s'], 'L0_ffn_W1': _L0_ffn_in['W1'], 'L0_ffn_W2': _L0_ffn_in['W2'], 'L0_ffn_W3': _L0_ffn_in['W3'], 'L0_ffn_Wg': _L0_ffn_in['Wg'], 'L1_xattn_Wq': _L1_xattn_in['Wq'], 'L1_xattn_Wk': _L1_xattn_in['Wk'], 'L1_xattn_Wv': _L1_xattn_in['Wv'], 'L1_xattn_Wo': _L1_xattn_in['Wo'], 'L1_xattn_rel_bias': _L1_xattn_in['rel_bias'], 'L1_ffn_router_DE': _L1_ffn_in['router_DE'], 'L1_ffn_w1_eDF': _L1_ffn_in['w1_eDF'], 'L1_ffn_w3_eDF': _L1_ffn_in['w3_eDF'], 'L1_ffn_w2_eFD': _L1_ffn_in['w2_eFD'], 'L1_ffn_ws1_DF': _L1_ffn_in['ws1_DF'], 'L1_ffn_ws3_DF': _L1_ffn_in['ws3_DF'], 'L1_ffn_ws2_FD': _L1_ffn_in['ws2_FD'], 'L2_xattn_wQ_w': _L2_xattn_in['wQ_w'], 'L2_xattn_wQ_b': _L2_xattn_in['wQ_b'], 'L2_xattn_wK_w': _L2_xattn_in['wK_w'], 'L2_xattn_wK_b': _L2_xattn_in['wK_b'], 'L2_xattn_wV_w': _L2_xattn_in['wV_w'], 'L2_xattn_wV_b': _L2_xattn_in['wV_b'], 'L2_xattn_wOut_w': _L2_xattn_in['wOut_w'], 'L2_xattn_wOut_b': _L2_xattn_in['wOut_b'], 'L2_ffn_W_exp': _L2_ffn_in['W_exp'], 'L2_ffn_b_exp': _L2_ffn_in['b_exp'], 'L2_ffn_up_weights': _L2_ffn_in['up_weights'], 'L2_ffn_up_bias': _L2_ffn_in['up_bias'], 'L2_ffn_down_weights': _L2_ffn_in['down_weights'], 'L2_ffn_W_con': _L2_ffn_in['W_con'], 'L2_ffn_b_con': _L2_ffn_in['b_con'], 'L2_ffn_down_bias': _L2_ffn_in['down_bias'], 'L3_xattn_Wq': _L3_xattn_in['Wq'], 'L3_xattn_Wkv': _L3_xattn_in['Wkv'], 'L3_xattn_Wout': _L3_xattn_in['Wout'], 'L3_ffn_router_w': _L3_ffn_in['router_w'], 'L3_ffn_gate_w': _L3_ffn_in['gate_w'], 'L3_ffn_up_w': _L3_ffn_in['up_w'], 'L3_ffn_down_w': _L3_ffn_in['down_w']}

def reference(x, ctx_1024, mask_Bx1x1xS2_bk0, mask_BxSxS2_bf0, g_xattn, g_ffn, L0_xattn_Wq, L0_xattn_bq, L0_xattn_Wk, L0_xattn_bk, L0_xattn_Wv, L0_xattn_bv, L0_xattn_Wo, L0_xattn_bo, L0_ffn_w1s, L0_ffn_w2s, L0_ffn_w3s, L0_ffn_W1, L0_ffn_W2, L0_ffn_W3, L0_ffn_Wg, L1_xattn_Wq, L1_xattn_Wk, L1_xattn_Wv, L1_xattn_Wo, L1_xattn_rel_bias, L1_ffn_router_DE, L1_ffn_w1_eDF, L1_ffn_w3_eDF, L1_ffn_w2_eFD, L1_ffn_ws1_DF, L1_ffn_ws3_DF, L1_ffn_ws2_FD, L2_xattn_wQ_w, L2_xattn_wQ_b, L2_xattn_wK_w, L2_xattn_wK_b, L2_xattn_wV_w, L2_xattn_wV_b, L2_xattn_wOut_w, L2_xattn_wOut_b, L2_ffn_W_exp, L2_ffn_b_exp, L2_ffn_up_weights, L2_ffn_up_bias, L2_ffn_down_weights, L2_ffn_W_con, L2_ffn_b_con, L2_ffn_down_bias, L3_xattn_Wq, L3_xattn_Wkv, L3_xattn_Wout, L3_ffn_router_w, L3_ffn_gate_w, L3_ffn_up_w, L3_ffn_down_w):
    import jax
    import jax.numpy as jnp

    def _L0_xattn_ref(query, key, value, Wq, bq, Wk, bk, Wv, bv, Wo, bo):
        import jax, jax.numpy as jnp
        import numpy as np
        EMBED_DIM = 128
        NUM_HEADS = 16
        HEAD_DIM = EMBED_DIM // NUM_HEADS

        def _split_heads(x):
            B, S, D = x.shape
            return x.reshape(B, S, NUM_HEADS, HEAD_DIM).transpose(0, 2, 1, 3)
        q = _split_heads(query @ Wq + bq)
        k = _split_heads(key @ Wk + bk)
        v = _split_heads(value @ Wv + bv)
        scores = jnp.einsum('bhqd,bhkd->bhqk', q, k) / np.sqrt(HEAD_DIM).astype(np.float32)
        attn = jax.nn.softmax(scores, axis=-1)
        ctx = jnp.einsum('bhqk,bhkd->bhqd', attn, v)
        B, H, S, hd = ctx.shape
        ctx = ctx.transpose(0, 2, 1, 3).reshape(B, S, H * hd)
        return ctx @ Wo + bo

    def _L0_ffn_ref(x, w1s, w2s, w3s, W1, W2, W3, Wg):
        import jax, jax.numpy as jnp
        import numpy as np
        HIDDEN = 128
        INTER = 512
        N_EXPERTS = 8

        def geglu(x, w1, w2, w3):
            return jax.nn.gelu(x @ w1, approximate=False) * (x @ w2) @ w3
        B, T, C = x.shape
        xf = x.reshape(-1, C)
        shared = geglu(xf, w1s, w2s, w3s)
        logits = xf @ Wg
        idx = jnp.argmax(logits, axis=-1)
        final = jnp.zeros_like(xf)
        for e in range(N_EXPERTS):
            y = geglu(xf, W1[e], W2[e], W3[e])
            final = final + jnp.where((idx == e)[:, None], y, 0.0)
        return (shared + final).reshape(B, T, C)

    def _L1_xattn_ref(src, dst, mask, Wq, Wk, Wv, Wo, rel_bias):
        import math
        import jax, jax.numpy as jnp
        import numpy as np
        NUM_BUCKETS = 32
        MAX_DISTANCE = 128
        H = 16
        D_MODEL = 128
        D_K = D_MODEL // H

        def _relative_position_bucket(relative_position):
            nb = NUM_BUCKETS // 2
            buckets = (relative_position > 0).astype(jnp.int32) * nb
            rp = jnp.abs(relative_position)
            max_exact = nb // 2
            is_small = rp < max_exact
            rp_large = max_exact + (jnp.log(jnp.maximum(rp, 1).astype(jnp.float32) / max_exact) / math.log(MAX_DISTANCE / max_exact) * (nb - max_exact)).astype(jnp.int32)
            rp_large = jnp.minimum(rp_large, nb - 1)
            return buckets + jnp.where(is_small, rp, rp_large)
        B, T_k, _ = src.shape
        T_q = dst.shape[1]
        q = (dst @ Wq.T).reshape(B, T_q, H, D_K)
        k = (src @ Wk.T).reshape(B, T_k, H, D_K)
        v = (src @ Wv.T).reshape(B, T_k, H, D_K)
        scores = jnp.einsum('bqhd,bkhd->bhqk', q, k)
        rel_pos = jnp.arange(T_k)[None, :] - jnp.arange(T_q)[:, None]
        rp_bucket = _relative_position_bucket(rel_pos)
        bias = rel_bias[:, rp_bucket]
        scores = scores + bias[None]
        scores = jnp.where(mask, scores, -1000000000.0)
        attn = jax.nn.softmax(scores, axis=-1)
        out = jnp.einsum('bhqk,bkhd->bqhd', attn, v).reshape(B, T_q, H * D_K)
        return out @ Wo.T

    def _L1_ffn_ref(x_bsD, router_DE, w1_eDF, w3_eDF, w2_eFD, ws1_DF, ws3_DF, ws2_FD):
        import jax, jax.numpy as jnp
        import numpy as np
        B, S, D, E, F, K = (4, 128, 128, 8, 352, 1)
        b, s, d = x_bsD.shape
        a = b * s
        x_aD = x_bsD.reshape(a, d)
        scores_aE = x_aD @ router_DE
        vals_aK, idx_aK = jax.lax.top_k(scores_aE, K)
        masked_aE = jnp.full_like(scores_aE, -jnp.inf).at[jnp.arange(a)[:, None], idx_aK].set(vals_aK)
        gates_Ea = jax.nn.sigmoid(masked_aE).T
        routed_in_EaD = jax.lax.stop_gradient(gates_Ea[:, :, None] * x_aD[None, :, :])
        mid_EaF = jax.nn.silu(jnp.einsum('ead,edf->eaf', routed_in_EaD, w1_eDF)) * jnp.einsum('ead,edf->eaf', routed_in_EaD, w3_eDF)
        routed_out_EaD = jnp.einsum('eaf,efd->ead', mid_EaF, w2_eFD)
        shared_aD = jax.nn.silu(x_aD @ ws1_DF) * (x_aD @ ws3_DF) @ ws2_FD
        out_aD = shared_aD + routed_out_EaD.sum(axis=0)
        return out_aD.reshape(b, s, d)

    def _L2_xattn_ref(Q, K, V, attnMask, wQ_w, wQ_b, wK_w, wK_b, wV_w, wV_b, wOut_w, wOut_b):
        import jax, jax.numpy as jnp
        import numpy as np
        B, S, D = (4, 256, 128)
        H, DK, DV = (16, 64, 64)
        N = Q.shape[0]
        q = (Q @ wQ_w.T + wQ_b).reshape(N, -1, H, DK).transpose(0, 2, 1, 3)
        k = (K @ wK_w.T + wK_b).reshape(N, -1, H, DK).transpose(0, 2, 1, 3)
        v = (V @ wV_w.T + wV_b).reshape(N, -1, H, DV).transpose(0, 2, 1, 3)
        scale = 1.0 / np.sqrt(DK).astype(np.float32)
        scores = jnp.einsum('bhqd,bhkd->bhqk', q, k) * scale
        scores = jnp.where(attnMask[:, None, :, :], jnp.float32(-10000.0), scores)
        attns = jax.nn.softmax(scores, axis=-1)
        out = jnp.einsum('bhqk,bhkd->bhqd', attns, v)
        out = out.transpose(0, 2, 1, 3).reshape(N, -1, DV * H)
        return out @ wOut_w.T + wOut_b

    def _L2_ffn_ref(x, W_exp, b_exp, up_weights, up_bias, down_weights, W_con, b_con, down_bias):
        import jax, jax.numpy as jnp
        import numpy as np
        D_MODEL = 128
        EXPANSION = 4
        D_HIDDEN = D_MODEL * EXPANSION
        NUM_STAGES = int(np.log2(D_HIDDEN))

        def butterfly(y, weights, dim):
            lead = y.shape[:-1]
            for stage in range(weights.shape[0]):
                s = 2 ** stage
                nb = dim // (2 * s)
                yr = y.reshape(*lead, nb, 2, s)
                a = yr[..., 0, :]
                b = yr[..., 1, :]
                w = weights[stage].reshape(nb, s, 2, 2)
                na = w[..., 0, 0] * a + w[..., 0, 1] * b
                nb2 = w[..., 1, 0] * a + w[..., 1, 1] * b
                y = jnp.stack([na, nb2], axis=-2).reshape(*lead, dim)
            return y
        h = jnp.einsum('bsd,dh->bsh', x, W_exp) + b_exp
        h = butterfly(h, up_weights, D_HIDDEN)
        h = jax.nn.gelu(h + up_bias, approximate=False)
        h = butterfly(h, down_weights, D_HIDDEN)
        y = jnp.einsum('bsh,hd->bsd', h, W_con) + b_con
        return y + down_bias

    def _L3_xattn_ref(x, xmel, Wq, Wkv, Wout):
        import jax, jax.numpy as jnp
        import numpy as np
        DIM = 128
        NHEADS = 8
        HEAD_DIM = DIM // NHEADS
        ROPE_BASE = 10000.0

        def _rope(t, positions):
            d = t.shape[-1]
            inv_freq = 1.0 / ROPE_BASE ** (jnp.arange(0, d, 2, dtype=jnp.float32) / d)
            freqs = positions[:, None].astype(jnp.float32) * inv_freq
            emb = jnp.concatenate([freqs, freqs], axis=-1)
            cos = jnp.cos(emb)[None, :, None, :].astype(t.dtype)
            sin = jnp.sin(emb)[None, :, None, :].astype(t.dtype)
            t1, t2 = jnp.split(t, 2, axis=-1)
            rot = jnp.concatenate([-t2, t1], axis=-1)
            return t * cos + rot * sin
        B, T, C = x.shape
        S = xmel.shape[1]
        H, D = (NHEADS, C // NHEADS)
        q = (x @ Wq.T).reshape(B, T, H, D)
        kv = (xmel @ Wkv.T).reshape(B, S, 2, H, D)
        q = _rope(q, jnp.arange(T))
        k = _rope(kv[:, :, 0], jnp.arange(S))
        v = kv[:, :, 1]
        scale = (C // H) ** (-0.25)
        q = q * scale
        k = k * scale
        scores = jnp.einsum('bthd,bshd->bhts', q, k)
        attn = jax.nn.softmax(scores, axis=-1)
        out = jnp.einsum('bhts,bshd->bthd', attn, v)
        out = out.reshape(B, T, C)
        return out @ Wout.T

    def _L3_ffn_ref(x, router_w, gate_w, up_w, down_w):
        import math
        import jax, jax.numpy as jnp
        from jax import lax
        import numpy as np
        E = 16
        K = 2
        CF = 1.25
        B, S, D = x.shape
        xf = x.reshape(-1, D)
        T = B * S
        capacity = max(1, math.ceil(T * K / E * CF))
        Cbuf = K * capacity
        logits = xf @ router_w
        probs = jax.nn.softmax(logits, axis=-1)
        w, idx = lax.top_k(probs, K)
        oh = jax.nn.one_hot(idx, E, dtype=w.dtype)
        rank = jnp.cumsum(oh, axis=0) - oh
        myrank = jnp.sum(rank * oh, axis=-1)
        keep = myrank < capacity
        w = jnp.where(keep, w, 0.0)
        flat_e = idx.reshape(-1)
        flat_w = w.reshape(-1)
        keep_f = keep.reshape(-1)
        tok = jnp.repeat(jnp.arange(T, dtype=jnp.int32), K)
        ohk = jax.nn.one_hot(flat_e, E, dtype=jnp.int32) * keep_f[:, None].astype(jnp.int32)
        pos = jnp.cumsum(ohk, axis=0) - ohk
        slot = jnp.sum(pos * ohk, axis=-1)
        e_idx = jnp.where(keep_f, flat_e, E)
        dispatch = jnp.full((E + 1, Cbuf), T, dtype=jnp.int32).at[e_idx, slot].set(tok)
        wbuf = jnp.zeros((E + 1, Cbuf), dtype=w.dtype).at[e_idx, slot].set(flat_w)
        dispatch = dispatch[:E]
        wbuf = wbuf[:E]
        x_pad = jnp.concatenate([xf, jnp.zeros((1, D), xf.dtype)], axis=0)
        xe = x_pad[dispatch]
        gate = jnp.einsum('ecd,edh->ech', xe, gate_w)
        up = jnp.einsum('ecd,edh->ech', xe, up_w)
        hidden = jax.nn.silu(gate) * up
        out = jnp.einsum('ech,ehd->ecd', hidden, down_w)
        out = out * wbuf[:, :, None]
        combined = jnp.zeros((T + 1, D), dtype=xf.dtype).at[dispatch.reshape(-1)].add(out.reshape(-1, D))
        return combined[:T].reshape(B, S, D)
    x = x + jnp.tanh(g_xattn[0]) * _L0_xattn_ref(_layernorm(x, axis=-1), ctx_1024, ctx_1024, L0_xattn_Wq, L0_xattn_bq, L0_xattn_Wk, L0_xattn_bk, L0_xattn_Wv, L0_xattn_bv, L0_xattn_Wo, L0_xattn_bo)
    x = x + jnp.tanh(g_ffn[0]) * _L0_ffn_ref(_layernorm(x, axis=-1), L0_ffn_w1s, L0_ffn_w2s, L0_ffn_w3s, L0_ffn_W1, L0_ffn_W2, L0_ffn_W3, L0_ffn_Wg)
    x = x + jnp.tanh(g_xattn[1]) * _L1_xattn_ref(ctx_1024, _layernorm(x, axis=-1), mask_Bx1x1xS2_bk0, L1_xattn_Wq, L1_xattn_Wk, L1_xattn_Wv, L1_xattn_Wo, L1_xattn_rel_bias)
    x = x + jnp.tanh(g_ffn[1]) * _L1_ffn_ref(_layernorm(x, axis=-1), L1_ffn_router_DE, L1_ffn_w1_eDF, L1_ffn_w3_eDF, L1_ffn_w2_eFD, L1_ffn_ws1_DF, L1_ffn_ws3_DF, L1_ffn_ws2_FD)
    x = x + jnp.tanh(g_xattn[2]) * _L2_xattn_ref(_layernorm(x, axis=-1), ctx_1024, ctx_1024, mask_BxSxS2_bf0, L2_xattn_wQ_w, L2_xattn_wQ_b, L2_xattn_wK_w, L2_xattn_wK_b, L2_xattn_wV_w, L2_xattn_wV_b, L2_xattn_wOut_w, L2_xattn_wOut_b)
    x = x + jnp.tanh(g_ffn[2]) * _L2_ffn_ref(_layernorm(x, axis=-1), L2_ffn_W_exp, L2_ffn_b_exp, L2_ffn_up_weights, L2_ffn_up_bias, L2_ffn_down_weights, L2_ffn_W_con, L2_ffn_b_con, L2_ffn_down_bias)
    x = x + jnp.tanh(g_xattn[3]) * _L3_xattn_ref(_layernorm(x, axis=-1), ctx_1024, L3_xattn_Wq, L3_xattn_Wkv, L3_xattn_Wout)
    x = x + jnp.tanh(g_ffn[3]) * _L3_ffn_ref(_layernorm(x, axis=-1), L3_ffn_router_w, L3_ffn_gate_w, L3_ffn_up_w, L3_ffn_down_w)
    return x

_drawn_inputs = setup_inputs


def setup_inputs(seed=0):
    import zlib

    import numpy as np

    out = dict(_drawn_inputs(seed))
    spreads = {'L0_xattn_bq': (0.0, 0.48),
     'L0_xattn_bk': (0.0, 2.0),
     'L0_xattn_bv': (0.0, 0.1),
     'L0_xattn_bo': (0.0, 0.1),
     'L2_ffn_b_exp': (0.0, 0.1),
     'L2_ffn_up_bias': (0.0, 0.1),
     'L2_ffn_b_con': (0.0, 0.8),
     'L2_ffn_down_bias': (0.0, 0.794)}
    factors = {'g_ffn': 8.0,
     'L0_ffn_w1s': 8.0,
     'L0_ffn_w2s': 8.0,
     'L0_ffn_w3s': 8.0,
     'L0_ffn_W1': 8.0,
     'L0_ffn_W2': 8.0,
     'L0_ffn_W3': 8.0,
     'L0_ffn_Wg': 8.0,
     'L1_xattn_rel_bias': 5.933,
     'L1_ffn_router_DE': 8.0,
     'L1_ffn_w1_eDF': 8.0,
     'L1_ffn_w3_eDF': 8.0,
     'L1_ffn_w2_eFD': 8.0,
     'L1_ffn_ws1_DF': 8.0,
     'L1_ffn_ws3_DF': 8.0,
     'L1_ffn_ws2_FD': 8.0,
     'L2_xattn_wQ_b': 14.038,
     'L2_xattn_wK_b': 64.0,
     'L2_xattn_wOut_b': 46.841,
     'L3_ffn_router_w': 8.0,
     'L3_ffn_gate_w': 8.0,
     'L3_ffn_up_w': 8.0,
     'L3_ffn_down_w': 8.0,
     'L2_xattn_wV_b': 5.021,
     'L3_xattn_Wq': 4.05}
    for name, (base, spread) in spreads.items():
        noise = np.random.default_rng([zlib.crc32(name.encode()), seed]).standard_normal(out[name].shape)
        drawn = base * np.exp(spread * noise) if base else spread * noise
        out[name] = jnp.asarray(drawn.astype(out[name].dtype))
    for name, factor in factors.items():
        out[name] = (out[name] * factor).astype(out[name].dtype)
    return out
```

```python
import numpy as np

import concourse.bass as bass
from concourse import mybir
from contextlib import ExitStack

P = 128
B, S, SK, D = 4, 512, 77, 128
TOKENS = B * S
TILES = TOKENS // P
QT = S // P
BK = B * SK
HG = 8
UW = HG * SK
BANK = 512
EPS = 1e-5
BUCKETS = 32
DELTAS = S + SK - 1
ROUTED_TILES = {0: TILES + 8, 1: TILES + 8, 3: 2 * TILES + 16}
SLOTS = ROUTED_TILES[3] * P
CAPACITY = 320
UPTO = None
STAGES = 9
HID = 512
BIG_ROW = -(2.0 ** 100)
MASKED_L1 = -1e9
MASKED_L2 = -1e4


def relative_buckets():
    rp = np.arange(DELTAS) - (S - 1)
    half = BUCKETS // 2
    exact = half // 2
    dist = np.abs(rp)
    ratio = np.log(np.maximum(dist, 1).astype(np.float32) / np.float32(exact)).astype(np.float32)
    large = exact + (ratio / np.float32(np.log(128 / exact)) * np.float32(half - exact)).astype(np.int32)
    large = np.minimum(large, half - 1)
    return (rp > 0) * half + np.where(dist < exact, dist, large)


def shape_constants():
    c = {}
    c["ident"] = np.eye(P, dtype=np.float32)
    for name, hd in (("heads8", 8), ("heads16", 16)):
        n = P // hd
        c[name] = (np.arange(P)[:, None] // hd == np.arange(n)[None, :]).astype(np.float32)
    c["earlier"] = (np.arange(P)[:, None] < np.arange(P)[None, :]).astype(np.float32)
    c["bucket_hot"] = (np.arange(BUCKETS)[:, None] == relative_buckets()[None, ::-1]).astype(np.float32)
    j = np.arange(0, 16, 2, dtype=np.float32)
    inv = (np.float32(1.0) / np.power(np.float32(10000.0), j / np.float32(16))).astype(np.float32)
    freq = np.arange(S, dtype=np.float32)[None, :] * inv[:, None]
    cos, sin = np.cos(freq).astype(np.float32), np.sin(freq).astype(np.float32)
    c["rope_cos"] = np.tile(np.concatenate([cos, cos]), (8, 1))
    c["rope_sin"] = np.tile(np.concatenate([-sin, sin]), (8, 1))
    for e in (8, 16):
        c[f"rev{e}"] = np.broadcast_to(np.arange(e, 0, -1, dtype=np.float32), (P, TILES, e)).reshape(P, TILES * e)
        c[f"step{e}"] = np.broadcast_to(np.arange(TILES, dtype=np.float32) * P, (P, e, TILES)).reshape(P, e * TILES)
        keep = np.ones((P, e, TILES), np.float32)
        keep[:, :, 0] = 0
        c[f"carry{e}"] = keep.reshape(P, e * TILES)
    n = ROUTED_TILES[0]
    c["slot8"] = np.broadcast_to(np.arange(n, dtype=np.float32)[None, :, None], (P, n, 8)).reshape(P, n * 8)
    n = ROUTED_TILES[3]
    c["slot16"] = np.broadcast_to(np.arange(n, dtype=np.float32)[None, :, None], (P, n, 16)).reshape(P, n * 16)
    return {k: np.ascontiguousarray(v, dtype=np.float32) for k, v in c.items()}


def flamingo_kernel(nc, d, out):
    f32, bf16, i32, u8 = mybir.dt.float32, mybir.dt.bfloat16, mybir.dt.int32, mybir.dt.uint8
    ALU, ACT, AX = mybir.AluOpType, mybir.ActivationFunctionType, mybir.AxisListType
    ds = bass.ds

    ctx = ExitStack()
    with ctx:
        ctx.enter_context(nc.allow_non_contiguous_dma(reason="small vectors and Toeplitz rows"))

        def sb(name, cols, dt=f32, parts=P):
            return ctx.enter_context(nc.sbuf_tensor(name, [parts, cols], dt))

        def sem(name):
            return ctx.enter_context(nc.semaphore(name))

        x = sb("x", TILES * D)
        xn_all = sb("xn_all", TILES * D)
        region_a = sb("region_a", 9 * 1024 + 9 * 512)
        region_b = sb("region_b", 9 * 704 + 9 * 384)
        region_c = sb("region_c", 4 * 16 * SK)
        keys = sb("keys", B * 16 * SK)
        values = sb("values", B * 16 * 9, parts=SK)
        ctxT = sb("ctxT", BK)
        kT = sb("kT", BK)
        ident = sb("ident", P)
        earlier = sb("earlier", P, bf16)
        ones_bf = sb("ones_bf", P, bf16)
        ones_row = sb("ones_row", P, parts=1)
        heads8 = sb("heads8", 16)
        heads16 = sb("heads16", 8)
        wq = sb("wq", D)
        wk = sb("wk", D)
        wv = sb("wv", D)
        wo = sb("wo", D)
        wqs = sb("wqs", D)
        wks = sb("wks", D)
        cols = sb("cols", 4)
        colk2 = sb("colk2", 24)
        brow = sb("brow", 5 * D, parts=1)
        gates_in = sb("gates_in", 8)
        tanh_g = sb("tanh_g", 8)
        stats = sb("stats", TILES * 6)
        mean_var = sb("mean_var", TILES * 2)
        rstd = sb("rstd", TILES)
        var_eps = sb("var_eps", TILES)
        minus_half = sb("minus_half", TILES)
        ones16 = sb("ones16", 16)
        xin = [sb(f"xin{s}", D) for s in range(2)]
        xnT = [sb(f"xnT{s}", D) for s in range(2)]
        qT = [sb(f"qT{s}", D) for s in range(2)]
        row_max = [sb(f"row_max{s}", HG) for s in range(2)]
        row_sum = [sb(f"row_sum{s}", HG) for s in range(2)]
        row_inv = [sb(f"row_inv{s}", HG) for s in range(2)]
        probs = [sb(f"probs{s}", UW) for s in range(2)]
        probsT = [sb(f"probsT{s}", HG * P, parts=SK) for s in range(2)]
        out_inv = [sb(f"out_inv{s}", 16) for s in range(2)]
        out_n = [sb(f"out_n{s}", D) for s in range(2)]
        outT = sb("outT", D)
        bucket_hot = xn_all[0:BUCKETS, 0:DELTAS]
        rel_by_delta = xn_all[0:16, DELTAS:2 * DELTAS]
        rope_cos, rope_sin = xn_all[:, 0:S], xn_all[:, S:2 * S]
        rel_T = sb("rel_T", 16, parts=BUCKETS)
        mask1_raw = sb("mask1_raw", BK, u8, parts=1)
        mask1_row = sb("mask1_row", BK, bf16, parts=1)
        mask2 = sb("mask2", TILES * SK, u8)
        mask2_tile = [sb(f"mask2_tile{s}", SK, u8) for s in range(2)]
        masked2 = sb("masked2", 1)
        wait_slot = sb("wait_slot", 1)
        router_w = sb("router_w", 16)
        hid = [sb(f"hid{s}", HID) for s in range(2)]
        hidT = [sb(f"hidT{s}", HID) for s in range(2)]
        earlier_f = hid[1][:, 0:D]
        ropeA, ropeB = hid[0][:, 0:D], hid[1][:, 0:D]
        y_out = [sb(f"y_out{s}", D) for s in range(2)]
        NR = TILES * 16
        region_r = sb("region_r", 10 * NR)
        r = {n: region_r[:, k * NR:(k + 1) * NR] for k, n in enumerate(
            ("logit", "a", "b", "hot1", "hot2", "tot1", "tot2", "scan1", "scan2", "prob"))}
        r_bf = [sb(f"r_bf{k}", NR, bf16) for k in range(2)]
        rc = {n: sb(f"rc_{n}", NR) for n in ("rev", "step", "carry")}
        slot_no = sb("slot_no", ROUTED_TILES[3] * 16)
        r_m = {n: sb(f"rm_{n}", 16) for n in ("m1", "m2", "m3", "cnt", "cnt1", "nt", "cum", "base", "w1", "w2", "sum", "pf", "kp", "sr")}
        pos = [sb(f"pos{k}", TILES, i32) for k in range(2)]
        expert_f = sb("expert_f", ROUTED_TILES[3])
        expert_of = sb("expert_of", ROUTED_TILES[3], i32)
        tail = 9 * 1536 - 3 * HID
        up_fold = region_a[:, tail:tail + 2 * HID]
        down_fold = region_a[:, tail + 2 * HID:]
        zeros = y_out[0]
        q_bias_row = region_b[0:1, 0:B * 16 * SK]

        psum = ctx.enter_context(nc.psum_tensor("psum", [P, 8 * BANK], f32))

        def bank(n, a=0, b=BANK, parts=P):
            return psum[0:parts, n * BANK + a:n * BANK + b]

        sorted_in = nc.dram_tensor("sorted_in", (SLOTS, D), f32).ap()
        sorted_out = {l: nc.dram_tensor(f"sorted_out{l}", (n * P, D), f32).ap() for l, n in ROUTED_TILES.items()}
        rel_dram = nc.dram_tensor("rel_dram", (16, DELTAS), f32)

        s = {n: sem(n) for n in (
            "phase_done", "loaded_first", "loaded_rest", "zeros_set", "slots_zeroed", "consts_set",
            "kv_psum", "kv_sbuf", "kv_chain", "rel_stored", "bias_loaded", "reloaded", "reloaded_b",
            "xn_ready", "xnT_psum", "xnT_sbuf", "qT_psum", "qT_sbuf", "rope_step",
            "scores_psum", "scores_prep", "row_max_done", "scores_shifted", "probs_ready",
            "probs_summed", "probs_inverted", "probs_scaled", "probsT_psum", "probsT_sbuf",
            "out_psum", "out_inverted", "out_scaled", "outT_psum", "outT_sbuf", "proj_psum", "x_new", "stats_done",
            "mask2_copied", "dve_chain", "pool_chain", "act_chain", "logits_psum", "rank_psum",
            "hots_ready", "pos_ready", "scattered", "up_psum", "act_ready", "hid_ready", "hidT_psum", "hidT_sbuf",
            "y_psum", "y_taken", "gathered", "bfly_loaded", "bfly_done", "stored",
            "tanh_done", "kv_evac", "mask_row_done", "l1_loaded", "rope_q", "tables_loaded", "experts_loaded", "rel_psum", "rel_evac", "kv_evac_v", "kv_evac_a", "rstd_ready", "mean_var_done",
            "fold_psum", "fold_done", "gate_ready", "softmax_done", "router_chain", "rank_done", "combined")}
        xin_loaded = [sem(f"xin_loaded{k}") for k in range(2)]
        y_stored = [sem(f"y_stored{k}") for k in range(2)]

        def count_from(done):
            return dict(done)

        def pairs(eng, n_pairs, body):
            body(0)
            with eng.Fori(1, n_pairs - 1) as i:
                body(i)
            body(n_pairs - 1)

        def exists(t, n):
            return 0 <= t < n if isinstance(t, int) else True

        ENGINES = 5

        def phase_end(eng, no):
            eng.drain().then_inc(s["phase_done"], 1)
            eng.wait_ge(s["phase_done"], ENGINES * no)

        ATT = {l: dict(layer=l, units=1 if l == 3 else 2) for l in range(4)}
        FFN = {0: dict(E=8, F=HID, act=ACT.Gelu), 1: dict(E=8, F=352, act=ACT.Silu),
               2: dict(E=0, F=HID, act=ACT.Gelu), 3: dict(E=16, F=128, act=ACT.Silu)}
        phases = [("load", 0, 0)]
        for l in range(4):
            phases.append(("stats", l, 0))
            phases.append(("keys", l, 0))
            phases.append(("attention", l, 0))
            phases.append(("stats", l, 1))
            if l == 2:
                phases.append(("dense", l, 0))
            else:
                if l == 1:
                    phases.append(("fold", l, 0))
                phases.append(("router", l, 0))
                if l < 2:
                    phases.append(("shared", l, 0))
                phases.append(("routed", l, 0))
                phases.append(("combine", l, 0))

        phases = phases[:UPTO]
        TILE_SEMS = ("xn_ready", "xnT_psum", "xnT_sbuf")
        totals, at = {k: 0 for k in s}, []
        totals |= {"xin_pairs": 0, "y_pairs": 0}
        for kind, l, _ in phases:
            at.append(dict(totals))
            if kind == "attention":
                units = TILES * ATT[l]["units"]
                for k in TILE_SEMS:
                    totals[k] += TILES
                if l != 2:
                    for k in ("qT_psum", "qT_sbuf", "out_psum", "out_inverted", "out_scaled", "outT_psum", "outT_sbuf"):
                        totals[k] += TILES
                for k in ("proj_psum", "x_new"):
                    totals[k] += TILES
                for k in ("scores_psum", "row_max_done", "scores_shifted", "probs_ready", "probsT_psum", "probsT_sbuf"):
                    totals[k] += units
                if l in (1, 2):
                    totals["scores_prep"] += units
                if l == 1:
                    totals["row_max_done"] += units
                if l == 2:
                    for k in ("probs_summed", "probs_inverted", "probs_scaled"):
                        totals[k] += units
                    totals["mask2_copied"] += TILES
                if l == 3:
                    totals["rope_step"] += 2 * TILES
            if kind == "router":
                for k in TILE_SEMS:
                    totals[k] += TILES
                totals["logits_psum"] += TILES
            if kind == "fold":
                pass
            if kind in ("shared", "dense"):
                for k in TILE_SEMS + ("up_psum", "act_ready", "hid_ready", "hidT_psum", "hidT_sbuf", "y_psum", "x_new"):
                    totals[k] += TILES
            if kind == "routed":
                n = ROUTED_TILES[l]
                for k in ("xnT_psum", "xnT_sbuf", "up_psum", "act_ready", "hid_ready", "hidT_psum", "hidT_sbuf", "y_psum", "y_taken"):
                    totals[k] += n
                totals["xin_pairs"] += n // 2
                totals["y_pairs"] += n // 2
        scatters_before, n_scat = {}, 0
        for l in (0, 1, 3):
            scatters_before[l] = n_scat
            n_scat += TILES * (2 if l == 3 else 1)

        up_w = {0: region_a[:, 0:9 * 1024], 1: region_b[:, 0:9 * 704], 3: region_b[:, 0:16 * 256]}
        down_w = {0: region_a[:, 9 * 1024:9 * 1536], 1: region_b[:, 9 * 704:9 * 1088], 3: region_b[:, 4096:4096 + 16 * 128]}
        vw = region_a[0:SK, 0:B * 16 * D]
        wkT2, wvT2 = region_a[:, 8192:9216], region_a[:, 9216:10240]
        wq2, woT2 = region_a[:, 10240:11264], region_a[:, 11264:12288]
        kT2, vT2 = region_c[:, 0:8 * BK], region_c[:, 8 * BK:16 * BK]
        bias1 = region_c

        def chunks(F):
            return [(c, min(P, F - c)) for c in range(0, F, P)]

        def rows(name):
            return d[name].rearrange("(a n) -> a n", a=1)

        def expert_loads(l, shared_names, names):
            F, E = FFN[l]["F"], FFN[l]["E"]
            n = E + bool(shared_names)
            up = up_w[l].rearrange("p (e w f) -> p e w f", e=n, w=2)
            down = down_w[l].rearrange("p (e c o) -> p e c o", e=n, o=D)
            loads = [(up[:, 0:E, w, :], d[names[w]].rearrange("e p f -> p e f")) for w in range(2)]
            for c, (c0, cn) in enumerate(chunks(F)):
                loads.append((down[0:cn, 0:E, c, :], d[names[2]][:, c0:c0 + cn, :].rearrange("e p o -> p e o")))
            if shared_names:
                loads += [(up[:, E, w, :], d[shared_names[w]]) for w in range(2)]
                for c, (c0, cn) in enumerate(chunks(F)):
                    loads.append((down[0:cn, E, c, :], d[shared_names[2]][c0:c0 + cn, :]))
            return loads

        first_loads = [
            (x[:, :].rearrange("p (t e) -> p t e", e=D), d["x"].rearrange("(t p) e -> p t e", p=P)),
            (ctxT[:, :], d["ctxT"]), (ident[:, :], d["ident"]), (heads8[:, :], d["heads8"]),
            (heads16[:, :], d["heads16"]), (wq[:, :], d["L0_xattn_Wq"]), (wk[:, :], d["L0_xattn_Wk"]),
            (wv[:, :], d["L0_xattn_Wv"]), (wo[:, :], d["L0_xattn_Wo"]),
            (cols[:, 0:1], d["L0_xattn_bq"].rearrange("(p a) -> p a", a=1)),
            (cols[:, 1:2], d["L0_xattn_bk"].rearrange("(p a) -> p a", a=1)),
            (brow[0:1, 0:D], rows("L0_xattn_bv")), (brow[0:1, D:2 * D], rows("L0_xattn_bo")),
            (gates_in[:, 0:4], rows("g_xattn").to_broadcast([P, 4])),
            (gates_in[:, 4:8], rows("g_ffn").to_broadcast([P, 4])),
            (earlier_f[:, :], d["earlier"])]
        rest_loads = expert_loads(0, ("L0_ffn_w1s", "L0_ffn_w2s", "L0_ffn_w3s"), ("L0_ffn_W1", "L0_ffn_W2", "L0_ffn_W3"))
        rest_loads += [
            (rel_T[:, :], d["rel_T"]), (mask1_raw[:, :], d["mask1"]),
            (mask2[:, :].rearrange("p (t k) -> p t k", k=SK), d["mask2"].rearrange("(t p) k -> p t k", p=P)),
            (brow[0:1, 2 * D:3 * D], rows("L2_xattn_wOut_b")), (brow[0:1, 3 * D:4 * D], rows("L2_ffn_b_con")),
            (brow[0:1, 4 * D:5 * D], rows("L2_ffn_down_bias")),
            (colk2[:, 0:8], d["L2_xattn_wQ_b"].rearrange("(c p) -> p c", p=P)),
            (colk2[:, 8:16], d["L2_xattn_wK_b"].rearrange("(c p) -> p c", p=P)),
            (colk2[:, 16:24], d["L2_xattn_wV_b"].rearrange("(c p) -> p c", p=P))]
        next_loads = {
            0: [(ctxT[:, :], d["ctxT_backwards"]), (wq[:, :], d["L1_xattn_WqT"]), (wk[:, :], d["L1_xattn_WkT"]), (wv[:, :], d["L1_xattn_WvT"]),
                (wo[:, :], d["L1_xattn_WoT"]), (router_w[:, 0:8], d["L0_ffn_Wg"])]
               + [(rc[n][:, 0:TILES * 8], d[n + "8"]) for n in ("rev", "step", "carry")]
               + [(slot_no[:, 0:ROUTED_TILES[0] * 8], d["slot8"])],
            1: [(ctxT[:, :], d["ctxT"]), (wkT2, d["L2_xattn_WkT"]), (wvT2, d["L2_xattn_WvT"]),
                (wq2.rearrange("p (c e) -> p c e", e=D), d["L2_xattn_wQ_w"].rearrange("(c p) e -> p c e", p=P)),
                (woT2.rearrange("p (c e) -> p c e", e=D), d["L2_xattn_WoT"].rearrange("(c p) e -> p c e", p=P)),
                (router_w[:, 0:8], d["L1_ffn_router_DE"])],
            2: [(wq[:, :], d["L3_xattn_WqT"]), (wk[:, :], d["L3_xattn_WkT"]), (wv[:, :], d["L3_xattn_WvT"]),
                (wo[:, :], d["L3_xattn_WoT"]), (wqs[:, :], d["L3_xattn_WqT_swapped"]),
                (wks[:, :], d["L3_xattn_WkT_swapped"]), (router_w[:, :], d["L3_ffn_router_w"]),
                (rope_cos, d["rope_cos"]), (rope_sin, d["rope_sin"])]
               + [(rc[n][:, :], d[n + "16"]) for n in ("rev", "step", "carry")]
               + [(slot_no[:, :], d["slot16"])],
            3: []}
        next_experts = {
            0: expert_loads(1, ("L1_ffn_ws1_DF", "L1_ffn_ws3_DF", "L1_ffn_ws2_FD"),
                            ("L1_ffn_w1_eDF", "L1_ffn_w3_eDF", "L1_ffn_w2_eFD")),
            1: [], 2: expert_loads(3, None, ("L3_ffn_gate_w", "L3_ffn_up_w", "L3_ffn_down_w")), 3: []}

        KV = {0: dict(kv_psum=0, kv_evac_v=0), 1: dict(kv_psum=5, kv_evac_v=1), 2: dict(kv_psum=10, kv_evac_v=2),
              3: dict(kv_psum=58, kv_evac_v=34)}
        HOTS = {0: 0, 1: 1, 3: 2}
        GATHERS = {0: TILES, 1: 2 * TILES, 3: 4 * TILES}
        STATS = {no: sum(p[0] == "stats" for p in phases[:no]) for no in range(len(phases))}
        down_T = region_a[:, HID:2 * HID]

        block = ctx.enter_context(nc.Block())

        @block.sync
        def _(sp):
            for dst, src in first_loads:
                sp.dma_start(dst, src).then_inc(s["loaded_first"], 16)
            sp.wait_ge(s["zeros_set"], 1)
            sp.dma_start(sorted_in.rearrange("(t p) e -> p t e", p=P),
                         zeros[:, :].rearrange("p (a e) -> p a e", a=1).to_broadcast([P, ROUTED_TILES[3], D]))\
                .then_inc(s["slots_zeroed"], 16)
            for dst, src in rest_loads:
                sp.dma_start(dst, src).then_inc(s["loaded_rest"], 16)
            sp.wait_ge(s["loaded_first"], 16 * len(first_loads))

            reloads = experts = 0
            for no, (kind, l, sub) in enumerate(phases):
                z = at[no]
                if kind == "stats" and sub == 1:
                    for dst, src in next_loads[l]:
                        sp.dma_start(dst, src).then_inc(s["reloaded"], 16)
                    for dst, src in next_experts[l]:
                        sp.dma_start(dst, src).then_inc(s["experts_loaded"], 16)
                    reloads += len(next_loads[l])
                    experts += len(next_experts[l])
                    if l == 0:
                        sp.wait_ge(s["loaded_rest"], 16 * len(rest_loads))
                    sp.wait_ge(s["reloaded"], 16 * reloads)
                if kind == "router":
                    sp.wait_ge(s["experts_loaded"], 16 * experts) if l else None
                if kind == "keys" and l == 1:
                    sp.dma_start(bucket_hot, d["bucket_hot"]).then_inc(s["tables_loaded"], 16)
                if kind == "keys" and l == 1:
                    sp.wait_ge(s["rel_evac"], 2)
                    sp.dma_start(rel_dram.ap(), rel_by_delta).then_inc(s["rel_stored"], 16)
                    sp.wait_ge(s["rel_stored"], 16)
                    for q in range(QT):
                        src = bass.AP(rel_dram, q * P, [[1, P], [DELTAS, 16], [1, SK]])
                        sp.dma_start(bias1[:, q * 16 * SK:(q + 1) * 16 * SK].rearrange("p (h k) -> p h k", k=SK), src)\
                            .then_inc(s["bias_loaded"], 16)
                    sp.wait_ge(s["bias_loaded"], 16 * QT)
                if kind == "routed":
                    n = ROUTED_TILES[l]
                    if l == 0:
                        sp.wait_ge(s["slots_zeroed"], 16)
                    sp.wait_ge(s["scattered"], 16 * (scatters_before[l] + TILES * (2 if l == 3 else 1)))

                    def load(i, k):
                        t = 2 * i + k
                        sp.dma_start(xin[k][:, :], sorted_in[ds(t * P, P), :]).then_inc(xin_loaded[k], 16)

                    def store(t, k):
                        sp.wait_ge(s["y_taken"], z["y_taken"] + t + 1)
                        sp.dma_start(sorted_out[l][ds(t * P, P), :], y_out[k][:, :]).then_inc(y_stored[k], 16)

                    for k in range(2):
                        load(0, k)

                    def body(i):
                        for k in range(2):
                            t = 2 * i + k
                            if exists(t + 2, n):
                                sp.wait_ge(s["xnT_psum"], z["xnT_psum"] + t + 1)
                                load(i + 1, k)
                            if exists(t - 2, n):
                                store(t - 2, k)
                    pairs(sp, n // 2, body)
                    for k in range(2):
                        store(n - 2 + k, k)
                    for k in range(2):
                        sp.wait_ge(y_stored[k], 16 * (z["y_pairs"] + n // 2))
                phase_end(sp, no + 1)
            sp.dma_start(out.rearrange("(t p) e -> p t e", p=P), x[:, :].rearrange("p (t e) -> p t e", e=D)).then_inc(s["stored"], 16)
            sp.wait_ge(s["stored"], 16)

        def scores(k):
            two = psum[:, 2 * k * BANK:(2 * k + 2) * BANK].rearrange("p (a c) -> p a c", a=2)
            return two[:, :, 0:UW // 2].rearrange("p a (h k) -> p a h k", k=SK)

        def by_head(ap):
            return ap.rearrange("p (a h k) -> p a h k", a=2, k=SK)

        def over_keys(ap):
            return ap.rearrange("p (a h o) -> p a h o", a=2, o=1).to_broadcast([P, 2, HG // 2, SK])

        HD = {0: 8, 1: 8, 3: 16}
        TRANSPOSED = 4 * BANK
        OUT, MIX = 6, 7

        def tile_step_order(l):
            return 2 if l == 3 else 1

        @block.tensor
        def _(pe):
            mm, tr = nc.tensor.matmul, nc.tensor.transpose

            def keys_phase(l, z):
                if l == 2:
                    return keys_phase2(z)
                mm(bank(0, 0, BK), wk[:, :], ctxT[:, :], start=True, stop=True).then_inc(s["kv_psum"], 1)
                if l == 3:
                    mm(bank(1, 0, BK), wks[:, :], ctxT[:, :], start=True, stop=True).then_inc(s["kv_psum"], 1)
                for b in range(B):
                    o = bank(2 + b, 0, D, parts=SK)
                    if l == 0:
                        mm(o, ones_row[0:1, 0:SK], brow[0:1, 0:D], start=True, stop=False)
                    mm(o, ctxT[:, b * SK:(b + 1) * SK], wv[:, :], start=l != 0, stop=True).then_inc(s["kv_psum"], 1)
                if l == 1:
                    pe.wait_ge(s["tables_loaded"], 16)
                    mm(bank(6, 0, BANK, parts=16), rel_T[:, :], bucket_hot[:, 0:BANK], start=True, stop=True).then_inc(s["rel_psum"], 1)
                    mm(bank(7, 0, DELTAS - BANK, parts=16), rel_T[:, :], bucket_hot[:, BANK:DELTAS], start=True, stop=True)\
                        .then_inc(s["rel_psum"], 1)

            def keys_phase2(z):
                for j in range(16):
                    if j >= 8:
                        pe.wait_ge(s["kv_evac_v"], z["kv_evac_v"] + j - 8 + 1)
                    w, c = (wkT2, j) if j < 8 else (wvT2, j - 8)
                    mm(bank(j % 8, 0, BK), w[:, c * P:(c + 1) * P], ctxT[:, :], start=True, stop=True).then_inc(s["kv_psum"], 1)
                for h in range(16):
                    rows_h = slice(64 * (h % 2), 64 * (h % 2) + 64)
                    k_h = kT2[rows_h, (h // 2) * BK:(h // 2 + 1) * BK]
                    pe.wait_ge(s["kv_evac_v"], z["kv_evac_v"] + 16)
                    if h >= 4:
                        pe.wait_ge(s["kv_evac_a"], 2 * (h - 4) + 2)
                    mm(bank(2 * (h % 4), 0, BK), wq2[rows_h, (h // 2) * P:(h // 2 + 1) * P], k_h, start=True, stop=True)
                    mm(bank(2 * (h % 4) + 1, 0, BK, parts=1), colk2[rows_h, h // 2:h // 2 + 1], k_h, start=True, stop=True)\
                        .then_inc(s["kv_psum"], 1)
                pe.wait_ge(s["kv_evac_a"], 32)
                for j in range(B * 4):
                    if j >= 8:
                        pe.wait_ge(s["kv_evac_v"], z["kv_evac_v"] + 16 + j - 8 + 1)
                    b, g = j // 4, j % 4
                    for i in range(4):
                        h = 8 * (g // 2) + 2 * i + g % 2
                        rows_h = slice(64 * (h % 2), 64 * (h % 2) + 64)
                        last = mm(bank(j % 8, i * D, (i + 1) * D, parts=SK),
                                  vT2[rows_h, (h // 2) * BK + b * SK:(h // 2) * BK + (b + 1) * SK],
                                  woT2[rows_h, (h // 2) * P:(h // 2 + 1) * P], start=True, stop=True)
                    last.then_inc(s["kv_psum"], 1)

            def attention_phase(l, z):
                units = ATT[l]["units"]
                ahead = tile_step_order(l)

                def normalised(t, k):
                    pe.wait_ge(s["xn_ready"], z["xn_ready"] + t + 1)
                    tr(bank(MIX, 0, D), xin[k][:, :], ident[:, :]).then_inc(s["xnT_psum"], 1)

                def queries(t, k):
                    if l == 2:
                        return
                    pe.wait_ge(s["xnT_sbuf"], z["xnT_sbuf"] + t + 1)
                    last = mm(bank(MIX, D, 2 * D), wq[:, :], xnT[k][:, :], start=True, stop=True)
                    if l == 3:
                        last = mm(bank(MIX, 2 * D, 3 * D), wqs[:, :], xnT[k][:, :], start=True, stop=True)
                    last.then_inc(s["qT_psum"], 1)

                def score(t, h, k, kt, first_two):
                    u = t * units + h
                    if l == 2:
                        pe.wait_ge(s["xnT_sbuf"], z["xnT_sbuf"] + t + 1)
                    else:
                        pe.wait_ge(s["qT_sbuf"], z["qT_sbuf"] + t + 1)
                    if not first_two:
                        pe.wait_ge(s["scores_shifted"], z["scores_shifted"] + u - 1)
                    q = (xnT if l == 2 else qT)[kt]
                    b = t // QT
                    for half in range(2):
                        o = bank(2 * k + half, 0, UW // 2)
                        at_k = b * (units * UW) + h * UW + half * (UW // 2)
                        last = mm(o, q[:, :], keys[:, ds(at_k, UW // 2)], start=True, stop=l in (0, 3))
                        if l == 1:
                            last = mm(o, ones_bf[0:1, :], mask1_row[0:1, ds(b * SK, SK)].rearrange("p (a k) -> p a k", a=1)
                                      .to_broadcast([1, HG // 2, SK]), start=False, stop=True)
                        if l == 2:
                            last = mm(o, ones_row[0:1, :], q_bias_row[0:1, ds(at_k, UW // 2)], start=False, stop=True)
                    last.then_inc(s["scores_psum"], 1)

                def transpose_probs(t, h, k, very_first):
                    u = t * units + h
                    ready = "probs_scaled" if l == 2 else "probs_ready"
                    pe.wait_ge(s[ready], z[ready] + u + 1)
                    if not very_first:
                        pe.wait_ge(s["probsT_sbuf"], z["probsT_sbuf"] + u)
                    for i in range(HG):
                        last = tr(psum[0:SK, TRANSPOSED + i * P:TRANSPOSED + (i + 1) * P],
                                  probs[k][:, i * SK:(i + 1) * SK], ident[:, :])
                    last.then_inc(s["probsT_psum"], 1)

                def attend(t, h, k, first_tile):
                    u = t * units + h
                    pe.wait_ge(s["probsT_sbuf"], z["probsT_sbuf"] + u + 1)
                    b = t // QT
                    if h == 0 and not first_tile:
                        if l == 2:
                            pe.wait_ge(s["x_new"], z["x_new"] + t)
                        else:
                            pe.wait_ge(s["out_scaled"], z["out_scaled"] + t)
                    for i in range(HG):
                        hh = h * HG + i
                        pT = probsT[k][:, i * P:(i + 1) * P]
                        if l == 2:
                            if h == 0 and i == 0:
                                mm(bank(OUT, 0, D), ones_row[0:1, :], brow[0:1, 2 * D:3 * D], start=True, stop=False)
                            last = mm(bank(OUT, 0, D), pT, region_a[0:SK, ds(b * (16 * D) + hh * D, D)], start=False, stop=hh == 15)
                        else:
                            w = HD[l] + 1
                            last = mm(bank(OUT, hh * w, (hh + 1) * w), pT, values[:, ds(b * (units * HG * w) + hh * w, w)],
                                      start=True, stop=True)
                    if h == units - 1:
                        last.then_inc(s["proj_psum" if l == 2 else "out_psum"], 1)

                def out_transpose(t, k):
                    pe.wait_ge(s["out_scaled"], z["out_scaled"] + t + 1)
                    tr(bank(MIX, 3 * D, 4 * D) if l == 3 else bank(MIX, 2 * D, 3 * D), out_n[k][:, :], ident[:, :]).then_inc(s["outT_psum"], 1)

                def project(t):
                    pe.wait_ge(s["outT_sbuf"], z["outT_sbuf"] + t + 1)
                    o = bank(MIX, 0, D)
                    if l == 0:
                        mm(o, ones_row[0:1, :], brow[0:1, D:2 * D], start=True, stop=False)
                    mm(o, outT[:, :], wo[:, :], start=l != 0, stop=True).then_inc(s["proj_psum"], 1)

                def mix_free(t):
                    if l != 2 and exists(t, TILES):
                        pe.wait_ge(s["x_new"], z["x_new"] + t + 1)

                for t in range(ahead):
                    if t:
                        pe.wait_ge(s["qT_sbuf"], z["qT_sbuf"] + t)
                    normalised(t, t % 2)
                    queries(t, t % 2)
                score(0, 0, 0, 0, True)

                def body(i):
                    for k in range(2):
                        t = 2 * i + k
                        if l == 3:
                            if exists(t + 2, TILES):
                                mix_free(t - 3)
                                normalised(t + 2, k)
                            if exists(t + 1, TILES):
                                score(t + 1, 0, 1 - k, 1 - k, isinstance(t, int) and t < 1)
                            transpose_probs(t, 0, k, isinstance(t, int) and t == 0)
                            if exists(t + 2, TILES):
                                queries(t + 2, k)
                            if exists(t - 1, TILES):
                                attend(t - 1, 0, 1 - k, isinstance(t, int) and t == 1)
                            if exists(t - 2, TILES):
                                if exists(t + 2, TILES):
                                    pe.wait_ge(s["qT_sbuf"], z["qT_sbuf"] + t + 3)
                                else:
                                    mix_free(t - 3)
                                out_transpose(t - 2, k)
                                project(t - 2)
                        else:
                            if exists(t + 1, TILES):
                                mix_free(t - 2)
                                normalised(t + 1, 1 - k)
                            score(t, 1, 1, k, isinstance(t, int) and t == 0)
                            transpose_probs(t, 0, 0, isinstance(t, int) and t == 0)
                            if exists(t + 1, TILES):
                                queries(t + 1, 1 - k)
                            if exists(t - 1, TILES):
                                attend(t - 1, 1, 1, False)
                            if exists(t + 1, TILES):
                                score(t + 1, 0, 0, 1 - k, False)
                            transpose_probs(t, 1, 1, False)
                            attend(t, 0, 0, isinstance(t, int) and t == 0)
                            if l != 2 and exists(t - 1, TILES):
                                if not exists(t + 1, TILES):
                                    mix_free(t - 2)
                                out_transpose(t - 1, 1 - k)
                                project(t - 1)
                pairs(pe, TILES // 2, body)
                last = TILES - 1
                if l == 3:
                    attend(last, 0, 1, False)
                    for t in (last - 1, last):
                        mix_free(t - 1)
                        out_transpose(t, t % 2)
                        project(t)
                else:
                    attend(last, 1, 1, False)
                    if l != 2:
                        mix_free(last - 1)
                        out_transpose(last, 1)
                        project(last)

            def router_phase(l, z):
                E = FFN[l]["E"]

                def normalised(t, k, first):
                    pe.wait_ge(s["xn_ready"], z["xn_ready"] + t + 1)
                    if not first:
                        pe.wait_ge(s["xnT_sbuf"], z["xnT_sbuf"] + t)
                    tr(bank(MIX, 0, D), xin[k][:, :], ident[:, :]).then_inc(s["xnT_psum"], 1)
                normalised(0, 0, True)

                def body(i):
                    for k in range(2):
                        t = 2 * i + k
                        if exists(t + 1, TILES):
                            normalised(t + 1, 1 - k, False)
                        pe.wait_ge(s["xnT_sbuf"], z["xnT_sbuf"] + t + 1)
                        mm(psum[:, ds(t * E, E)], xnT[k][:, :], router_w[:, 0:E], start=True, stop=True).then_inc(s["logits_psum"], 1)
                pairs(pe, TILES // 2, body)
                for c in range(2 if l == 3 else 1):
                    pe.wait_ge(s["hots_ready"], HOTS[l] + c + 1)
                    mm(bank(1 + 2 * c, 0, TILES * E), earlier[:, :], r_bf[c][:, 0:TILES * E], start=True, stop=True)
                    mm(bank(2 + 2 * c, 0, TILES * E), ones_bf[:, :], r_bf[c][:, 0:TILES * E], start=True, stop=True)\
                        .then_inc(s["rank_psum"], 1)

            def ffn_phase(kind, l, z):
                F, E = FFN[l]["F"], FFN[l]["E"]
                n = ROUTED_TILES[l] if kind == "routed" else TILES
                C = len(chunks(F))

                def expert(t):
                    return pe.value_load(expert_of[0:1, ds(t, 1)], min_val=0, max_val=E - 1) if kind == "routed" else E

                def normalised(t, k, first):
                    if kind == "routed":
                        pe.wait_ge(xin_loaded[k], 16 * (z["xin_pairs"] + (t - k) // 2 + 1) if isinstance(t, int)
                                   else 16 * (z["xin_pairs"] + 1) + (t - k) * 8)
                    else:
                        pe.wait_ge(s["xn_ready"], z["xn_ready"] + t + 1)
                    if not first:
                        pe.wait_ge(s["xnT_sbuf"], z["xnT_sbuf"] + t)
                    tr(bank(7, 0, D), xin[k][:, :], ident[:, :]).then_inc(s["xnT_psum"], 1)

                def up(t, k, first_two):
                    e = expert(t)
                    pe.wait_ge(s["xnT_sbuf"], z["xnT_sbuf"] + t + 1)
                    if not first_two:
                        pe.wait_ge(s["hid_ready"], z["hid_ready"] + t - 1)
                    if kind == "dense":
                        last = mm(bank(k, 0, F), xnT[k][:, :], up_fold[:, 0:F], start=True, stop=True)
                    else:
                        w = up_w[l]
                        mm(bank(k, 0, F), xnT[k][:, :], w[:, ds(e * (2 * F), F)], start=True, stop=True)
                        last = mm(bank(2 + k, 0, F), xnT[k][:, :], w[:, ds(e * (2 * F) + F, F)], start=True, stop=True)
                    last.then_inc(s["up_psum"], 1)

                def hidden_transpose(t, k):
                    pe.wait_ge(s["hid_ready"], z["hid_ready"] + t + 1)
                    for c, (c0, cn) in enumerate(chunks(F)):
                        last = tr(bank(4 + k, c * P, (c + 1) * P, parts=cn), hid[k][:, c0:c0 + cn], ident[:, :])
                    last.then_inc(s["hidT_psum"], 1)

                def down(t, k, first):
                    e = expert(t)
                    pe.wait_ge(s["hidT_sbuf"], z["hidT_sbuf"] + t + 1)
                    if not first:
                        taken = "y_taken" if kind == "routed" else "x_new"
                        pe.wait_ge(s[taken], z[taken] + t)
                    o = bank(6, 0, D)
                    if kind == "dense":
                        mm(o, ones_row[0:1, :], brow[0:1, 3 * D:4 * D], start=True, stop=False)
                        mm(o, ones_row[0:1, :], brow[0:1, 4 * D:5 * D], start=False, stop=False)
                    for c, (c0, cn) in enumerate(chunks(F)):
                        w = down_fold[0:cn, c * D:(c + 1) * D] if kind == "dense" else down_w[l][0:cn, ds(e * (C * D) + c * D, D)]
                        last = mm(o, hidT[k][0:cn, c * P:(c + 1) * P], w, start=c == 0 and kind != "dense", stop=c == C - 1)
                    last.then_inc(s["y_psum"], 1)

                normalised(0, 0, True)
                normalised(1, 1, False)
                up(0, 0, True)

                def body(i):
                    for k in range(2):
                        t = 2 * i + k
                        if exists(t + 1, n):
                            up(t + 1, 1 - k, isinstance(t, int) and t == 0)
                        if exists(t + 2, n):
                            normalised(t + 2, k, False)
                        hidden_transpose(t, k)
                        if exists(t - 1, n):
                            down(t - 1, 1 - k, isinstance(t, int) and t == 1)
                pairs(pe, n // 2, body)
                down(n - 1, 1, False)

            for no, (kind, l, sub) in enumerate(phases):
                z = at[no]
                if kind == "keys":
                    keys_phase(l, KV[l])
                elif kind == "attention":
                    attention_phase(l, z)
                elif kind == "router":
                    router_phase(l, z)
                elif kind in ("shared", "routed", "dense"):
                    ffn_phase(kind, l, z)
                elif kind == "fold":
                    for c in range(4):
                        last = tr(bank(0, c * P, (c + 1) * P), down_T[:, c * P:(c + 1) * P], ident[:, :])
                    last.then_inc(s["fold_psum"], 1)
                phase_end(pe, no + 1)

        @block.scalar
        def _(act):
            run = nc.scalar.activation

            def keys_phase(l, z):
                if l == 2:
                    for h in range(16):
                        act.wait_ge(s["kv_psum"], z["kv_psum"] + 16 + h + 1)
                        run(keys[:, :].rearrange("p (b h k) -> p b h k", b=B, k=SK)[:, :, h, :],
                            bank(2 * (h % 4), 0, BK).rearrange("p (b k) -> p b k", k=SK), ACT.Copy, scale=0.125).then_inc(s["kv_evac_a"], 1)
                        run(q_bias_row.rearrange("p (b h k) -> p b h k", b=B, k=SK)[:, :, h, :],
                            bank(2 * (h % 4) + 1, 0, BK, parts=1).rearrange("p (b k) -> p b k", k=SK), ACT.Copy, scale=0.125)\
                            .then_inc(s["kv_evac_a"], 1)
                    return
                heads, w = (8, 17) if l == 3 else (16, 9)
                v = values[:, 0:B * heads * w].rearrange("p (b h w) -> p b h w", b=B, w=w)
                act.wait_ge(s["kv_evac_v"], z["kv_evac_v"] + 1)
                for b in range(B):
                    act.wait_ge(s["kv_psum"], z["kv_psum"] + (2 if l == 3 else 1) + b + 1)
                    run(v[:, b, :, 0:w - 1], bank(2 + b, 0, D, parts=SK).rearrange("p (h w) -> p h w", w=w - 1), ACT.Copy)
                if l == 1:
                    act.wait_ge(s["rel_psum"], 2)
                    run(rel_by_delta[:, 0:BANK], bank(6, 0, BANK, parts=16), ACT.Copy).then_inc(s["rel_evac"], 1)
                    run(rel_by_delta[:, BANK:DELTAS], bank(7, 0, DELTAS - BANK, parts=16), ACT.Copy).then_inc(s["rel_evac"], 1)

            def attention_phase(l, z):
                units = ATT[l]["units"]

                def normalised(t, k):
                    act.wait_ge(s["xnT_psum"], z["xnT_psum"] + t + 1)
                    run(xnT[k][:, :], bank(MIX, 0, D), ACT.Copy).then_inc(s["xnT_sbuf"], 1)

                def queries(t, k):
                    if l in (2, 3):
                        return
                    act.wait_ge(s["qT_psum"], z["qT_psum"] + t + 1)
                    if l == 0:
                        run(qT[k][:, :], bank(MIX, D, 2 * D), ACT.Identity, bias=cols[:, 0:1]).then_inc(s["qT_sbuf"], 1)
                    else:
                        run(qT[k][:, :], bank(MIX, D, 2 * D), ACT.Copy).then_inc(s["qT_sbuf"], 1)

                def exps(t, h, k):
                    act.wait_ge(s["scores_shifted"], z["scores_shifted"] + t * units + h + 1)
                    run(probs[k][:, :], probs[k][:, :], ACT.Exp).then_inc(s["probs_ready"], 1)

                def probs_copy(t, h, k):
                    act.wait_ge(s["probsT_psum"], z["probsT_psum"] + t * units + h + 1)
                    run(probsT[k][:, :], psum[0:SK, TRANSPOSED:TRANSPOSED + HG * P], ACT.Copy).then_inc(s["probsT_sbuf"], 1)

                def out_copy(t):
                    act.wait_ge(s["outT_psum"], z["outT_psum"] + t + 1)
                    run(outT[:, :], bank(MIX, 3 * D, 4 * D) if l == 3 else bank(MIX, 2 * D, 3 * D), ACT.Copy).then_inc(s["outT_sbuf"], 1)

                for t in range(tile_step_order(l)):
                    normalised(t, t % 2)
                    queries(t, t % 2)

                def body(i):
                    for k in range(2):
                        t = 2 * i + k
                        if l == 3:
                            if exists(t + 2, TILES):
                                normalised(t + 2, k)
                            exps(t, 0, k)
                            probs_copy(t, 0, k)
                            if exists(t - 2, TILES):
                                out_copy(t - 2)
                        else:
                            if exists(t + 1, TILES):
                                normalised(t + 1, 1 - k)
                            exps(t, 0, 0)
                            probs_copy(t, 0, 0)
                            if exists(t + 1, TILES):
                                queries(t + 1, 1 - k)
                            exps(t, 1, 1)
                            probs_copy(t, 1, 1)
                            if l != 2 and exists(t - 1, TILES):
                                out_copy(t - 1)
                pairs(act, TILES // 2, body)
                if l == 3:
                    out_copy(TILES - 2)
                if l != 2:
                    out_copy(TILES - 1)

            def router_phase(l, z):
                def body(i):
                    for k in range(2):
                        t = 2 * i + k
                        act.wait_ge(s["xnT_psum"], z["xnT_psum"] + t + 1)
                        run(xnT[k][:, :], bank(MIX, 0, D), ACT.Copy).then_inc(s["xnT_sbuf"], 1)
                pairs(act, TILES // 2, body)
                if l == 1:
                    act.wait_ge(s["hots_ready"], HOTS[l] + 1)
                    run(r_m["kp"][:, :], r_m["m1"][:, :], ACT.Sigmoid).then_inc(s["gate_ready"], 1)
                if l == 3:
                    act.wait_ge(s["softmax_done"], 1)
                    run(r["prob"], r["prob"], ACT.Exp).then_inc(s["softmax_done"], 1)

            def ffn_phase(kind, l, z):
                F = FFN[l]["F"]
                n = ROUTED_TILES[l] if kind == "routed" else TILES

                def normalised(t, k):
                    act.wait_ge(s["xnT_psum"], z["xnT_psum"] + t + 1)
                    run(xnT[k][:, :], bank(7, 0, D), ACT.Copy).then_inc(s["xnT_sbuf"], 1)

                def activate(t, k):
                    if kind == "dense":
                        act.wait_ge(s["act_ready"], z["act_ready"] + t + 1)
                        run(hid[k][:, 0:F], hid[k][:, 0:F], FFN[l]["act"]).then_inc(s["hid_ready"], 1)
                    else:
                        act.wait_ge(s["up_psum"], z["up_psum"] + t + 1)
                        run(hid[k][:, 0:F], bank(k, 0, F), FFN[l]["act"]).then_inc(s["act_ready"], 1)

                def take_y(t, k, first_two):
                    if kind != "routed":
                        return
                    act.wait_ge(s["y_psum"], z["y_psum"] + t + 1)
                    if not first_two:
                        act.wait_ge(y_stored[k], 16 * (z["y_pairs"] + (t - k) // 2) if isinstance(t, int) else 16 * z["y_pairs"] + (t - k) * 8)
                    run(y_out[k][:, :], bank(6, 0, D), ACT.Copy).then_inc(s["y_taken"], 1)

                normalised(0, 0)
                normalised(1, 1)
                activate(0, 0)

                def body(i):
                    for k in range(2):
                        t = 2 * i + k
                        if exists(t + 1, n):
                            activate(t + 1, 1 - k)
                        if exists(t + 2, n):
                            normalised(t + 2, k)
                        if exists(t - 1, n):
                            take_y(t - 1, 1 - k, isinstance(t, int) and t - 1 < 2)
                pairs(act, n // 2, body)
                take_y(n - 1, 1, False)

            for no, (kind, l, sub) in enumerate(phases):
                z = at[no]
                if kind == "load":
                    act.wait_ge(s["loaded_first"], 16 * len(first_loads))
                    run(tanh_g[:, :], gates_in[:, :], ACT.Tanh)
                elif kind == "keys":
                    keys_phase(l, KV[l])
                elif kind == "attention":
                    attention_phase(l, z)
                elif kind == "router":
                    router_phase(l, z)
                elif kind in ("shared", "routed", "dense"):
                    ffn_phase(kind, l, z)
                elif kind == "fold":
                    act.wait_ge(s["fold_psum"], 1)
                    run(down_fold[:, :], bank(0), ACT.Copy)
                phase_end(act, no + 1)

        @block.vector
        def _(dve):
            tt, copy = nc.vector.tensor_tensor, nc.vector.tensor_copy
            links = [0]

            def link(instruction):
                links[0] += 1
                instruction.then_inc(s["dve_chain"], 1)
                dve.wait_ge(s["dve_chain"], links[0])

            def x_tile(t):
                return x[:, ds(t * D, D)]

            def normalise(t, k, out_tile=None):
                return nc.vector.tensor_scalar(xin[k][:, :] if out_tile is None else out_tile, x_tile(t),
                                               mean_var[:, ds(2 * t, 1)], rstd[:, ds(t, 1)], ALU.subtract, ALU.mult)

            def update_x(t, y, gate, z, with_stats):
                nc.vector.scalar_tensor_tensor(x_tile(t), y, tanh_g[:, gate:gate + 1], x_tile(t), ALU.mult, ALU.add)\
                    .then_inc(s["x_new"], 1)
                if with_stats:
                    dve.wait_ge(s["x_new"], z["x_new"] + t + 1)
                    nc.vector.bn_stats(stats[:, ds(6 * t, 6)], x_tile(t))

            def all_stats():
                for t in range(TILES):
                    nc.vector.bn_stats(stats[:, 6 * t:6 * t + 6], x[:, t * D:(t + 1) * D])

            def stats_phase(l, sub):
                for t in range(TILES):
                    last = nc.vector.bn_aggr(mean_var[:, 2 * t:2 * t + 2], stats[:, 6 * t:6 * t + 6])
                last.then_inc(s["mean_var_done"], 1)

            def keys_phase(l, z):
                if l == 2:
                    for j in range(16):
                        dve.wait_ge(s["kv_psum"], z["kv_psum"] + j + 1)
                        dst = (kT2 if j < 8 else vT2)[:, (j % 8) * BK:(j % 8 + 1) * BK]
                        nc.vector.tensor_scalar(dst, bank(j % 8, 0, BK), colk2[:, 8 + j:9 + j], None, ALU.add)\
                            .then_inc(s["kv_evac_v"], 1)
                    for j in range(B * 4):
                        dve.wait_ge(s["kv_psum"], z["kv_psum"] + 32 + j + 1)
                        b, g = j // 4, j % 4
                        copy(vw.rearrange("p (b f i h e) -> p b f i h e", b=B, f=2, h=2, e=D)[:, b, g // 2, :, g % 2, :],
                             bank(j % 8, parts=SK).rearrange("p (i e) -> p i e", e=D)).then_inc(s["kv_evac_v"], 1)
                    return
                nc.vector.memset(values[:, :], 1.0).then_inc(s["kv_evac_v"], 1)
                if l == 1:
                    nc.vector.tensor_scalar(mask1_row[0:1, :], mask1_raw[0:1, :], 0.0, BIG_ROW, ALU.is_equal, ALU.mult)
                dve.wait_ge(s["kv_psum"], z["kv_psum"] + (2 if l == 3 else 1))
                if l == 0:
                    link(nc.vector.tensor_scalar(kT[:, :], bank(0, 0, BK), cols[:, 1:2], float(8.0 ** -0.5), ALU.add, ALU.mult))
                elif l == 1:
                    link(copy(kT[:, :], bank(0, 0, BK)))
                else:
                    rot = hid[0][:, 0:BK].rearrange("p (b k) -> p b k", k=SK)
                    k3 = kT[:, :].rearrange("p (b k) -> p b k", k=SK)
                    for table, n, o in ((rope_cos, 0, k3), (rope_sin, 1, rot)):
                        c = table[:, 0:SK].rearrange("p (b k) -> p b k", b=1).to_broadcast([P, B, SK])
                        last = tt(o, bank(n, 0, BK).rearrange("p (b k) -> p b k", k=SK), c, ALU.mult)
                    link(last)
                    link(tt(kT[:, :], kT[:, :], hid[0][:, 0:BK], ALU.add))
                    link(nc.vector.tensor_scalar(kT[:, :], kT[:, :], 0.25, None, ALU.mult))
                n, sel = (8, heads16) if l == 3 else (16, heads8)
                for b in range(B):
                    tt(keys[:, b * n * SK:(b + 1) * n * SK].rearrange("p (h k) -> p h k", k=SK),
                       kT[:, b * SK:(b + 1) * SK].rearrange("p (h k) -> p h k", h=1).to_broadcast([P, n, SK]),
                       sel[:, :].rearrange("p (h k) -> p h k", k=1).to_broadcast([P, n, SK]), ALU.mult)

            def attention_phase(l, z):
                units = ATT[l]["units"]

                def normalised(t, k, first_two):
                    if not first_two:
                        dve.wait_ge(s["xnT_psum"], z["xnT_psum"] + t - 1)
                    normalise(t, k).then_inc(s["xn_ready"], 1)

                def shift(t, h, k, first_two):
                    u = t * units + h
                    dve.wait_ge(s["scores_psum"], z["scores_psum"] + u + 1)
                    src = scores(k)
                    if not first_two:
                        dve.wait_ge(s["probsT_psum"], z["probsT_psum"] + u - 1)
                    if l == 1:
                        tt(by_head(probs[k][:, :]), src, by_head(bias1[:, ds((t % QT) * (2 * UW) + h * UW, UW)]), ALU.add)\
                            .then_inc(s["scores_prep"], 1)
                        dve.wait_ge(s["scores_prep"], z["scores_prep"] + u + 1)
                        src = by_head(probs[k][:, :])
                    if l == 2:
                        if h == 0:
                            dve.wait_ge(s["mask2_copied"], z["mask2_copied"] + t + 1)
                        kt = (t % 2) if isinstance(t, int) else tile_slot[0]
                        m = mask2_tile[kt][:, :].rearrange("p (a h k) -> p a h k", a=1, h=1).to_broadcast([P, 2, HG // 2, SK])
                        c = masked2[:, :].rearrange("p (a h k) -> p a h k", a=1, h=1).to_broadcast([P, 2, HG // 2, SK])
                        nc.vector.memset(wait_slot[:, :], 0.0)
                        nc.vector.copy_predicated(src, m, c).then_inc(s["scores_prep"], 1)
                        dve.wait_ge(s["scores_prep"], z["scores_prep"] + u + 1)
                    nc.vector.reduce_max(row_max[k][:, :].rearrange("p (a h) -> p a h", a=2), src, AX.X).then_inc(s["row_max_done"], 1)
                    n = 1
                    if l == 1:
                        dve.wait_ge(s["row_max_done"], z["row_max_done"] + 2 * u + 1)
                        nc.vector.tensor_scalar(row_max[k][:, :], row_max[k][:, :], MASKED_L1, None, ALU.max).then_inc(s["row_max_done"], 1)
                        dve.wait_ge(s["row_max_done"], z["row_max_done"] + 2 * u + 2)
                        p3 = probs[k][:, :].rearrange("p (h k) -> p h k", k=SK)
                        nc.vector.scalar_tensor_tensor(p3, p3, MASKED_L1, row_max[k][:, :].rearrange("p (h k) -> p h k", k=1)
                                                       .to_broadcast([P, HG, SK]), ALU.max, ALU.subtract).then_inc(s["scores_shifted"], 1)
                    else:
                        dve.wait_ge(s["row_max_done"], z["row_max_done"] + u + 1)
                        tt(by_head(probs[k][:, :]), src, over_keys(row_max[k][:, :]), ALU.subtract).then_inc(s["scores_shifted"], 1)

                def scale_probs(t, h, k):
                    if l != 2:
                        return
                    u = t * units + h
                    dve.wait_ge(s["probs_ready"], z["probs_ready"] + u + 1)
                    p3 = probs[k][:, :].rearrange("p (h k) -> p h k", k=SK)
                    nc.vector.reduce_sum(row_sum[k][:, :], p3, AX.X).then_inc(s["probs_summed"], 1)
                    dve.wait_ge(s["probs_summed"], z["probs_summed"] + u + 1)
                    nc.vector.reciprocal(row_inv[k][:, :], row_sum[k][:, :]).then_inc(s["probs_inverted"], 1)
                    dve.wait_ge(s["probs_inverted"], z["probs_inverted"] + u + 1)
                    tt(p3, p3, row_inv[k][:, :].rearrange("p (h k) -> p h k", k=1).to_broadcast([P, HG, SK]), ALU.mult)\
                        .then_inc(s["probs_scaled"], 1)

                def rotate(t, k):
                    dve.wait_ge(s["qT_psum"], z["qT_psum"] + t + 1)
                    at_q = ds((t % QT) * P, P)
                    tt(ropeA, bank(MIX, D, 2 * D), rope_cos[:, at_q], ALU.mult).then_inc(s["rope_step"], 1)
                    tt(ropeB, bank(MIX, 2 * D, 3 * D), rope_sin[:, at_q], ALU.mult).then_inc(s["rope_step"], 1)
                    dve.wait_ge(s["rope_step"], z["rope_step"] + 2 * t + 2)
                    tt(qT[k][:, :], ropeA, ropeB, ALU.add).then_inc(s["qT_sbuf"], 1)

                def scale_out(t, k):
                    if l == 2:
                        return
                    w = HD[l] + 1
                    o = bank(OUT, 0, units * HG * w).rearrange("p (h w) -> p h w", w=w)
                    dve.wait_ge(s["out_psum"], z["out_psum"] + t + 1)
                    inv = out_inv[k][:, 0:units * HG].rearrange("p (h o) -> p h o", o=1)
                    nc.vector.reciprocal(inv, o[:, :, w - 1:w]).then_inc(s["out_inverted"], 1)
                    dve.wait_ge(s["out_inverted"], z["out_inverted"] + t + 1)
                    tt(out_n[k][:, :].rearrange("p (h w) -> p h w", w=w - 1), o[:, :, 0:w - 1],
                       inv.to_broadcast([P, units * HG, w - 1]), ALU.mult).then_inc(s["out_scaled"], 1)

                def new_x(t):
                    dve.wait_ge(s["proj_psum"], z["proj_psum"] + t + 1)
                    update_x(t, bank(OUT if l == 2 else MIX, 0, D), l, z, True)

                tile_slot = [0]
                for t in range(tile_step_order(l)):
                    normalised(t, t, True)
                    if l == 3:
                        rotate(t, t)
                shift(0, 0, 0, True)

                def body(i):
                    for k in range(2):
                        t = 2 * i + k
                        early = isinstance(t, int)
                        if l == 3:
                            if exists(t + 2, TILES):
                                normalised(t + 2, k, False)
                            if exists(t + 1, TILES):
                                shift(t + 1, 0, 1 - k, early and t == 0)
                            if exists(t + 2, TILES):
                                rotate(t + 2, k)
                            if exists(t - 1, TILES):
                                scale_out(t - 1, 1 - k)
                            if exists(t - 2, TILES):
                                new_x(t - 2)
                        else:
                            if exists(t + 1, TILES):
                                normalised(t + 1, 1 - k, early and t == 0)
                            tile_slot[0] = k
                            shift(t, 1, 1, early and t == 0)
                            scale_probs(t, 0, 0)
                            if exists(t - 1, TILES):
                                scale_out(t - 1, 1 - k)
                            if exists(t + 1, TILES):
                                tile_slot[0] = 1 - k
                                shift(t + 1, 0, 0, False)
                            scale_probs(t, 1, 1)
                            if exists(t - 1, TILES):
                                new_x(t - 1)
                pairs(dve, TILES // 2, body)
                scale_out(TILES - 1, 1)
                if l == 3:
                    new_x(TILES - 2)
                new_x(TILES - 1)

            def first_best(values_, hot, E):
                v = values_[:, 0:TILES * E].rearrange("p (t e) -> p t e", e=E)
                a = r["a"][:, 0:TILES * E]
                a3 = a.rearrange("p (t e) -> p t e", e=E)
                top = r_m["m3"][:, :].rearrange("p (t e) -> p t e", e=1).to_broadcast([P, TILES, E])
                link(nc.vector.reduce_max(r_m["m3"][:, :], v, AX.X))
                link(tt(a3, v, top, ALU.is_equal))
                link(tt(a, a, rc["rev"][:, 0:TILES * E], ALU.mult))
                link(nc.vector.reduce_max(r_m["m2"][:, :], a3, AX.X))
                link(tt(hot[:, 0:TILES * E].rearrange("p (t e) -> p t e", e=E), a3,
                        r_m["m2"][:, :].rearrange("p (t e) -> p t e", e=1).to_broadcast([P, TILES, E]), ALU.is_equal))

            def router_phase(l, z):
                E = FFN[l]["E"]
                W = TILES * E
                choices = 2 if l == 3 else 1

                def te(ap):
                    return ap[:, 0:W].rearrange("p (t e) -> p t e", e=E)

                def et(ap):
                    return ap[:, 0:W].rearrange("p (e t) -> p e t", t=TILES)

                def t_by_e(ap):
                    return ap[:, 0:W].rearrange("p (e t) -> p t e", t=TILES)

                def body(i):
                    for k in range(2):
                        t = 2 * i + k
                        if not (isinstance(t, int) and t < 2):
                            dve.wait_ge(s["xnT_psum"], z["xnT_psum"] + t - 1)
                        normalise(t, k).then_inc(s["xn_ready"], 1)
                        normalise(t, k, xn_all[:, ds(t * D, D)])
                pairs(dve, TILES // 2, body)

                dve.wait_ge(s["logits_psum"], z["logits_psum"] + TILES)
                link(copy(r["logit"][:, 0:W], bank(0, 0, W)))
                first_best(r["logit"], r["hot1"], E)
                link(copy(r_m["m1"][:, :], r_m["m3"][:, :]))
                copy(r_bf[0][:, 0:W], r["hot1"][:, 0:W]).then_inc(s["hots_ready"], 1)
                if l == 3:
                    link(nc.vector.scalar_tensor_tensor(r["b"][:, 0:W], r["hot1"][:, 0:W], -3e38, r["logit"][:, 0:W], ALU.mult, ALU.add))
                    first_best(r["b"], r["hot2"], E)
                    copy(r_bf[1][:, 0:W], r["hot2"][:, 0:W]).then_inc(s["hots_ready"], 1)
                    tt(te(r["prob"]), te(r["logit"]), r_m["m1"][:, :].rearrange("p (t e) -> p t e", e=1)
                       .to_broadcast([P, TILES, E]), ALU.subtract).then_inc(s["softmax_done"], 1)
                dve.wait_ge(s["rank_psum"], HOTS[l] + choices)
                for c in range(choices):
                    tot, scan = r[f"tot{c + 1}"], r[f"scan{c + 1}"]
                    link(copy(et(tot), bank(2 + 2 * c, 0, W).rearrange("p (t e) -> p e t", e=E)))
                    link(nc.vector.tensor_tensor_scan(scan[:, 0:W], rc["carry"][:, 0:W], tot[:, 0:W], 0.0, ALU.mult, ALU.add))
                    link(copy(r_m["cnt1" if c == 0 else "kp"][:, 0:E], et(scan)[:, :, TILES - 1]))
                    link(tt(tot[:, 0:W], scan[:, 0:W], tot[:, 0:W], ALU.subtract))
                if choices == 2:
                    link(tt(r_m["cnt"][:, 0:E], r_m["cnt1"][:, 0:E], r_m["kp"][:, 0:E], ALU.add))
                else:
                    link(copy(r_m["cnt"][:, 0:E], r_m["cnt1"][:, 0:E]))
                link(tt(et(r["a"]), r_m["cnt"][:, 0:E].rearrange("p (e t) -> p e t", t=1).to_broadcast([P, E, TILES]),
                        et(rc["step"]), ALU.is_gt))
                link(nc.vector.reduce_sum(r_m["nt"][:, 0:E], et(r["a"]), AX.X))
                link(nc.vector.tensor_tensor_scan(r_m["cum"][:, 0:E], ones16[:, 0:E], r_m["nt"][:, 0:E], 0.0, ALU.mult, ALU.add))
                link(tt(r_m["base"][:, 0:E], r_m["cum"][:, 0:E], r_m["nt"][:, 0:E], ALU.subtract))
                link(nc.vector.tensor_scalar(r_m["base"][:, 0:E], r_m["base"][:, 0:E], float(P), None, ALU.mult))
                for c in range(choices):
                    hot = r[f"hot{c + 1}"]
                    link(tt(te(r["a"]), bank(1 + 2 * c, 0, W).rearrange("p (t e) -> p t e", e=E), t_by_e(r[f"tot{c + 1}"]), ALU.add))
                    link(tt(r["a"][:, 0:W], r["a"][:, 0:W], hot[:, 0:W], ALU.mult))
                    link(nc.vector.reduce_sum(r_m["sr"][:, :], te(r["a"]), AX.X))
                    if c == 1:
                        link(tt(r_m["base"][:, 0:E], r_m["base"][:, 0:E], r_m["cnt1"][:, 0:E], ALU.add))
                    link(tt(te(r["a"]), te(hot), r_m["base"][:, 0:E].rearrange("p (t e) -> p t e", t=1).to_broadcast([P, TILES, E]), ALU.mult))
                    link(nc.vector.reduce_sum(r_m["pf"][:, :], te(r["a"]), AX.X))
                    link(tt(r_m["pf"][:, :], r_m["pf"][:, :], r_m["sr"][:, :], ALU.add))
                    link(copy(pos[c][:, :], r_m["pf"][:, :]))
                    if l == 3:
                        w = r_m[f"w{c + 1}"]
                        link(nc.vector.tensor_scalar(r_m["kp"][:, :], r_m["sr"][:, :], float(CAPACITY), None, ALU.is_lt))
                        if c == 0:
                            dve.wait_ge(s["softmax_done"], 2)
                            link(nc.vector.reduce_sum(r_m["sum"][:, :], te(r["prob"]), AX.X))
                            link(nc.vector.reciprocal(r_m["sum"][:, :], r_m["sum"][:, :]))
                        link(tt(r["b"][:, 0:W], r["prob"][:, 0:W], hot[:, 0:W], ALU.mult))
                        link(nc.vector.reduce_sum(w[:, :], te(r["b"]), AX.X))
                        link(tt(w[:, :], w[:, :], r_m["sum"][:, :], ALU.mult))
                        link(tt(w[:, :], w[:, :], r_m["kp"][:, :], ALU.mult))
                n = ROUTED_TILES[l]
                over = psum[:, 5 * BANK:5 * BANK + n * E].rearrange("p (n e) -> p n e", e=E)
                link(tt(over, r_m["cum"][:, 0:E].rearrange("p (n e) -> p n e", n=1).to_broadcast([P, n, E]),
                        slot_no[:, 0:n * E].rearrange("p (n e) -> p n e", e=E), ALU.is_le))
                link(nc.vector.reduce_sum(expert_f[:, 0:n], over, AX.X))
                link(nc.vector.tensor_scalar(expert_f[:, 0:n], expert_f[:, 0:n], float(E - 1), None, ALU.min))
                link(copy(expert_of[:, 0:n], expert_f[:, 0:n]))
                if l == 1:
                    dve.wait_ge(s["gate_ready"], 1)
                    rows3 = xn_all[:, :].rearrange("p (t e) -> p t e", e=D)
                    link(tt(rows3, rows3, r_m["kp"][:, :].rearrange("p (t e) -> p t e", e=1).to_broadcast([P, TILES, D]), ALU.mult))

            def ffn_phase(kind, l, z):
                F = FFN[l]["F"]
                n = ROUTED_TILES[l] if kind == "routed" else TILES

                def normalised(t, k, first_two):
                    if kind == "routed":
                        return
                    if not first_two:
                        dve.wait_ge(s["xnT_psum"], z["xnT_psum"] + t - 1)
                    normalise(t, k).then_inc(s["xn_ready"], 1)

                def gate(t, k):
                    if kind == "dense":
                        dve.wait_ge(s["up_psum"], z["up_psum"] + t + 1)
                        tt(hid[k][:, :], bank(k), up_fold[:, HID:2 * HID], ALU.add).then_inc(s["act_ready"], 1)
                    else:
                        dve.wait_ge(s["act_ready"], z["act_ready"] + t + 1)
                        tt(hid[k][:, 0:F], hid[k][:, 0:F], bank(2 + k, 0, F), ALU.mult).then_inc(s["hid_ready"], 1)

                def hidden_copy(t, k):
                    dve.wait_ge(s["hidT_psum"], z["hidT_psum"] + t + 1)
                    full = F // P * P
                    last = copy(hidT[k][:, 0:full], bank(4 + k, 0, full))
                    if F > full:
                        last = copy(hidT[k][0:F - full, full:full + P], bank(4 + k, full, full + P, parts=F - full))
                    last.then_inc(s["hidT_sbuf"], 1)

                def new_x(t):
                    if kind == "routed":
                        return
                    dve.wait_ge(s["y_psum"], z["y_psum"] + t + 1)
                    update_x(t, bank(6, 0, D), 4 + l, z, kind == "dense")

                normalised(0, 0, True)
                normalised(1, 1, True)
                gate(0, 0)

                def body(i):
                    for k in range(2):
                        t = 2 * i + k
                        if exists(t + 1, n):
                            gate(t + 1, 1 - k)
                        if exists(t + 2, n):
                            normalised(t + 2, k, False)
                        hidden_copy(t, k)
                        if exists(t - 1, n):
                            new_x(t - 1)
                pairs(dve, n // 2, body)
                new_x(n - 1)

            def combine_phase(l):
                dve.wait_ge(s["gathered"], 16 * GATHERS[l])
                if l < 3:
                    link(nc.vector.scalar_tensor_tensor(x[:, :], xn_all[:, :], tanh_g[:, 4 + l:5 + l], x[:, :], ALU.mult, ALU.add))
                    all_stats()
                    return
                for buf, w in ((xn_all[:, :], "w1"), (keys[:, 0:TILES * D], "w2")):
                    y3 = buf.rearrange("p (t e) -> p t e", e=D)
                    link(tt(y3, y3, r_m[w][:, :].rearrange("p (t e) -> p t e", e=1).to_broadcast([P, TILES, D]), ALU.mult))
                    link(nc.vector.scalar_tensor_tensor(x[:, :], buf, tanh_g[:, 4 + l:5 + l], x[:, :], ALU.mult, ALU.add))

            for no, (kind, l, sub) in enumerate(phases):
                z = at[no]
                if kind == "load":
                    nc.vector.memset(zeros[:, :], 0.0).then_inc(s["zeros_set"], 1)
                    nc.vector.memset(ones_bf[:, :], 1.0)
                    nc.vector.memset(ones_row[:, :], 1.0)
                    nc.vector.memset(ones16[:, :], 1.0)
                    nc.vector.memset(minus_half[:, :], -0.5)
                    nc.vector.memset(masked2[:, :], MASKED_L2)
                    dve.wait_ge(s["loaded_first"], 16 * len(first_loads))
                    copy(earlier[:, :], earlier_f[:, :])
                    all_stats()
                elif kind == "stats":
                    stats_phase(l, sub)
                elif kind == "keys":
                    keys_phase(l, KV[l])
                elif kind == "attention":
                    attention_phase(l, z)
                elif kind == "router":
                    router_phase(l, z)
                elif kind in ("shared", "routed", "dense"):
                    ffn_phase(kind, l, z)
                elif kind == "combine":
                    combine_phase(l)
                phase_end(dve, no + 1)

        @block.gpsimd
        def _(pool):
            tt = nc.gpsimd.tensor_tensor
            links = [0]
            loads = [0]

            def link(instruction):
                links[0] += 1
                instruction.then_inc(s["pool_chain"], 1)
                pool.wait_ge(s["pool_chain"], links[0])

            def load(dst, src):
                loads[0] += 1
                pool.dma_start(dst, src).then_inc(s["bfly_loaded"], 16)
                pool.wait_ge(s["bfly_loaded"], 16 * loads[0])

            def butterfly(src, dst_last, other, temps, weights, w_sb, rows_, stages, transposed):
                bufs = [src, other]
                for n, stage in enumerate(stages):
                    load(w_sb, weights[stage, :, :, :].rearrange("(a k) i j -> a (k i j)", a=1).to_broadcast([P, 4 * (HID // 2)]))
                    st = 2 ** stage
                    nb = HID // (2 * st)
                    i, o = bufs[n % 2], dst_last if n == len(stages) - 1 else bufs[(n + 1) % 2]

                    def half(buf, which):
                        return buf.rearrange("p (r n h s) -> p r n h s", r=rows_, h=2, s=st)[:, :, :, which, :]

                    def weight(a, b):
                        c = 2 * b + a if transposed else 2 * a + b
                        w = w_sb.rearrange("p (r n s c) -> p r n s c", r=1, s=st, c=4)[:, :, :, :, c]
                        return w.to_broadcast([P, rows_, nb, st]) if rows_ > 1 else w

                    def temp(k):
                        return temps[k].rearrange("p (r n s) -> p r n s", r=rows_, s=st)
                    for a in range(2):
                        tt(temp(0), half(i, 0), weight(a, 0), ALU.mult)
                        link(tt(temp(1), half(i, 1), weight(a, 1), ALU.mult))
                        link(tt(half(o, a), temp(0), temp(1), ALU.add))

            for no, (kind, l, sub) in enumerate(phases):
                z = at[no]
                if kind == "stats":
                    pool.wait_ge(s["mean_var_done"], STATS[no] + 1)
                    link(nc.gpsimd.tensor_scalar(var_eps[:, :], mean_var[:, :].rearrange("p (t c) -> p t c", c=2)[:, :, 1],
                                                 EPS, None, ALU.add))
                    link(tt(rstd[:, :], var_eps[:, :], minus_half[:, :], ALU.pow))
                elif kind == "attention" and l == 1:
                    weights_sb, temps = region_a[:, 2048:3072], [region_a[:, 3072:3584], region_a[:, 3584:4096]]
                    load(region_a[:, 0:HID], d["L2_ffn_W_conT"])
                    butterfly(region_a[:, 0:HID], down_T, down_T, [t[:, 0:HID // 2] for t in temps], d["L2_ffn_down_weights"],
                              weights_sb, 1, list(range(STAGES))[::-1], True)
                    a, b2 = region_a[:, 4096:5120], region_a[:, 5120:6144]
                    load(a[:, 0:HID], d["L2_ffn_W_exp"])
                    load(a[:, HID:2 * HID], rows("L2_ffn_b_exp").to_broadcast([P, HID]))
                    load(region_a[:, 6144:6144 + HID], rows("L2_ffn_up_bias").to_broadcast([P, HID]))
                    butterfly(a, up_fold, b2, temps, d["L2_ffn_up_weights"], weights_sb, 2, list(range(STAGES)), False)
                    link(tt(up_fold[:, HID:], up_fold[:, HID:], region_a[:, 6144:6144 + HID], ALU.add))
                elif kind == "attention" and l == 2:
                    def body(i):
                        for k in range(2):
                            t = 2 * i + k
                            if not (isinstance(t, int) and t < 2):
                                pool.wait_ge(s["scores_prep"], z["scores_prep"] + 2 * (t - 1))
                            nc.gpsimd.tensor_copy(mask2_tile[k][:, :], mask2[:, ds(t * SK, SK)]).then_inc(s["mask2_copied"], 1)
                    pairs(pool, TILES // 2, body)
                elif (kind == "shared") or (kind == "routed" and l == 3):
                    pool.wait_ge(s["slots_zeroed"], 16)
                    for c in range(2 if l == 3 else 1):
                        for t in range(TILES):
                            pool.indirect_dma_start(sorted_in, bass.IndirectOffsetOnAxis(ap=pos[c][:, t:t + 1], axis=0),
                                                    xn_all[:, t * D:(t + 1) * D], None).then_inc(s["scattered"], 16)
                elif kind == "combine":
                    for c in range(2 if l == 3 else 1):
                        buf = keys if c else xn_all
                        for t in range(TILES):
                            pool.indirect_dma_start(buf[:, t * D:(t + 1) * D], None, sorted_out[l],
                                                    bass.IndirectOffsetOnAxis(ap=pos[c][:, t:t + 1], axis=0)).then_inc(s["gathered"], 16)
                phase_end(pool, no + 1)


def kernel(**inputs):
    import numpy as _np
    import concourse.bacc as _bacc
    from concourse import mybir as _mybir
    from concourse.bass_utils import run_bass_kernel_spmd as _run

    a = {k: _np.asarray(v) for k, v in inputs.items()}
    T = lambda m: _np.ascontiguousarray(_np.swapaxes(m, -1, -2))
    keep = {"g_xattn", "g_ffn"}
    g = {k: a[k] for k in a if k in keep or (k.startswith("L") and k not in (
        "L1_xattn_Wq", "L1_xattn_Wk", "L1_xattn_Wv", "L1_xattn_Wo", "L1_xattn_rel_bias", "L2_xattn_wK_w", "L2_xattn_wV_w",
        "L2_xattn_wOut_w", "L2_ffn_W_con", "L3_xattn_Wq", "L3_xattn_Wkv", "L3_xattn_Wout"))}
    g["x"] = a["x"].reshape(TOKENS, D)
    g["ctxT"] = T(a["ctx_1024"].reshape(BK, D))
    g["ctxT_backwards"] = T(a["ctx_1024"][:, ::-1].reshape(BK, D))
    for n in ("Wq", "Wk", "Wv", "Wo"):
        g[f"L1_xattn_{n}T"] = T(a[f"L1_xattn_{n}"])
    g["rel_T"] = T(a["L1_xattn_rel_bias"])
    g["L2_xattn_WkT"], g["L2_xattn_WvT"] = T(a["L2_xattn_wK_w"]), T(a["L2_xattn_wV_w"])
    g["L2_xattn_WoT"] = T(a["L2_xattn_wOut_w"])
    g["L2_ffn_W_conT"] = T(a["L2_ffn_W_con"])
    halves = _np.arange(D).reshape(8, 2, 8)[:, ::-1, :].reshape(D)
    wk3, wv3 = a["L3_xattn_Wkv"][:D], a["L3_xattn_Wkv"][D:]
    g["L3_xattn_WqT"], g["L3_xattn_WqT_swapped"] = T(a["L3_xattn_Wq"]), T(a["L3_xattn_Wq"][halves])
    g["L3_xattn_WkT"], g["L3_xattn_WkT_swapped"] = T(wk3), T(wk3[halves])
    g["L3_xattn_WvT"], g["L3_xattn_WoT"] = T(wv3), T(a["L3_xattn_Wout"])
    g["mask1"] = _np.ascontiguousarray(a["mask_Bx1x1xS2_bk0"].reshape(B, SK)[:, ::-1]).reshape(1, BK)
    g["mask2"] = a["mask_BxSxS2_bf0"].reshape(TOKENS, SK)
    g.update(shape_constants())

    nc = _bacc.Bacc("TRN2", target_bir_lowering=False, num_devices=1)
    arrays, d = {}, {}
    for name, v in g.items():
        v = _np.ascontiguousarray(v)
        arrays[f"in_{name}"] = v
        d[name] = nc.dram_tensor(f"in_{name}", v.shape, _mybir.dt.from_np(v.dtype), kind="ExternalInput").ap()
    out = nc.dram_tensor("out_x", (TOKENS, D), _mybir.dt.float32, kind="ExternalOutput").ap()
    flamingo_kernel(nc, d, out)
    r = _run(nc, [arrays], core_ids=[0])
    return r.results[0]["out_x"].reshape(B, S, D)
```

```python
import numpy as np

import concourse.bass as bass
from concourse import mybir
from contextlib import ExitStack

P = 128
B, S, SK, D = 4, 512, 77, 128
TOKENS = B * S
TILES = TOKENS // P
QT = S // P
BK = B * SK
HG = 8
UW = HG * SK
CHUNKS = tuple(min(c, UW - P) for c in range(0, UW, P))
NC = len(CHUNKS)
TW = NC * P
BANK = 512
EPS = 1e-5
BUCKETS = 32
DELTAS = S + SK - 1
ROUTED_TILES = {0: TILES + 8, 1: TILES + 8, 3: 2 * TILES + 16}
SLOTS = ROUTED_TILES[3] * P
CAPACITY = 320
UPTO = None
STAGES = 9
HID = 512
BIG_ROW = -(2.0 ** 100)
MASKED_L1 = -1e9
MASKED_L2 = -1e4


def relative_buckets():
    rp = np.arange(DELTAS) - (S - 1)
    half = BUCKETS // 2
    exact = half // 2
    dist = np.abs(rp)
    ratio = np.log(np.maximum(dist, 1).astype(np.float32) / np.float32(exact)).astype(np.float32)
    large = exact + (ratio / np.float32(np.log(128 / exact)) * np.float32(half - exact)).astype(np.int32)
    large = np.minimum(large, half - 1)
    return (rp > 0) * half + np.where(dist < exact, dist, large)


def shape_constants():
    c = {}
    c["ident"] = np.eye(P, dtype=np.float32)
    for name, hd in (("heads8", 8), ("heads16", 16)):
        n = P // hd
        c[name] = (np.arange(P)[:, None] // hd == np.arange(n)[None, :]).astype(np.float32)
    row = np.arange(P)[:, None] + np.array(CHUNKS)[None, :]
    seen = np.array([0] + [c + P for c in CHUNKS[:-1]])[None, :]
    c["row_head"] = ((row[:, :, None] // SK == np.arange(HG)) & (row >= seen)[:, :, None]).astype(np.float32).reshape(P, NC * HG)
    half, chunk, h = np.ogrid[0:P, 0:8, 0:16]
    c["half_head"] = ((h == 2 * chunk + half // 64)).astype(np.float32).reshape(P, 8 * 16)
    c["earlier"] = (np.arange(P)[:, None] < np.arange(P)[None, :]).astype(np.float32)
    c["bucket_hot"] = (np.arange(BUCKETS)[:, None] == relative_buckets()[None, ::-1]).astype(np.float32)
    j = np.arange(0, 16, 2, dtype=np.float32)
    inv = (np.float32(1.0) / np.power(np.float32(10000.0), j / np.float32(16))).astype(np.float32)
    freq = np.arange(S, dtype=np.float32)[None, :] * inv[:, None]
    cos, sin = np.cos(freq).astype(np.float32), np.sin(freq).astype(np.float32)
    c["rope_cos"] = np.tile(np.concatenate([cos, cos]), (8, 1))
    c["rope_sin"] = np.tile(np.concatenate([-sin, sin]), (8, 1))
    for e in (8, 16):
        c[f"rev{e}"] = np.broadcast_to(np.arange(e, 0, -1, dtype=np.float32), (P, TILES, e)).reshape(P, TILES * e)
        c[f"step{e}"] = np.broadcast_to(np.arange(TILES, dtype=np.float32) * P, (P, e, TILES)).reshape(P, e * TILES)
        keep = np.ones((P, e, TILES), np.float32)
        keep[:, :, 0] = 0
        c[f"carry{e}"] = keep.reshape(P, e * TILES)
    c["digits"] = np.broadcast_to(np.tile(16.0 ** np.arange(4), ROUTED_TILES[3] // 4), (P, ROUTED_TILES[3]))
    n = ROUTED_TILES[0]
    c["slot8"] = np.broadcast_to(np.arange(n, dtype=np.float32)[None, :, None], (P, n, 8)).reshape(P, n * 8)
    n = ROUTED_TILES[3]
    c["slot16"] = np.broadcast_to(np.arange(n, dtype=np.float32)[None, :, None], (P, n, 16)).reshape(P, n * 16)
    return {k: np.ascontiguousarray(v, dtype=np.float32) for k, v in c.items()}


def flamingo_kernel(nc, d, out):
    f32, bf16, i32, u8 = mybir.dt.float32, mybir.dt.bfloat16, mybir.dt.int32, mybir.dt.uint8
    ALU, ACT, AX = mybir.AluOpType, mybir.ActivationFunctionType, mybir.AxisListType
    ds = bass.ds

    ctx = ExitStack()
    with ctx:
        ctx.enter_context(nc.allow_non_contiguous_dma(reason="small vectors and Toeplitz rows"))

        def sb(name, cols, dt=f32, parts=P):
            return ctx.enter_context(nc.sbuf_tensor(name, [parts, cols], dt))

        def sem(name):
            return ctx.enter_context(nc.semaphore(name))

        x = sb("x", TILES * D)
        xn_all = sb("xn_all", TILES * D)
        region_a = sb("region_a", 9 * 1024 + 9 * 512)
        region_b = sb("region_b", 9 * 704 + 9 * 384)
        region_c = sb("region_c", 4 * 16 * SK)
        keys = sb("keys", B * 16 * SK)
        ctxT = sb("ctxT", BK)
        kT = sb("kT", BK)
        ident = sb("ident", P)
        earlier = sb("earlier", P, bf16)
        ones_bf = sb("ones_bf", P, bf16)
        ones_row = sb("ones_row", P, parts=1)
        heads8 = sb("heads8", 16)
        heads16 = sb("heads16", 8)
        row_head = sb("row_head", NC * HG)
        half_head = sb("half_head", 8 * 16)
        wq = sb("wq", D)
        wk = sb("wk", D)
        wv = sb("wv", D)
        wo = sb("wo", D)
        wqs = sb("wqs", D)
        wks = sb("wks", D)
        cols = sb("cols", 4)
        colk2 = sb("colk2", 24)
        brow = sb("brow", 5 * D, parts=1)
        gates_in = sb("gates_in", 8)
        tanh_g = sb("tanh_g", 8)
        stats = sb("stats", TILES * 6)
        mean_var = sb("mean_var", TILES * 2)
        rstd = sb("rstd", TILES)
        var_eps = sb("var_eps", TILES)
        minus_half = sb("minus_half", TILES)
        ones16 = sb("ones16", 16)
        xin = [sb(f"xin{s}", D) for s in range(2)]
        xnT = [sb(f"xnT{s}", D) for s in range(2)]
        qT = [sb(f"qT{s}", D) for s in range(2)]
        row_max = [sb(f"row_max{s}", HG) for s in range(4)]
        row_sum = [sb(f"row_sum{s}", HG) for s in range(4)]
        row_inv = [sb(f"row_inv{s}", HG) for s in range(4)]
        probs = [sb(f"probs{s}", UW) for s in range(2)]
        probsT = [sb(f"probsT{s}", TW) for s in range(2)]
        out_inv = [sb(f"out_inv{s}", 16) for s in range(2)]
        out_n = [sb(f"out_n{s}", D) for s in range(2)]
        outT = sb("outT", D)
        bucket_hot = xn_all[0:BUCKETS, 0:DELTAS]
        rel_by_delta = xn_all[0:16, DELTAS:2 * DELTAS]
        rope_cos, rope_sin = xn_all[:, 0:S], xn_all[:, S:2 * S]
        rel_T = sb("rel_T", 16, parts=BUCKETS)
        mask1_raw = sb("mask1_raw", BK, u8, parts=1)
        mask1_row = sb("mask1_row", BK, bf16, parts=1)
        mask2 = sb("mask2", TILES * SK, u8)
        mask2_tile = [sb(f"mask2_tile{s}", SK, u8) for s in range(2)]
        up_col = sb("up_col", 4)
        masked2 = sb("masked2", 1)
        wait_slot = sb("wait_slot", 1)
        router_w = sb("router_w", 16)
        hid = [sb(f"hid{s}", HID) for s in range(2)]
        hidT = [sb(f"hidT{s}", HID) for s in range(2)]
        earlier_f = hid[1][:, 0:D]
        ropeA, ropeB = hid[0][:, 0:D], hid[1][:, 0:D]
        y_out = [sb(f"y_out{s}", D) for s in range(2)]
        NR = TILES * 16
        region_r = sb("region_r", 10 * NR)
        r = {n: region_r[:, k * NR:(k + 1) * NR] for k, n in enumerate(
            ("logit", "a", "b", "hot1", "hot2", "tot1", "tot2", "scan1", "scan2", "prob"))}
        r_bf = [sb(f"r_bf{k}", NR, bf16) for k in range(2)]
        rc = {n: sb(f"rc_{n}", NR) for n in ("rev", "step", "carry")}
        slot_no = sb("slot_no", ROUTED_TILES[3] * 16)
        r_m = {n: sb(f"rm_{n}", 16) for n in ("m1", "m2", "m3", "cnt", "cnt1", "nt", "cum", "base", "w1", "w2", "sum", "pf", "kp", "sr")}
        pos = [sb(f"pos{k}", TILES, i32) for k in range(2)]
        expert_f = sb("expert_f", ROUTED_TILES[3])
        expert_of = sb("expert_of", ROUTED_TILES[0], i32)
        digits = sb("digits", ROUTED_TILES[3])
        tail = 9 * 1536 - 3 * HID
        up_fold = region_a[:, tail:tail + 2 * HID]
        down_fold = region_a[:, tail + 2 * HID:]
        zeros = y_out[0]
        q_bias = region_r[0:3, 0:B * 16 * SK // 2].bitcast(bf16)

        psum = ctx.enter_context(nc.psum_tensor("psum", [P, 8 * BANK], f32))

        def bank(n, a=0, b=BANK, parts=P):
            return psum[0:parts, n * BANK + a:n * BANK + b]

        sorted_in = nc.dram_tensor("sorted_in", (SLOTS, D), f32).ap()
        sorted_out = {l: nc.dram_tensor(f"sorted_out{l}", (n * P, D), f32).ap() for l, n in ROUTED_TILES.items()}
        vw_dram = nc.dram_tensor("vw_dram", (B, 2, UW, D), f32).ap()
        rel_dram = nc.dram_tensor("rel_dram", (16, DELTAS), f32)

        s = {n: sem(n) for n in (
            "phase_done", "loaded_first", "loaded_rest", "zeros_set", "slots_zeroed", "consts_set",
            "kv_psum", "kv_sbuf", "kv_chain", "rel_stored", "bias_loaded", "reloaded", "reloaded_b",
            "xn_ready", "xnT_psum", "xnT_sbuf", "qT_psum", "qT_sbuf", "rope_step",
            "scores_psum", "scores_prep", "row_max_done", "scores_shifted", "probs_ready",
            "probs_inverted", "probs_scaled", "probsT_psum", "probsT_sbuf",
            "out_psum", "out_inverted", "out_scaled", "outT_psum", "outT_sbuf", "proj_psum", "x_new", "stats_done",
            "mask2_copied", "dve_chain", "pool_chain", "act_chain", "logits_psum", "rank_psum",
            "hots_ready", "pos_ready", "scattered", "up_psum", "act_ready", "hid_ready", "hidT_psum", "hidT_sbuf",
            "y_psum", "y_taken", "gathered", "bfly_loaded", "bfly_done", "stored",
            "v_taken", "kv_evac", "mask_row_done", "l1_loaded", "rope_q", "tables_loaded", "experts_loaded", "rel_psum", "rel_evac", "kv_evac_v", "kv_evac_a", "vw_zeroed", "rstd_ready", "mean_var_done",
            "fold_psum", "q_bias_parts", "q_bias_loaded", "vw_stored", "vw_loaded", "gate_ready", "softmax_done", "router_chain", "rank_done", "combined")}
        xin_loaded = [sem(f"xin_loaded{k}") for k in range(2)]
        bfly_weights = [sem(f"bfly_weights{k}") for k in range(2)]
        y_stored = [sem(f"y_stored{k}") for k in range(2)]

        def count_from(done):
            return dict(done)

        def pairs(eng, n_pairs, body, first=1, last=1):
            for i in range(first):
                body(i)
            with eng.Fori(first, n_pairs - last) as i:
                body(i)
            for i in range(n_pairs - last, n_pairs):
                body(i)

        def exists(t, n):
            return 0 <= t < n if isinstance(t, int) else True

        ENGINES = 5

        def phase_end(eng, no):
            eng.drain().then_inc(s["phase_done"], 1)
            eng.wait_ge(s["phase_done"], ENGINES * no)

        ATT = {l: dict(layer=l, units=1 if l == 3 else 2) for l in range(4)}
        FFN = {0: dict(E=8, F=HID, act=ACT.Gelu), 1: dict(E=8, F=352, act=ACT.Silu),
               2: dict(E=0, F=HID, act=ACT.Gelu), 3: dict(E=16, F=128, act=ACT.Silu)}
        phases = [("load", 0, 0)]
        for l in range(4):
            phases.append(("stats", l, 0))
            phases.append(("keys", l, 0))
            phases.append(("attention", l, 0))
            phases.append(("stats", l, 1))
            if l == 2:
                phases.append(("router", l, 0))
                phases.append(("dense", l, 0))
            else:
                if l == 1:
                    phases.append(("fold", l, 0))
                phases.append(("router", l, 0))
                if l < 2:
                    phases.append(("shared", l, 0))
                phases.append(("routed", l, 0))
                if l < 2:
                    phases.append(("shared", l, 1))
                phases.append(("combine", l, 0))

        phases = phases[:UPTO]
        GROUPS = TILES // 4
        UNIT = {0: 1, 1: 1, 3: 4}

        def group_range(kind, part):
            return range(GROUPS) if kind == "dense" else range(part * GROUPS // 2, (part + 1) * GROUPS // 2)

        def chunks(F):
            return [(c, min(P, F - c)) for c in range(0, F, P)]

        TILE_SEMS = ("xn_ready", "xnT_psum", "xnT_sbuf")
        totals, at = {k: 0 for k in s}, []
        totals |= {"xin_pairs": 0, "y_pairs": 0}
        for kind, l, _ in phases:
            at.append(dict(totals))
            if kind == "attention":
                units = TILES * ATT[l]["units"]
                for k in TILE_SEMS:
                    totals[k] += TILES
                if l != 2:
                    for k in ("qT_psum", "qT_sbuf", "out_psum", "out_inverted", "out_scaled", "outT_psum", "outT_sbuf"):
                        totals[k] += TILES
                for k in ("proj_psum", "x_new"):
                    totals[k] += TILES
                for k in ("scores_psum", "row_max_done", "probs_ready", "probsT_psum", "probsT_sbuf"):
                    totals[k] += units
                if l != 2:
                    totals["scores_shifted"] += units
                if l in (1, 2):
                    totals["scores_prep"] += units
                if l == 1:
                    totals["row_max_done"] += units
                if l == 2:
                    for k in ("probs_inverted", "probs_scaled"):
                        totals[k] += units
                    totals["mask2_copied"] += TILES
                if l == 3:
                    totals["rope_step"] += 2 * TILES
            if kind == "router":
                totals["xn_ready"] += TILES
                totals["xnT_psum"] += GROUPS
                totals["xnT_sbuf"] += GROUPS
                if l != 2:
                    totals["logits_psum"] += TILES
            if kind in ("shared", "dense"):
                groups = len(group_range(kind, _))
                jobs = groups * len(chunks(FFN[l]["F"]))
                for k in ("up_psum", "hid_ready") + (("act_ready",) if kind == "shared" else ()):
                    totals[k] += jobs
                for k in ("y_psum", "x_new"):
                    totals[k] += groups
            if kind == "routed":
                n = ROUTED_TILES[l] // UNIT[l]
                for k in ("xnT_psum", "xnT_sbuf", "up_psum", "act_ready", "hid_ready", "hidT_psum", "hidT_sbuf", "y_psum", "y_taken"):
                    totals[k] += n
                totals["xin_pairs"] += n // 2
                totals["y_pairs"] += n // 2
        scatters_before, n_scat = {}, 0
        for l in (0, 1, 3):
            scatters_before[l] = n_scat
            n_scat += TILES * (2 if l == 3 else 1)

        up_w = {0: region_a[:, 0:9 * 1024], 1: region_b[:, 0:9 * 704], 3: region_b[:, 0:16 * 256]}
        down_w = {0: region_a[:, 9 * 1024:9 * 1536], 1: region_b[:, 9 * 704:9 * 1088], 3: region_b[:, 4096:4096 + 16 * 128]}
        xnT_all = keys[:, 0:TILES * P]
        hidT_all = region_c[:, 0:4096]
        wide = [region_c[:, k * 512:(k + 1) * 512] for k in range(6)]
        ffn_in = {0: xin, 1: xin, 3: wide[0:2]}
        ffn_inT = {0: xnT, 1: xnT, 3: wide[2:4]}
        ffn_out = {0: y_out, 1: y_out, 3: wide[4:6]}
        extra = {0: region_c[:, 0:2 * UW], 1: region_a[:, 6656:6656 + 2 * UW], 2: region_c[:, 0:2 * UW]}
        P_SLOTS = {l: [probs[0][:, :], probs[1][:, :], e[:, 0:UW], e[:, UW:2 * UW]] for l, e in extra.items()}
        P_SLOTS[3] = P_SLOTS[0][0:2]
        r_bf_parts = hidT[0][:, 0:3 * BK // 2].bitcast(bf16)
        values = {0: region_b, 1: region_a[:, 8192:12288], 3: region_a}
        vw_keys = region_a[0:SK, 0:B * 16 * D]
        vw = region_b[:, 0:B * 2 * NC * D]
        repeated = region_r[:, 0:B * UW]
        wkT2, wvT2 = region_a[:, 8192:9216], region_a[:, 9216:10240]
        wq2, woT2 = region_a[:, 10240:11264], region_a[:, 11264:12288]
        kT2, vT2 = region_c[:, 0:8 * BK], region_c[:, 8 * BK:16 * BK]
        bias1 = region_c

        def rows(name):
            return d[name].rearrange("(a n) -> a n", a=1)

        def expert_loads(l, shared_names, names):
            F, E = FFN[l]["F"], FFN[l]["E"]
            n = E + bool(shared_names)
            up = up_w[l].rearrange("p (e w f) -> p e w f", e=n, w=2)
            down = down_w[l].rearrange("p (e c o) -> p e c o", e=n, o=D)
            loads = [(up[:, 0:E, w, :], d[names[w]].rearrange("e p f -> p e f")) for w in range(2)]
            for c, (c0, cn) in enumerate(chunks(F)):
                loads.append((down[0:cn, 0:E, c, :], d[names[2]][:, c0:c0 + cn, :].rearrange("e p o -> p e o")))
            if shared_names:
                loads += [(up[:, E, w, :], d[shared_names[w]]) for w in range(2)]
                for c, (c0, cn) in enumerate(chunks(F)):
                    loads.append((down[0:cn, E, c, :], d[shared_names[2]][c0:c0 + cn, :]))
            return loads

        first_loads = [
            (x[:, :].rearrange("p (t e) -> p t e", e=D), d["x"].rearrange("(t p) e -> p t e", p=P)),
            (ctxT[:, :], d["ctxT"]), (ident[:, :], d["ident"]), (heads8[:, :], d["heads8"]),
            (heads16[:, :], d["heads16"]), (row_head[:, :], d["row_head"]), (wq[:, :], d["L0_xattn_Wq"]), (wk[:, :], d["L0_xattn_Wk"]),
            (wv[:, :], d["L0_xattn_Wv"]), (wo[:, :], d["L0_xattn_Wo"]),
            (cols[:, 0:1], d["L0_xattn_bq"].rearrange("(p a) -> p a", a=1)),
            (cols[:, 1:2], d["L0_xattn_bk"].rearrange("(p a) -> p a", a=1)),
            (brow[0:1, 0:D], rows("L0_xattn_bv")), (brow[0:1, D:2 * D], rows("L0_xattn_bo")),
            (gates_in[:, 0:4], rows("g_xattn").to_broadcast([P, 4])),
            (gates_in[:, 4:8], rows("g_ffn").to_broadcast([P, 4])),
            (earlier_f[:, :], d["earlier"])]
        rest_loads = expert_loads(0, ("L0_ffn_w1s", "L0_ffn_w2s", "L0_ffn_w3s"), ("L0_ffn_W1", "L0_ffn_W2", "L0_ffn_W3"))
        rest_loads += [
            (half_head[:, :], d["half_head"]),
            (rel_T[:, :], d["rel_T"]), (mask1_raw[:, :], d["mask1"]),
            (mask2[:, :].rearrange("p (t k) -> p t k", k=SK), d["mask2"].rearrange("(t p) k -> p t k", p=P)),
            (brow[0:1, 2 * D:3 * D], rows("L2_xattn_wOut_b")), (brow[0:1, 3 * D:4 * D], rows("L2_ffn_b_con")),
            (brow[0:1, 4 * D:5 * D], rows("L2_ffn_down_bias")),
            (colk2[:, 0:8], d["L2_xattn_wQ_b"].rearrange("(c p) -> p c", p=P)),
            (colk2[:, 8:16], d["L2_xattn_wK_b"].rearrange("(c p) -> p c", p=P)),
            (colk2[:, 16:24], d["L2_xattn_wV_b"].rearrange("(c p) -> p c", p=P))]
        next_loads = {
            0: [(ctxT[:, :], d["ctxT_backwards"]), (wq[:, :], d["L1_xattn_WqT"]), (wk[:, :], d["L1_xattn_WkT"]), (wv[:, :], d["L1_xattn_WvT"]),
                (wo[:, :], d["L1_xattn_WoT"]), (router_w[:, 0:8], d["L0_ffn_Wg"])]
               + [(rc[n][:, 0:TILES * 8], d[n + "8"]) for n in ("rev", "step", "carry")]
               + [(slot_no[:, 0:ROUTED_TILES[0] * 8], d["slot8"])],
            1: [(ctxT[:, :], d["ctxT"]), (wkT2, d["L2_xattn_WkT"]), (wvT2, d["L2_xattn_WvT"]),
                (wq2.rearrange("p (c e) -> p c e", e=D), d["L2_xattn_wQ_w"].rearrange("(c p) e -> p c e", p=P)),
                (woT2.rearrange("p (c e) -> p c e", e=D), d["L2_xattn_WoT"].rearrange("(c p) e -> p c e", p=P)),
                (router_w[:, 0:8], d["L1_ffn_router_DE"])],
            2: [(wq[:, :], d["L3_xattn_WqT"]), (wk[:, :], d["L3_xattn_WkT"]), (wv[:, :], d["L3_xattn_WvT"]),
                (wo[:, :], d["L3_xattn_WoT"]), (wqs[:, :], d["L3_xattn_WqT_swapped"]),
                (wks[:, :], d["L3_xattn_WkT_swapped"]), (router_w[:, :], d["L3_ffn_router_w"]),
                ]
               + [(rc[n][:, :], d[n + "16"]) for n in ("rev", "step", "carry")]
               + [(slot_no[:, :], d["slot16"]), (digits[:, :], d["digits"])],
            3: []}
        next_experts = {
            0: expert_loads(1, ("L1_ffn_ws1_DF", "L1_ffn_ws3_DF", "L1_ffn_ws2_FD"),
                            ("L1_ffn_w1_eDF", "L1_ffn_w3_eDF", "L1_ffn_w2_eFD")),
            1: [], 2: expert_loads(3, None, ("L3_ffn_gate_w", "L3_ffn_up_w", "L3_ffn_down_w")), 3: []}

        VJ = B * NC // 4
        KV = {0: dict(kv_psum=0, kv_evac_v=0)}
        KV[1] = dict(kv_psum=1 + VJ, kv_evac_v=1)
        KV[2] = dict(kv_psum=2 * (1 + VJ), kv_evac_v=2)
        KV[3] = dict(kv_psum=2 * (1 + VJ) + 16 + 1 + 16 + B * 4, kv_evac_v=2 + 16 + 1 + B * 4)
        HOTS = {0: 0, 1: 1, 3: 2}
        GATHERS = {0: TILES, 1: 2 * TILES, 3: 4 * TILES}
        STATS = {no: sum(p[0] == "stats" for p in phases[:no]) for no in range(len(phases))}
        V_TAKEN = {0: 0, 1: VJ, 3: 2 * VJ}
        down_T = region_a[:, 0:HID]

        block = ctx.enter_context(nc.Block())

        @block.sync
        def _(sp):
            for dst, src in first_loads:
                sp.dma_start(dst, src).then_inc(s["loaded_first"], 16)
            sp.wait_ge(s["zeros_set"], 1)
            sp.dma_start(sorted_in.rearrange("(t p) e -> p t e", p=P),
                         zeros[:, :].rearrange("p (a e) -> p a e", a=1).to_broadcast([P, ROUTED_TILES[3], D]))\
                .then_inc(s["slots_zeroed"], 16)
            for dst, src in rest_loads:
                sp.dma_start(dst, src).then_inc(s["loaded_rest"], 16)
            sp.wait_ge(s["loaded_first"], 16 * len(first_loads))

            reloads = experts = 0
            for no, (kind, l, sub) in enumerate(phases):
                z = at[no]
                if kind == "stats" and sub == 1:
                    for dst, src in next_loads[l]:
                        sp.dma_start(dst, src).then_inc(s["reloaded"], 16)
                    for dst, src in next_experts[l]:
                        sp.dma_start(dst, src).then_inc(s["experts_loaded"], 16)
                    reloads += len(next_loads[l])
                    experts += len(next_experts[l])
                    if l == 0:
                        sp.wait_ge(s["loaded_rest"], 16 * len(rest_loads))
                    sp.wait_ge(s["reloaded"], 16 * reloads)
                if kind == "router":
                    sp.wait_ge(s["experts_loaded"], 16 * experts) if l else None
                if kind == "keys" and l == 1:
                    sp.dma_start(bucket_hot, d["bucket_hot"]).then_inc(s["tables_loaded"], 16)
                if kind == "dense":
                    for dst, src in ((rope_cos, d["rope_cos"]), (rope_sin, d["rope_sin"])):
                        sp.dma_start(dst, src).then_inc(s["tables_loaded"], 16)
                    sp.wait_ge(s["tables_loaded"], 48)
                if kind == "keys" and l == 1:
                    sp.wait_ge(s["rel_evac"], 2)
                    sp.dma_start(rel_dram.ap(), rel_by_delta).then_inc(s["rel_stored"], 16)
                    sp.wait_ge(s["rel_stored"], 16)
                    for q in range(QT):
                        src = bass.AP(rel_dram, q * P, [[1, P], [DELTAS, 16], [1, SK]])
                        sp.dma_start(bias1[:, q * 16 * SK:(q + 1) * 16 * SK].rearrange("p (h k) -> p h k", k=SK), src)\
                            .then_inc(s["bias_loaded"], 16)
                    sp.wait_ge(s["bias_loaded"], 16 * QT)
                if kind == "keys" and l == 2:
                    sp.wait_ge(s["kv_evac_v"], KV[2]["kv_evac_v"] + 17 + 4 * B)
                    for b in range(B):
                        sp.dma_start(vw_dram[b].rearrange("u (h k) e -> k u h e", k=SK),
                                     vw_keys.rearrange("p (b u h e) -> p b u h e", b=B, u=2, e=D)[:, b, :, :, :]).then_inc(s["vw_stored"], 16)
                    sp.wait_ge(s["q_bias_parts"], 1)
                    for part in range(3):
                        for b in range(B):
                            at_b = part * BK + b * SK
                            sp.dma_start(q_bias[part:part + 1, b * 16 * SK:(b + 1) * 16 * SK].rearrange("p (h k) -> p h k", k=SK),
                                         r_bf_parts[0:16, at_b:at_b + SK]).then_inc(s["q_bias_loaded"], 16)
                    sp.wait_ge(s["vw_stored"], 16 * B)
                    sp.wait_ge(s["vw_zeroed"], 1)
                    vw5 = vw.rearrange("p (b u c e) -> p b u c e", b=B, u=2, e=D)
                    for b in range(B):
                        for u in range(2):
                            sp.dma_start(vw5[:, b, u, 0:NC - 1, :], vw_dram[b, u, 0:(NC - 1) * P, :].rearrange("(c p) e -> p c e", p=P))\
                                .then_inc(s["vw_loaded"], 16)
                        sp.dma_start(vw5[P - (UW - (NC - 1) * P):P, b, :, NC - 1, :], vw_dram[b, :, (NC - 1) * P:UW, :].rearrange("u p e -> p u e"))\
                            .then_inc(s["vw_loaded"], 16)
                    sp.wait_ge(s["vw_loaded"], 16 * 3 * B)
                    sp.wait_ge(s["q_bias_loaded"], 16 * 3 * B)
                if kind == "routed":
                    U = UNIT[l]
                    n = ROUTED_TILES[l] // U
                    if l == 0:
                        sp.wait_ge(s["slots_zeroed"], 16)
                    sp.wait_ge(s["scattered"], 16 * (scatters_before[l] + TILES * (2 if l == 3 else 1)))

                    def sorted_rows(dram, t):
                        return dram[ds(t * (U * P), U * P), :].rearrange("(a p) e -> p a e", p=P)

                    def load(i, k):
                        sp.dma_start(ffn_in[l][k][:, :].rearrange("p (a e) -> p a e", e=D), sorted_rows(sorted_in, 2 * i + k))\
                            .then_inc(xin_loaded[k], 16)

                    def store(t, k):
                        sp.wait_ge(s["y_taken"], z["y_taken"] + t + 1)
                        sp.dma_start(sorted_rows(sorted_out[l], t), ffn_out[l][k][:, :].rearrange("p (a e) -> p a e", e=D))\
                            .then_inc(y_stored[k], 16)

                    for k in range(2):
                        load(0, k)

                    def body(i):
                        for k in range(2):
                            t = 2 * i + k
                            if exists(t + 2, n):
                                sp.wait_ge(s["xnT_psum"], z["xnT_psum"] + t + 1)
                                load(i + 1, k)
                            if exists(t - 2, n):
                                store(t - 2, k)
                    pairs(sp, n // 2, body)
                    for k in range(2):
                        store(n - 2 + k, k)
                    for k in range(2):
                        sp.wait_ge(y_stored[k], 16 * (z["y_pairs"] + n // 2))
                phase_end(sp, no + 1)
            sp.dma_start(out.rearrange("(t p) e -> p t e", p=P), x[:, :].rearrange("p (t e) -> p t e", e=D)).then_inc(s["stored"], 16)
            sp.wait_ge(s["stored"], 16)

        def scores(k):
            two = psum[:, 2 * k * BANK:(2 * k + 2) * BANK].rearrange("p (a c) -> p a c", a=2)
            return two[:, :, 0:UW // 2].rearrange("p a (h k) -> p a h k", k=SK)

        def by_head(ap):
            return ap.rearrange("p (a h k) -> p a h k", a=2, k=SK)

        def over_keys(ap):
            return ap.rearrange("p (a h o) -> p a h o", a=2, o=1).to_broadcast([P, 2, HG // 2, SK])

        HD = {0: 8, 1: 8, 3: 16}
        TRANSPOSED = 4 * BANK
        OUT, MIX = 6, 7

        def tile_step_order(l):
            return 2 if l == 3 else 1

        @block.tensor
        def _(pe):
            mm, tr = nc.tensor.matmul, nc.tensor.transpose

            def keys_phase(l, z):
                if l == 2:
                    return keys_phase2(z)
                mm(bank(0, 0, BK), wk[:, :], ctxT[:, :], start=True, stop=True).then_inc(s["kv_psum"], 1)
                if l == 3:
                    mm(bank(1, 0, BK), wks[:, :], ctxT[:, :], start=True, stop=True).then_inc(s["kv_psum"], 1)
                pe.wait_ge(s["kv_evac_v"], z["kv_evac_v"] + 1)
                for j in range(VJ):
                    for i in range(4):
                        b, c = (4 * j + i) // NC, (4 * j + i) % NC
                        o = bank(2 + j % 4, i * D, (i + 1) * D)
                        if i == 0 and j >= 4:
                            pe.wait_ge(s["v_taken"], V_TAKEN[l] + j - 3)
                        last = mm(o, repeated[:, b * UW + CHUNKS[c]:b * UW + CHUNKS[c] + P], wv[:, :], start=True, stop=l != 0)
                        if l == 0:
                            last = mm(o, ones_row[0:1, :], brow[0:1, 0:D], start=False, stop=True)
                    last.then_inc(s["kv_psum"], 1)
                if l == 1:
                    pe.wait_ge(s["tables_loaded"], 16)
                    mm(bank(6, 0, BANK, parts=16), rel_T[:, :], bucket_hot[:, 0:BANK], start=True, stop=True).then_inc(s["rel_psum"], 1)
                    mm(bank(7, 0, DELTAS - BANK, parts=16), rel_T[:, :], bucket_hot[:, BANK:DELTAS], start=True, stop=True)\
                        .then_inc(s["rel_psum"], 1)

            def keys_phase2(z):
                for j in range(16):
                    if j >= 8:
                        pe.wait_ge(s["kv_evac_v"], z["kv_evac_v"] + j - 8 + 1)
                    w, c = (wkT2, j) if j < 8 else (wvT2, j - 8)
                    mm(bank(j % 8, 0, BK), w[:, c * P:(c + 1) * P], ctxT[:, :], start=True, stop=True).then_inc(s["kv_psum"], 1)
                pe.wait_ge(s["kv_evac_v"], z["kv_evac_v"] + 17)
                for c in range(8):
                    last = mm(bank(0, 0, BK, parts=16), hid[1][:, c * 16:(c + 1) * 16], kT2[:, c * BK:(c + 1) * BK], start=c == 0, stop=c == 7)
                last.then_inc(s["kv_psum"], 1)
                for h in range(16):
                    rows_h = slice(64 * (h % 2), 64 * (h % 2) + 64)
                    k_h = kT2[rows_h, (h // 2) * BK:(h // 2 + 1) * BK]
                    if h >= 6:
                        pe.wait_ge(s["kv_evac_a"], h - 4)
                    mm(bank(2 + h % 6, 0, BK), wq2[rows_h, (h // 2) * P:(h // 2 + 1) * P], k_h, start=True, stop=True)\
                        .then_inc(s["kv_psum"], 1)
                pe.wait_ge(s["kv_evac_a"], 17)
                for j in range(B * 4):
                    if j >= 8:
                        pe.wait_ge(s["kv_evac_v"], z["kv_evac_v"] + 17 + j - 8 + 1)
                    b, g = j // 4, j % 4
                    for i in range(4):
                        h = 8 * (g // 2) + 2 * i + g % 2
                        rows_h = slice(64 * (h % 2), 64 * (h % 2) + 64)
                        last = mm(bank(j % 8, i * D, (i + 1) * D, parts=SK),
                                  vT2[rows_h, (h // 2) * BK + b * SK:(h // 2) * BK + (b + 1) * SK],
                                  woT2[rows_h, (h // 2) * P:(h // 2 + 1) * P], start=True, stop=True)
                    last.then_inc(s["kv_psum"], 1)

            def attention_phase(l, z):
                units = ATT[l]["units"]
                ahead = tile_step_order(l)

                def normalised(t, k):
                    pe.wait_ge(s["xn_ready"], z["xn_ready"] + t + 1)
                    tr(bank(MIX, 0, D), xin[k][:, :], ident[:, :]).then_inc(s["xnT_psum"], 1)

                def queries(t, k):
                    if l == 2:
                        return
                    pe.wait_ge(s["xnT_sbuf"], z["xnT_sbuf"] + t + 1)
                    last = mm(bank(MIX, D, 2 * D), wq[:, :], xnT[k][:, :], start=True, stop=True)
                    if l == 3:
                        last = mm(bank(MIX, 2 * D, 3 * D), wqs[:, :], xnT[k][:, :], start=True, stop=True)
                    last.then_inc(s["qT_psum"], 1)

                def score(t, h, k, kt, first_two):
                    u = t * units + h
                    if l == 2:
                        pe.wait_ge(s["xnT_sbuf"], z["xnT_sbuf"] + t + 1)
                    else:
                        pe.wait_ge(s["qT_sbuf"], z["qT_sbuf"] + t + 1)
                    if not first_two:
                        read = "probs_ready" if l == 2 else "scores_shifted"
                        pe.wait_ge(s[read], z[read] + u - 1)
                    q = (xnT if l == 2 else qT)[kt]
                    b = t // QT
                    for half in range(2):
                        o = bank(2 * k + half, 0, UW // 2)
                        at_k = b * (units * UW) + h * UW + half * (UW // 2)
                        last = mm(o, q[:, :], keys[:, ds(at_k, UW // 2)], start=True, stop=l in (0, 3))
                        if l == 1:
                            last = mm(o, ones_bf[0:1, :], mask1_row[0:1, ds(b * SK, SK)].rearrange("p (a k) -> p a k", a=1)
                                      .to_broadcast([1, HG // 2, SK]), start=False, stop=True)
                        if l == 2:
                            last = mm(o, ones_bf[0:3, :], q_bias[:, ds(at_k, UW // 2)], start=False, stop=True)
                    last.then_inc(s["scores_psum"], 1)

                def transpose_probs(t, h, k, very_first):
                    u = t * units + h
                    ready = "probs_scaled" if l == 2 else "probs_ready"
                    pe.wait_ge(s[ready], z[ready] + u + 1)
                    if not very_first:
                        pe.wait_ge(s["probsT_sbuf"], z["probsT_sbuf"] + u)
                    for i, c in enumerate(CHUNKS):
                        last = tr(psum[:, TRANSPOSED + i * P:TRANSPOSED + (i + 1) * P], P_SLOTS[l][k][:, c:c + P], ident[:, :])
                    last.then_inc(s["probsT_psum"], 1)

                def attend(t, h, k, first_tile):
                    u = t * units + h
                    pe.wait_ge(s["probsT_sbuf"], z["probsT_sbuf"] + u + 1)
                    b = t // QT
                    if h == 0 and not first_tile:
                        if l == 2:
                            pe.wait_ge(s["x_new"], z["x_new"] + t)
                        else:
                            pe.wait_ge(s["out_scaled"], z["out_scaled"] + t)
                    if l == 2 and h == 0:
                        mm(bank(OUT, 0, D), ones_row[0:1, :], brow[0:1, 2 * D:3 * D], start=True, stop=False)
                    for i in range(NC):
                        pT = probsT[k][:, i * P:(i + 1) * P]
                        if l == 2:
                            last = mm(bank(OUT, 0, D), pT, vw[:, ds(b * (2 * NC * D) + (h * NC + i) * D, D)],
                                      start=False, stop=h == 1 and i == NC - 1)
                        else:
                            w = HG * (HD[l] + 1)
                            last = mm(bank(OUT, h * w, (h + 1) * w), pT, values[l][:, ds(b * (units * NC * w) + (h * NC + i) * w, w)],
                                      start=i == 0, stop=i == NC - 1)
                    if h == units - 1:
                        last.then_inc(s["proj_psum" if l == 2 else "out_psum"], 1)

                def out_transpose(t, k):
                    pe.wait_ge(s["out_scaled"], z["out_scaled"] + t + 1)
                    tr(bank(MIX, 3 * D, 4 * D) if l == 3 else bank(MIX, 2 * D, 3 * D), out_n[k][:, :], ident[:, :]).then_inc(s["outT_psum"], 1)

                def project(t):
                    pe.wait_ge(s["outT_sbuf"], z["outT_sbuf"] + t + 1)
                    o = bank(OUT, 256, 256 + D) if l == 3 else bank(MIX, 0, D)
                    if l == 3:
                        pe.wait_ge(s["out_scaled"], z["out_scaled"] + (t + 2 if exists(t + 1, TILES) else t + 1))
                    if l == 0:
                        mm(o, ones_row[0:1, :], brow[0:1, D:2 * D], start=True, stop=False)
                    mm(o, outT[:, :], wo[:, :], start=l != 0, stop=True).then_inc(s["proj_psum"], 1)

                def new_x_read(t):
                    if l != 2 and exists(t, TILES):
                        pe.wait_ge(s["x_new"], z["x_new"] + t + 1)

                def queries_read(t):
                    if l != 2:
                        pe.wait_ge(s["qT_sbuf"], z["qT_sbuf"] + t + 1)

                for t in range(2):
                    normalised(t, t)
                    queries(t, t)
                    if l == 2:
                        pe.wait_ge(s["xnT_sbuf"], z["xnT_sbuf"] + t + 1)
                    queries_read(t)
                if l == 3:
                    normalised(2, 0)
                    score(0, 0, 0, 0, True)
                    score(1, 0, 1, 1, True)
                else:
                    score(0, 0, 0, 0, True)
                    score(0, 1, 1, 0, True)
                    score(1, 0, 0, 1, False)

                def body(i):
                    for k in range(2):
                        t = 2 * i + k
                        start = isinstance(t, int) and t == 0
                        if l == 3:
                            transpose_probs(t, 0, k, start)
                            if exists(t + 2, TILES):
                                queries(t + 2, k)
                            if exists(t - 1, TILES):
                                if exists(t - 3, TILES):
                                    new_x_read(t - 3)
                                attend(t - 1, 0, 1 - k, isinstance(t, int) and t == 1)
                            if exists(t - 2, TILES):
                                if exists(t + 2, TILES):
                                    queries_read(t + 2)
                                out_transpose(t - 2, k)
                            if exists(t + 2, TILES):
                                score(t + 2, 0, k, k, False)
                            if exists(t + 3, TILES):
                                if exists(t - 2, TILES):
                                    pe.wait_ge(s["outT_sbuf"], z["outT_sbuf"] + t - 1)
                                else:
                                    queries_read(t + 2)
                                normalised(t + 3, 1 - k)
                            if exists(t - 2, TILES):
                                project(t - 2)
                        else:
                            p = 2 * k
                            transpose_probs(t, 0, p, start)
                            if exists(t + 2, TILES):
                                if exists(t - 2, TILES):
                                    new_x_read(t - 2)
                                normalised(t + 2, k)
                            if exists(t - 1, TILES):
                                attend(t - 1, 1, 1, False)
                            if exists(t + 2, TILES):
                                queries(t + 2, k)
                            if exists(t + 1, TILES):
                                score(t + 1, 1, 1, 1 - k, False)
                            transpose_probs(t, 1, p + 1, False)
                            if l != 2 and exists(t - 1, TILES):
                                if exists(t + 2, TILES):
                                    queries_read(t + 2)
                                else:
                                    new_x_read(t - 2)
                                out_transpose(t - 1, 1 - k)
                            attend(t, 0, 0, start)
                            if l != 2 and exists(t - 1, TILES):
                                project(t - 1)
                            if exists(t + 2, TILES):
                                score(t + 2, 0, 0, k, False)
                pairs(pe, TILES // 2, body, 2 if l == 3 else 1, 2)
                last = TILES - 1
                if l == 3:
                    new_x_read(last - 2)
                    attend(last, 0, 1, False)
                    for t in (last - 1, last):
                        out_transpose(t, t % 2)
                        if t == last:
                            new_x_read(last - 1)
                        project(t)
                else:
                    attend(last, 1, 1, False)
                    if l != 2:
                        new_x_read(last - 1)
                        out_transpose(last, 1)
                        project(last)

            def router_phase(l, z):
                E = FFN[l]["E"]
                for g in range(GROUPS):
                    if g >= 2:
                        pe.wait_ge(s["xnT_sbuf"], z["xnT_sbuf"] + g - 1)
                    for i in range(4):
                        t = 4 * g + i
                        pe.wait_ge(s["xn_ready"], z["xn_ready"] + t + 1)
                        last = tr(bank(6 + g % 2, i * P, (i + 1) * P), xn_all[:, t * D:(t + 1) * D], ident[:, :])
                    last.then_inc(s["xnT_psum"], 1)
                if l == 2:
                    return
                for t in range(TILES):
                    pe.wait_ge(s["xnT_sbuf"], z["xnT_sbuf"] + t // 4 + 1)
                    mm(bank(0, t * E, (t + 1) * E), xnT_all[:, t * P:(t + 1) * P], router_w[:, 0:E], start=True, stop=True)\
                        .then_inc(s["logits_psum"], 1)
                for c in range(2 if l == 3 else 1):
                    pe.wait_ge(s["hots_ready"], HOTS[l] + c + 1)
                    mm(bank(1 + 2 * c, 0, TILES * E), earlier[:, :], r_bf[c][:, 0:TILES * E], start=True, stop=True)
                    mm(bank(2 + 2 * c, 0, TILES * E), ones_bf[:, :], r_bf[c][:, 0:TILES * E], start=True, stop=True)\
                        .then_inc(s["rank_psum"], 1)

            def shared_phase(kind, part, l, z):
                F, E = FFN[l]["F"], FFN[l]["E"]
                cs = chunks(F)
                C = len(cs)
                groups = group_range(kind, part)

                def up(g, c):
                    j = (g - groups[0]) * C + c
                    c0, cn = cs[c]
                    if j >= 2:
                        pe.wait_ge(s["hid_ready"], z["hid_ready"] + j - 1)
                    tokens = xnT_all[:, g * 512:(g + 1) * 512]
                    if kind == "dense":
                        last = mm(bank(j % 2), up_fold[:, c0:c0 + cn], tokens, start=True, stop=True)
                    else:
                        at_w = E * 2 * F + c0
                        mm(bank(j % 2, parts=cn), up_w[l][:, at_w:at_w + cn], tokens, start=True, stop=True)
                        last = mm(bank(2 + j % 2, parts=cn), up_w[l][:, at_w + F:at_w + F + cn], tokens, start=True, stop=True)
                    last.then_inc(s["up_psum"], 1)

                def down(g):
                    n = g - groups[0]
                    pe.wait_ge(s["hid_ready"], z["hid_ready"] + (n + 1) * C)
                    if n >= 2:
                        pe.wait_ge(s["x_new"], z["x_new"] + n - 1)
                    for i in range(4):
                        o = bank(6 + n % 2, i * D, (i + 1) * D)
                        if kind == "dense":
                            mm(o, ones_row[0:1, :], brow[0:1, 3 * D:4 * D], start=True, stop=False)
                        for c, (c0, cn) in enumerate(cs):
                            w = down_fold[:, c * D:(c + 1) * D] if kind == "dense" else \
                                down_w[l][0:cn, (E * C + c) * D:(E * C + c + 1) * D]
                            h = ((n % 2) * C + c) * 512 + i * P
                            last = mm(o, hidT_all[0:cn, h:h + P], w, start=c == 0 and kind != "dense", stop=c == C - 1)
                    last.then_inc(s["y_psum"], 1)

                for g in groups:
                    for c in range(C):
                        up(g, c)
                        if c == 1 and g > groups[0]:
                            down(g - 1)
                down(groups[-1])

            def routed_phase(l, z):
                F, E, U = FFN[l]["F"], FFN[l]["E"], UNIT[l]
                n = ROUTED_TILES[l] // U
                C = len(chunks(F))
                x_in, x_T = ffn_in[l], ffn_inT[l]

                def experts(t):
                    word = pe.value_load(expert_of[0:1, ds(t, 1)], min_val=0, max_val=E ** U - 1)
                    return [(word // E ** i) % E if U > 1 else word for i in range(U)]

                def normalised(t, k, first):
                    pe.wait_ge(xin_loaded[k], 16 * (z["xin_pairs"] + (t - k) // 2 + 1) if isinstance(t, int)
                               else 16 * (z["xin_pairs"] + 1) + (t - k) * 8)
                    if not first:
                        pe.wait_ge(s["xnT_sbuf"], z["xnT_sbuf"] + t)
                    for i in range(U):
                        last = tr(bank(7, i * D, (i + 1) * D), x_in[k][:, i * D:(i + 1) * D], ident[:, :])
                    last.then_inc(s["xnT_psum"], 1)

                def up(t, k, first_two):
                    es = experts(t)
                    pe.wait_ge(s["xnT_sbuf"], z["xnT_sbuf"] + t + 1)
                    if not first_two:
                        pe.wait_ge(s["hid_ready"], z["hid_ready"] + t - 1)
                    for i, e in enumerate(es):
                        for w in range(2):
                            last = mm(bank(2 * w + k, i * F, (i + 1) * F), x_T[k][:, i * D:(i + 1) * D],
                                      up_w[l][:, ds(e * (2 * F) + w * F, F)], start=True, stop=True)
                    last.then_inc(s["up_psum"], 1)

                def hidden_transpose(t, k):
                    pe.wait_ge(s["hid_ready"], z["hid_ready"] + t + 1)
                    for c, (c0, cn) in enumerate(chunks(U * F)):
                        last = tr(bank(4 + k, c * P, (c + 1) * P, parts=cn), hid[k][:, c0:c0 + cn], ident[:, :])
                    last.then_inc(s["hidT_psum"], 1)

                def down(t, k, first):
                    es = experts(t)
                    pe.wait_ge(s["hidT_sbuf"], z["hidT_sbuf"] + t + 1)
                    if not first:
                        pe.wait_ge(s["y_taken"], z["y_taken"] + t)
                    for i, e in enumerate(es):
                        for c, (c0, cn) in enumerate(chunks(F)):
                            last = mm(bank(6, i * D, (i + 1) * D), hidT[k][0:cn, (i * C + c) * P:(i * C + c + 1) * P],
                                      down_w[l][0:cn, ds(e * (C * D) + c * D, D)], start=c == 0, stop=c == C - 1)
                    last.then_inc(s["y_psum"], 1)

                normalised(0, 0, True)
                normalised(1, 1, False)
                up(0, 0, True)

                def body(i):
                    for k in range(2):
                        t = 2 * i + k
                        if exists(t + 1, n):
                            up(t + 1, 1 - k, isinstance(t, int) and t == 0)
                        if exists(t + 2, n):
                            normalised(t + 2, k, False)
                        hidden_transpose(t, k)
                        if exists(t - 1, n):
                            down(t - 1, 1 - k, isinstance(t, int) and t == 1)
                pairs(pe, n // 2, body)
                down(n - 1, 1, False)

            for no, (kind, l, sub) in enumerate(phases):
                z = at[no]
                if kind == "keys":
                    keys_phase(l, KV[l])
                elif kind == "attention":
                    attention_phase(l, z)
                elif kind == "router":
                    router_phase(l, z)
                elif kind in ("shared", "dense"):
                    shared_phase(kind, sub, l, z)
                elif kind == "routed":
                    routed_phase(l, z)
                elif kind == "fold":
                    for c in range(4):
                        tr(bank(0, c * P, (c + 1) * P), down_T[:, c * P:(c + 1) * P], ident[:, :])
                        last = tr(bank(1, c * P, (c + 1) * P), up_fold[:, HID + c * P:HID + (c + 1) * P], ident[:, :])
                    last.then_inc(s["fold_psum"], 1)
                phase_end(pe, no + 1)

        @block.scalar
        def _(act):
            run = nc.scalar.activation

            def keys_phase(l, z):
                if l == 2:
                    act.wait_ge(s["kv_psum"], z["kv_psum"] + 17)
                    run(hid[0][0:16, 0:BK], bank(0, 0, BK, parts=16), ACT.Copy, scale=0.125).then_inc(s["kv_evac_a"], 1)
                    for h in range(16):
                        act.wait_ge(s["kv_psum"], z["kv_psum"] + 17 + h + 1)
                        run(keys[:, :].rearrange("p (b h k) -> p b h k", b=B, k=SK)[:, :, h, :],
                            bank(2 + h % 6, 0, BK).rearrange("p (b k) -> p b k", k=SK), ACT.Copy, scale=0.125).then_inc(s["kv_evac_a"], 1)
                    return
                if l == 1:
                    act.wait_ge(s["rel_psum"], 2)
                    run(rel_by_delta[:, 0:BANK], bank(6, 0, BANK, parts=16), ACT.Copy).then_inc(s["rel_evac"], 1)
                    run(rel_by_delta[:, BANK:DELTAS], bank(7, 0, DELTAS - BANK, parts=16), ACT.Copy).then_inc(s["rel_evac"], 1)

            def attention_phase(l, z):
                units = ATT[l]["units"]

                def normalised(t, k):
                    act.wait_ge(s["xnT_psum"], z["xnT_psum"] + t + 1)
                    run(xnT[k][:, :], bank(MIX, 0, D), ACT.Copy).then_inc(s["xnT_sbuf"], 1)

                def queries(t, k):
                    if l in (2, 3):
                        return
                    act.wait_ge(s["qT_psum"], z["qT_psum"] + t + 1)
                    if l == 0:
                        run(qT[k][:, :], bank(MIX, D, 2 * D), ACT.Identity, bias=cols[:, 0:1]).then_inc(s["qT_sbuf"], 1)
                    else:
                        run(qT[k][:, :], bank(MIX, D, 2 * D), ACT.Copy).then_inc(s["qT_sbuf"], 1)

                def exps(t, h, k):
                    if l != 2:
                        act.wait_ge(s["scores_shifted"], z["scores_shifted"] + t * units + h + 1)
                        run(P_SLOTS[l][k], P_SLOTS[l][k], ACT.Exp).then_inc(s["probs_ready"], 1)
                        return
                    act.wait_ge(s["row_max_done"], z["row_max_done"] + t * units + h + 1)
                    if not (isinstance(t, int) and t < 2):
                        act.wait_ge(s["probsT_psum"], z["probsT_psum"] + t * units + h - 3)
                    for i in range(HG):
                        last = run(P_SLOTS[l][k][:, i * SK:(i + 1) * SK], bank(2 * h + i // 4, (i % 4) * SK, (i % 4 + 1) * SK), ACT.Exp,
                                   bias=row_max[k][:, i:i + 1], accum_out=row_sum[k][:, i:i + 1])
                    last.then_inc(s["probs_ready"], 1)

                def probs_copy(t, h, k):
                    act.wait_ge(s["probsT_psum"], z["probsT_psum"] + t * units + h + 1)
                    run(probsT[k][:, :], psum[:, TRANSPOSED:TRANSPOSED + TW], ACT.Copy).then_inc(s["probsT_sbuf"], 1)

                def out_copy(t):
                    act.wait_ge(s["outT_psum"], z["outT_psum"] + t + 1)
                    run(outT[:, :], bank(MIX, 3 * D, 4 * D) if l == 3 else bank(MIX, 2 * D, 3 * D), ACT.Copy).then_inc(s["outT_sbuf"], 1)

                for t in range(2):
                    normalised(t, t)
                    queries(t, t)
                if l == 3:
                    normalised(2, 0)
                exps(0, 0, 0)
                if l != 3:
                    exps(0, 1, 1)

                def body(i):
                    for k in range(2):
                        t = 2 * i + k
                        if l == 3:
                            probs_copy(t, 0, k)
                            if exists(t + 1, TILES):
                                exps(t + 1, 0, 1 - k)
                            if exists(t - 2, TILES):
                                out_copy(t - 2)
                            if exists(t + 3, TILES):
                                normalised(t + 3, 1 - k)
                        else:
                            probs_copy(t, 0, 0)
                            if exists(t + 2, TILES):
                                normalised(t + 2, k)
                            if exists(t + 1, TILES):
                                exps(t + 1, 0, 2 - 2 * k)
                            if exists(t + 2, TILES):
                                queries(t + 2, k)
                            probs_copy(t, 1, 1)
                            if l != 2 and exists(t - 1, TILES):
                                out_copy(t - 1)
                            if exists(t + 1, TILES):
                                exps(t + 1, 1, 3 - 2 * k)
                pairs(act, TILES // 2, body, 2 if l == 3 else 1, 2)
                if l == 3:
                    out_copy(TILES - 2)
                if l != 2:
                    out_copy(TILES - 1)

            def router_phase(l, z):
                for g in range(GROUPS):
                    act.wait_ge(s["xnT_psum"], z["xnT_psum"] + g + 1)
                    run(xnT_all[:, g * 512:(g + 1) * 512], bank(6 + g % 2), ACT.Copy).then_inc(s["xnT_sbuf"], 1)
                if l == 1:
                    act.wait_ge(s["hots_ready"], HOTS[l] + 1)
                    run(r_m["kp"][:, :], r_m["m1"][:, :], ACT.Sigmoid).then_inc(s["gate_ready"], 1)
                if l == 3:
                    act.wait_ge(s["softmax_done"], 1)
                    run(r["prob"], r["prob"], ACT.Exp).then_inc(s["softmax_done"], 1)

            def shared_phase(kind, part, l, z):
                cs = chunks(FFN[l]["F"])
                C = len(cs)
                groups = group_range(kind, part)
                for g in groups:
                    for c, (c0, cn) in enumerate(cs):
                        n = g - groups[0]
                        j = n * C + c
                        h = ((n % 2) * C + c) * 512
                        act.wait_ge(s["up_psum"], z["up_psum"] + j + 1)
                        bias = {"bias": up_col[:, c:c + 1]} if kind == "dense" else {}
                        run(hidT_all[0:cn, h:h + 512], bank(j % 2, parts=cn), FFN[l]["act"], **bias)\
                            .then_inc(s["hid_ready" if kind == "dense" else "act_ready"], 1)

            def routed_phase(l, z):
                F, U = FFN[l]["F"], UNIT[l]
                n = ROUTED_TILES[l] // U
                x_T, y = ffn_inT[l], ffn_out[l]

                def normalised(t, k):
                    act.wait_ge(s["xnT_psum"], z["xnT_psum"] + t + 1)
                    run(x_T[k][:, :], bank(7, 0, U * D), ACT.Copy).then_inc(s["xnT_sbuf"], 1)

                def activate(t, k):
                    act.wait_ge(s["up_psum"], z["up_psum"] + t + 1)
                    run(hid[k][:, 0:U * F], bank(k, 0, U * F), FFN[l]["act"]).then_inc(s["act_ready"], 1)

                def take_y(t, k, first_two):
                    act.wait_ge(s["y_psum"], z["y_psum"] + t + 1)
                    if not first_two:
                        act.wait_ge(y_stored[k], 16 * (z["y_pairs"] + (t - k) // 2) if isinstance(t, int) else 16 * z["y_pairs"] + (t - k) * 8)
                    run(y[k][:, :], bank(6, 0, U * D), ACT.Copy).then_inc(s["y_taken"], 1)

                normalised(0, 0)
                normalised(1, 1)
                activate(0, 0)

                def body(i):
                    for k in range(2):
                        t = 2 * i + k
                        if exists(t + 1, n):
                            activate(t + 1, 1 - k)
                        if exists(t + 2, n):
                            normalised(t + 2, k)
                        if exists(t - 1, n):
                            take_y(t - 1, 1 - k, isinstance(t, int) and t - 1 < 2)
                pairs(act, n // 2, body)
                take_y(n - 1, 1, False)

            for no, (kind, l, sub) in enumerate(phases):
                z = at[no]
                if kind == "load":
                    act.wait_ge(s["loaded_first"], 16 * len(first_loads))
                    run(tanh_g[:, :], gates_in[:, :], ACT.Tanh)
                elif kind == "keys":
                    keys_phase(l, KV[l])
                elif kind == "attention":
                    attention_phase(l, z)
                elif kind == "router":
                    router_phase(l, z)
                elif kind in ("shared", "dense"):
                    shared_phase(kind, sub, l, z)
                elif kind == "routed":
                    routed_phase(l, z)
                elif kind == "fold":
                    act.wait_ge(s["fold_psum"], 1)
                    run(down_fold[:, :], bank(0), ACT.Copy)
                    run(up_col[:, :], bank(1).rearrange("p (c e) -> p c e", e=P)[:, :, 0], ACT.Copy)
                phase_end(act, no + 1)

        @block.vector
        def _(dve):
            tt, copy = nc.vector.tensor_tensor, nc.vector.tensor_copy
            links = [0]

            def link(instruction):
                links[0] += 1
                instruction.then_inc(s["dve_chain"], 1)
                dve.wait_ge(s["dve_chain"], links[0])

            def x_tile(t):
                return x[:, ds(t * D, D)]

            def normalise(t, k, out_tile=None):
                return nc.vector.tensor_scalar(xin[k][:, :] if out_tile is None else out_tile, x_tile(t),
                                               mean_var[:, ds(2 * t, 1)], rstd[:, ds(t, 1)], ALU.subtract, ALU.mult)

            def update_x(t, y, gate, z):
                nc.vector.scalar_tensor_tensor(x_tile(t), y, tanh_g[:, gate:gate + 1], x_tile(t), ALU.mult, ALU.add)\
                    .then_inc(s["x_new"], 1)
                dve.wait_ge(s["x_new"], z["x_new"] + t + 1)
                nc.vector.bn_stats(stats[:, ds(6 * t, 6)], x_tile(t))

            def all_stats():
                for t in range(TILES):
                    nc.vector.bn_stats(stats[:, 6 * t:6 * t + 6], x[:, t * D:(t + 1) * D])

            def stats_phase(l, sub):
                for t in range(TILES):
                    last = nc.vector.bn_aggr(mean_var[:, 2 * t:2 * t + 2], stats[:, 6 * t:6 * t + 6])
                last.then_inc(s["mean_var_done"], 1)

            def keys_phase(l, z):
                if l == 2:
                    for j in range(16):
                        dve.wait_ge(s["kv_psum"], z["kv_psum"] + j + 1)
                        dst = (kT2 if j < 8 else vT2)[:, (j % 8) * BK:(j % 8 + 1) * BK]
                        nc.vector.tensor_scalar(dst, bank(j % 8, 0, BK), colk2[:, 8 + j:9 + j], None, ALU.add)\
                            .then_inc(s["kv_evac_v"], 1)
                    tt(hid[1][:, 0:128].rearrange("p (c h) -> p c h", h=16), half_head[:, :].rearrange("p (c h) -> p c h", h=16),
                       colk2[:, 0:8].rearrange("p (c h) -> p c h", h=1).to_broadcast([P, 8, 16]), ALU.mult).then_inc(s["kv_evac_v"], 1)
                    nc.vector.memset(vw[0:CHUNKS[-2] + P - CHUNKS[-1], :], 0.0).then_inc(s["vw_zeroed"], 1)
                    for j in range(B * 4):
                        dve.wait_ge(s["kv_psum"], z["kv_psum"] + 33 + j + 1)
                        b, g = j // 4, j % 4
                        copy(vw_keys.rearrange("p (b f i h e) -> p b f i h e", b=B, f=2, h=2, e=D)[:, b, g // 2, :, g % 2, :],
                             bank(j % 8, parts=SK).rearrange("p (i e) -> p i e", e=D)).then_inc(s["kv_evac_v"], 1)
                    dve.wait_ge(s["kv_evac_a"], 1)
                    rest = hid[0][0:16, 0:BK]
                    for part in range(3):
                        to = r_bf_parts[0:16, part * BK:(part + 1) * BK]
                        link(copy(to, rest))
                        if part < 2:
                            link(tt(rest, rest, to, ALU.subtract))
                    nc.vector.memset(wait_slot[:, :], 0.0).then_inc(s["q_bias_parts"], 1)
                    return
                copy(repeated.rearrange("p (b h k) -> p b h k", b=B, k=SK),
                     ctxT[:, :].rearrange("p (b h k) -> p b h k", b=B, h=1).to_broadcast([P, B, HG, SK])).then_inc(s["kv_evac_v"], 1)
                if l == 1:
                    nc.vector.tensor_scalar(mask1_row[0:1, :], mask1_raw[0:1, :], 0.0, BIG_ROW, ALU.is_equal, ALU.mult)
                dve.wait_ge(s["kv_psum"], z["kv_psum"] + (2 if l == 3 else 1))
                if l == 0:
                    link(nc.vector.tensor_scalar(kT[:, :], bank(0, 0, BK), cols[:, 1:2], float(8.0 ** -0.5), ALU.add, ALU.mult))
                elif l == 1:
                    link(copy(kT[:, :], bank(0, 0, BK)))
                else:
                    rot = hid[0][:, 0:BK].rearrange("p (b k) -> p b k", k=SK)
                    k3 = kT[:, :].rearrange("p (b k) -> p b k", k=SK)
                    for table, n, o in ((rope_cos, 0, k3), (rope_sin, 1, rot)):
                        c = table[:, 0:SK].rearrange("p (b k) -> p b k", b=1).to_broadcast([P, B, SK])
                        last = tt(o, bank(n, 0, BK).rearrange("p (b k) -> p b k", k=SK), c, ALU.mult)
                    link(last)
                    link(tt(kT[:, :], kT[:, :], hid[0][:, 0:BK], ALU.add))
                    link(nc.vector.tensor_scalar(kT[:, :], kT[:, :], 0.25, None, ALU.mult))
                n, sel = (8, heads16) if l == 3 else (16, heads8)
                for b in range(B):
                    tt(keys[:, b * n * SK:(b + 1) * n * SK].rearrange("p (h k) -> p h k", k=SK),
                       kT[:, b * SK:(b + 1) * SK].rearrange("p (h k) -> p h k", h=1).to_broadcast([P, n, SK]),
                       sel[:, :].rearrange("p (h k) -> p h k", k=1).to_broadcast([P, n, SK]), ALU.mult)
                units, hd = ATT[l]["units"], HD[l]
                w = hd + 1
                v = values[l][:, 0:B * units * NC * HG * w].rearrange("p (b u c h w) -> p b u c h w", b=B, u=units, c=NC, w=w)
                for j in range(VJ):
                    dve.wait_ge(s["kv_psum"], z["kv_psum"] + (2 if l == 3 else 1) + j + 1)
                    for i in range(4):
                        b, c = (4 * j + i) // NC, (4 * j + i) % NC
                        last = tt(v[:, b, :, c, :, 0:hd], bank(2 + j % 4, i * D, (i + 1) * D).rearrange("p (u h w) -> p u h w", u=units, w=hd),
                                  row_head[:, c * HG:(c + 1) * HG].rearrange("p (u h w) -> p u h w", u=1, w=1)
                                  .to_broadcast([P, units, HG, hd]), ALU.mult)
                    last.then_inc(s["v_taken"], 1)
                for b in range(B):
                    for u in range(units):
                        copy(v[:, b, u, :, :, hd], row_head[:, :].rearrange("p (c h) -> p c h", h=HG))

            def attention_phase(l, z):
                units = ATT[l]["units"]

                def normalised(t, k, first_two):
                    if not first_two:
                        dve.wait_ge(s["xnT_psum"], z["xnT_psum"] + t - 1)
                    normalise(t, k).then_inc(s["xn_ready"], 1)

                def shift(t, h, p, first_ones):
                    u = t * units + h
                    k = p % 2
                    place = P_SLOTS[l][p]
                    dve.wait_ge(s["scores_psum"], z["scores_psum"] + u + 1)
                    src = scores(k)
                    if l == 2:
                        if h == 0:
                            dve.wait_ge(s["mask2_copied"], z["mask2_copied"] + t + 1)
                        m = mask2_tile[p // 2][:, :].rearrange("p (a h k) -> p a h k", a=1, h=1).to_broadcast([P, 2, HG // 2, SK])
                        c = masked2[:, :].rearrange("p (a h k) -> p a h k", a=1, h=1).to_broadcast([P, 2, HG // 2, SK])
                        nc.vector.memset(wait_slot[:, :], 0.0)
                        nc.vector.copy_predicated(src, m, c).then_inc(s["scores_prep"], 1)
                        dve.wait_ge(s["scores_prep"], z["scores_prep"] + u + 1)
                        nc.vector.tensor_reduce(row_max[p][:, :].rearrange("p (a h) -> p a h", a=2), src, AX.X, ALU.max, negate=True)\
                            .then_inc(s["row_max_done"], 1)
                        return
                    if not first_ones:
                        dve.wait_ge(s["probsT_psum"], z["probsT_psum"] + u - len(P_SLOTS[l]) + 1)
                    if l == 1:
                        tt(by_head(place), src, by_head(bias1[:, ds((t % QT) * (2 * UW) + h * UW, UW)]), ALU.add)\
                            .then_inc(s["scores_prep"], 1)
                        dve.wait_ge(s["scores_prep"], z["scores_prep"] + u + 1)
                        src = by_head(place)
                    nc.vector.reduce_max(row_max[p][:, :].rearrange("p (a h) -> p a h", a=2), src, AX.X).then_inc(s["row_max_done"], 1)
                    if l == 1:
                        dve.wait_ge(s["row_max_done"], z["row_max_done"] + 2 * u + 1)
                        nc.vector.tensor_scalar(row_max[p][:, :], row_max[p][:, :], MASKED_L1, None, ALU.max).then_inc(s["row_max_done"], 1)
                        dve.wait_ge(s["row_max_done"], z["row_max_done"] + 2 * u + 2)
                        p3 = place.rearrange("p (h k) -> p h k", k=SK)
                        nc.vector.scalar_tensor_tensor(p3, p3, MASKED_L1, row_max[p][:, :].rearrange("p (h k) -> p h k", k=1)
                                                       .to_broadcast([P, HG, SK]), ALU.max, ALU.subtract).then_inc(s["scores_shifted"], 1)
                    else:
                        dve.wait_ge(s["row_max_done"], z["row_max_done"] + u + 1)
                        tt(by_head(place), src, over_keys(row_max[p][:, :]), ALU.subtract).then_inc(s["scores_shifted"], 1)

                def scale_probs(t, h, p):
                    u = t * units + h
                    dve.wait_ge(s["probs_ready"], z["probs_ready"] + u + 1)
                    nc.vector.reciprocal(row_inv[p][:, :], row_sum[p][:, :]).then_inc(s["probs_inverted"], 1)
                    dve.wait_ge(s["probs_inverted"], z["probs_inverted"] + u + 1)
                    p3 = P_SLOTS[l][p].rearrange("p (h k) -> p h k", k=SK)
                    tt(p3, p3, row_inv[p][:, :].rearrange("p (h k) -> p h k", k=1).to_broadcast([P, HG, SK]), ALU.mult)\
                        .then_inc(s["probs_scaled"], 1)

                def rotate(t, k):
                    dve.wait_ge(s["qT_psum"], z["qT_psum"] + t + 1)
                    at_q = ds((t % QT) * P, P)
                    tt(ropeA, bank(MIX, D, 2 * D), rope_cos[:, at_q], ALU.mult).then_inc(s["rope_step"], 1)
                    tt(ropeB, bank(MIX, 2 * D, 3 * D), rope_sin[:, at_q], ALU.mult).then_inc(s["rope_step"], 1)
                    dve.wait_ge(s["rope_step"], z["rope_step"] + 2 * t + 2)
                    tt(qT[k][:, :], ropeA, ropeB, ALU.add).then_inc(s["qT_sbuf"], 1)

                def scale_out(t, k):
                    if l == 2:
                        return
                    w = HD[l] + 1
                    o = bank(OUT, 0, units * HG * w).rearrange("p (h w) -> p h w", w=w)
                    dve.wait_ge(s["out_psum"], z["out_psum"] + t + 1)
                    inv = out_inv[k][:, 0:units * HG].rearrange("p (h o) -> p h o", o=1)
                    nc.vector.reciprocal(inv, o[:, :, w - 1:w]).then_inc(s["out_inverted"], 1)
                    dve.wait_ge(s["out_inverted"], z["out_inverted"] + t + 1)
                    tt(out_n[k][:, :].rearrange("p (h w) -> p h w", w=w - 1), o[:, :, 0:w - 1],
                       inv.to_broadcast([P, units * HG, w - 1]), ALU.mult).then_inc(s["out_scaled"], 1)

                def new_x(t):
                    dve.wait_ge(s["proj_psum"], z["proj_psum"] + t + 1)
                    y = bank(OUT, 256, 256 + D) if l == 3 else bank(OUT if l == 2 else MIX, 0, D)
                    update_x(t, y, l, z)

                for t in range(2):
                    normalised(t, t, True)
                    if l == 3:
                        rotate(t, t)
                normalised(2, 0, False)
                shift(0, 0, 0, True)
                if l != 3:
                    shift(0, 1, 1, True)
                if l == 2:
                    scale_probs(0, 0, 0)

                def body(i):
                    for k in range(2):
                        t = 2 * i + k
                        early = isinstance(t, int)
                        if l == 3:
                            if exists(t + 1, TILES):
                                shift(t + 1, 0, 1 - k, early and t == 0)
                            if exists(t - 3, TILES):
                                new_x(t - 3)
                            if exists(t + 2, TILES):
                                rotate(t + 2, k)
                            if exists(t - 1, TILES):
                                scale_out(t - 1, 1 - k)
                            if exists(t + 3, TILES):
                                normalised(t + 3, 1 - k, False)
                        else:
                            if l != 2 and exists(t - 2, TILES):
                                new_x(t - 2)
                            if exists(t + 1, TILES):
                                shift(t + 1, 0, 2 - 2 * k, early and t == 0)
                            if l == 2:
                                scale_probs(t, 1, 2 * k + 1)
                            if exists(t - 1, TILES):
                                scale_out(t - 1, 1 - k)
                                if l == 2:
                                    new_x(t - 1)
                            if exists(t + 3, TILES):
                                normalised(t + 3, 1 - k, False)
                            if exists(t + 1, TILES):
                                shift(t + 1, 1, 3 - 2 * k, early and t == 0)
                                if l == 2:
                                    scale_probs(t + 1, 0, 2 - 2 * k)
                pairs(dve, TILES // 2, body, 2 if l == 3 else 1, 2)
                if l != 2:
                    new_x(TILES - 3 if l == 3 else TILES - 2)
                scale_out(TILES - 1, 1)
                if l == 3:
                    new_x(TILES - 2)
                new_x(TILES - 1)

            def first_best(values_, hot, E):
                v = values_[:, 0:TILES * E].rearrange("p (t e) -> p t e", e=E)
                a = r["a"][:, 0:TILES * E]
                a3 = a.rearrange("p (t e) -> p t e", e=E)
                top = r_m["m3"][:, :].rearrange("p (t e) -> p t e", e=1).to_broadcast([P, TILES, E])
                link(nc.vector.reduce_max(r_m["m3"][:, :], v, AX.X))
                link(tt(a3, v, top, ALU.is_equal))
                link(tt(a, a, rc["rev"][:, 0:TILES * E], ALU.mult))
                link(nc.vector.reduce_max(r_m["m2"][:, :], a3, AX.X))
                link(tt(hot[:, 0:TILES * E].rearrange("p (t e) -> p t e", e=E), a3,
                        r_m["m2"][:, :].rearrange("p (t e) -> p t e", e=1).to_broadcast([P, TILES, E]), ALU.is_equal))

            def router_phase(l, z):
                E = FFN[l]["E"]
                W = TILES * E
                choices = 2 if l == 3 else 1

                def te(ap):
                    return ap[:, 0:W].rearrange("p (t e) -> p t e", e=E)

                def et(ap):
                    return ap[:, 0:W].rearrange("p (e t) -> p e t", t=TILES)

                def t_by_e(ap):
                    return ap[:, 0:W].rearrange("p (e t) -> p t e", t=TILES)

                for t in range(TILES):
                    normalise(t, 0, xn_all[:, t * D:(t + 1) * D]).then_inc(s["xn_ready"], 1)
                if l == 2:
                    tt(brow[0:1, 3 * D:4 * D], brow[0:1, 3 * D:4 * D], brow[0:1, 4 * D:5 * D], ALU.add)
                    return
                dve.wait_ge(s["logits_psum"], z["logits_psum"] + TILES)
                link(copy(r["logit"][:, 0:W], bank(0, 0, W)))
                first_best(r["logit"], r["hot1"], E)
                link(copy(r_m["m1"][:, :], r_m["m3"][:, :]))
                copy(r_bf[0][:, 0:W], r["hot1"][:, 0:W]).then_inc(s["hots_ready"], 1)
                if l == 3:
                    link(nc.vector.scalar_tensor_tensor(r["b"][:, 0:W], r["hot1"][:, 0:W], -3e38, r["logit"][:, 0:W], ALU.mult, ALU.add))
                    first_best(r["b"], r["hot2"], E)
                    copy(r_bf[1][:, 0:W], r["hot2"][:, 0:W]).then_inc(s["hots_ready"], 1)
                    tt(te(r["prob"]), te(r["logit"]), r_m["m1"][:, :].rearrange("p (t e) -> p t e", e=1)
                       .to_broadcast([P, TILES, E]), ALU.subtract).then_inc(s["softmax_done"], 1)
                dve.wait_ge(s["rank_psum"], HOTS[l] + choices)
                for c in range(choices):
                    tot, scan = r[f"tot{c + 1}"], r[f"scan{c + 1}"]
                    link(copy(et(tot), bank(2 + 2 * c, 0, W).rearrange("p (t e) -> p e t", e=E)))
                    link(nc.vector.tensor_tensor_scan(scan[:, 0:W], rc["carry"][:, 0:W], tot[:, 0:W], 0.0, ALU.mult, ALU.add))
                    link(copy(r_m["cnt1" if c == 0 else "kp"][:, 0:E], et(scan)[:, :, TILES - 1]))
                    link(tt(tot[:, 0:W], scan[:, 0:W], tot[:, 0:W], ALU.subtract))
                if choices == 2:
                    link(tt(r_m["cnt"][:, 0:E], r_m["cnt1"][:, 0:E], r_m["kp"][:, 0:E], ALU.add))
                else:
                    link(copy(r_m["cnt"][:, 0:E], r_m["cnt1"][:, 0:E]))
                link(tt(et(r["a"]), r_m["cnt"][:, 0:E].rearrange("p (e t) -> p e t", t=1).to_broadcast([P, E, TILES]),
                        et(rc["step"]), ALU.is_gt))
                link(nc.vector.reduce_sum(r_m["nt"][:, 0:E], et(r["a"]), AX.X))
                link(nc.vector.tensor_tensor_scan(r_m["cum"][:, 0:E], ones16[:, 0:E], r_m["nt"][:, 0:E], 0.0, ALU.mult, ALU.add))
                link(tt(r_m["base"][:, 0:E], r_m["cum"][:, 0:E], r_m["nt"][:, 0:E], ALU.subtract))
                link(nc.vector.tensor_scalar(r_m["base"][:, 0:E], r_m["base"][:, 0:E], float(P), None, ALU.mult))
                for c in range(choices):
                    hot = r[f"hot{c + 1}"]
                    link(tt(te(r["a"]), bank(1 + 2 * c, 0, W).rearrange("p (t e) -> p t e", e=E), t_by_e(r[f"tot{c + 1}"]), ALU.add))
                    link(tt(r["a"][:, 0:W], r["a"][:, 0:W], hot[:, 0:W], ALU.mult))
                    link(nc.vector.reduce_sum(r_m["sr"][:, :], te(r["a"]), AX.X))
                    if c == 1:
                        link(tt(r_m["base"][:, 0:E], r_m["base"][:, 0:E], r_m["cnt1"][:, 0:E], ALU.add))
                    link(tt(te(r["a"]), te(hot), r_m["base"][:, 0:E].rearrange("p (t e) -> p t e", t=1).to_broadcast([P, TILES, E]), ALU.mult))
                    link(nc.vector.reduce_sum(r_m["pf"][:, :], te(r["a"]), AX.X))
                    link(tt(r_m["pf"][:, :], r_m["pf"][:, :], r_m["sr"][:, :], ALU.add))
                    link(copy(pos[c][:, :], r_m["pf"][:, :]))
                    if l == 3:
                        w = r_m[f"w{c + 1}"]
                        link(nc.vector.tensor_scalar(r_m["kp"][:, :], r_m["sr"][:, :], float(CAPACITY), None, ALU.is_lt))
                        if c == 0:
                            dve.wait_ge(s["softmax_done"], 2)
                            link(nc.vector.reduce_sum(r_m["sum"][:, :], te(r["prob"]), AX.X))
                            link(nc.vector.reciprocal(r_m["sum"][:, :], r_m["sum"][:, :]))
                        link(tt(r["b"][:, 0:W], r["prob"][:, 0:W], hot[:, 0:W], ALU.mult))
                        link(nc.vector.reduce_sum(w[:, :], te(r["b"]), AX.X))
                        link(tt(w[:, :], w[:, :], r_m["sum"][:, :], ALU.mult))
                        link(tt(w[:, :], w[:, :], r_m["kp"][:, :], ALU.mult))
                n = ROUTED_TILES[l]
                over = psum[:, 5 * BANK:5 * BANK + n * E].rearrange("p (n e) -> p n e", e=E)
                link(tt(over, r_m["cum"][:, 0:E].rearrange("p (n e) -> p n e", n=1).to_broadcast([P, n, E]),
                        slot_no[:, 0:n * E].rearrange("p (n e) -> p n e", e=E), ALU.is_le))
                link(nc.vector.reduce_sum(expert_f[:, 0:n], over, AX.X))
                link(nc.vector.tensor_scalar(expert_f[:, 0:n], expert_f[:, 0:n], float(E - 1), None, ALU.min))
                if UNIT[l] > 1:
                    link(tt(expert_f[:, 0:n], expert_f[:, 0:n], digits[:, 0:n], ALU.mult))
                    n = n // UNIT[l]
                    link(nc.vector.reduce_sum(expert_f[:, 0:n], expert_f[:, :].rearrange("p (n u) -> p n u", u=UNIT[l]), AX.X))
                link(copy(expert_of[:, 0:n], expert_f[:, 0:n]))
                if l == 1:
                    dve.wait_ge(s["gate_ready"], 1)
                    rows3 = xn_all[:, :].rearrange("p (t e) -> p t e", e=D)
                    link(tt(rows3, rows3, r_m["kp"][:, :].rearrange("p (t e) -> p t e", e=1).to_broadcast([P, TILES, D]), ALU.mult))

            def shared_phase(kind, part, l, z):
                cs = chunks(FFN[l]["F"])
                C = len(cs)
                groups = group_range(kind, part)

                def new_x(g):
                    n = g - groups[0]
                    dve.wait_ge(s["y_psum"], z["y_psum"] + n + 1)
                    x_group = x[:, g * 512:(g + 1) * 512]
                    nc.vector.scalar_tensor_tensor(x_group, bank(6 + n % 2), tanh_g[:, 4 + l:5 + l], x_group, ALU.mult, ALU.add)\
                        .then_inc(s["x_new"], 1)
                    if kind == "dense":
                        dve.wait_ge(s["x_new"], z["x_new"] + n + 1)
                        for t in range(4 * g, 4 * g + 4):
                            nc.vector.bn_stats(stats[:, 6 * t:6 * t + 6], x[:, t * D:(t + 1) * D])

                for g in groups:
                    for c, (c0, cn) in enumerate(cs):
                        n = g - groups[0]
                        j = n * C + c
                        h = ((n % 2) * C + c) * 512
                        if kind != "dense":
                            dve.wait_ge(s["act_ready"], z["act_ready"] + j + 1)
                            tt(hidT_all[0:cn, h:h + 512], hidT_all[0:cn, h:h + 512], bank(2 + j % 2, parts=cn), ALU.mult)\
                                .then_inc(s["hid_ready"], 1)
                        if c == 2 and n >= 1:
                            new_x(g - 1)
                new_x(groups[-1])

            def routed_phase(l, z):
                F, U = FFN[l]["F"], UNIT[l]
                n = ROUTED_TILES[l] // U

                def gate(t, k):
                    dve.wait_ge(s["act_ready"], z["act_ready"] + t + 1)
                    tt(hid[k][:, 0:U * F], hid[k][:, 0:U * F], bank(2 + k, 0, U * F), ALU.mult).then_inc(s["hid_ready"], 1)

                def hidden_copy(t, k):
                    dve.wait_ge(s["hidT_psum"], z["hidT_psum"] + t + 1)
                    full = U * F // P * P
                    last = copy(hidT[k][:, 0:full], bank(4 + k, 0, full))
                    if U * F > full:
                        last = copy(hidT[k][0:U * F - full, full:full + P], bank(4 + k, full, full + P, parts=U * F - full))
                    last.then_inc(s["hidT_sbuf"], 1)

                gate(0, 0)

                def body(i):
                    for k in range(2):
                        t = 2 * i + k
                        if exists(t + 1, n):
                            gate(t + 1, 1 - k)
                        hidden_copy(t, k)
                pairs(dve, n // 2, body)

            def combine_phase(l):
                dve.wait_ge(s["gathered"], 16 * GATHERS[l])
                if l < 3:
                    link(nc.vector.scalar_tensor_tensor(x[:, :], xn_all[:, :], tanh_g[:, 4 + l:5 + l], x[:, :], ALU.mult, ALU.add))
                    all_stats()
                    return
                for buf, w in ((xn_all[:, :], "w1"), (keys[:, 0:TILES * D], "w2")):
                    y3 = buf.rearrange("p (t e) -> p t e", e=D)
                    link(tt(y3, y3, r_m[w][:, :].rearrange("p (t e) -> p t e", e=1).to_broadcast([P, TILES, D]), ALU.mult))
                    link(nc.vector.scalar_tensor_tensor(x[:, :], buf, tanh_g[:, 4 + l:5 + l], x[:, :], ALU.mult, ALU.add))

            for no, (kind, l, sub) in enumerate(phases):
                z = at[no]
                if kind == "load":
                    nc.vector.memset(zeros[:, :], 0.0).then_inc(s["zeros_set"], 1)
                    nc.vector.memset(ones_bf[:, :], 1.0)
                    nc.vector.memset(ones_row[:, :], 1.0)
                    nc.vector.memset(ones16[:, :], 1.0)
                    nc.vector.memset(minus_half[:, :], -0.5)
                    nc.vector.memset(masked2[:, :], MASKED_L2)
                    dve.wait_ge(s["loaded_first"], 16 * len(first_loads))
                    copy(earlier[:, :], earlier_f[:, :])
                    all_stats()
                elif kind == "stats":
                    stats_phase(l, sub)
                elif kind == "keys":
                    keys_phase(l, KV[l])
                elif kind == "attention":
                    attention_phase(l, z)
                elif kind == "router":
                    router_phase(l, z)
                elif kind in ("shared", "dense"):
                    shared_phase(kind, sub, l, z)
                elif kind == "routed":
                    routed_phase(l, z)
                elif kind == "combine":
                    combine_phase(l)
                phase_end(dve, no + 1)

        @block.gpsimd
        def _(pool):
            tt = nc.gpsimd.tensor_tensor
            links = [0]
            loads, weight_loads = [0], [0, 0]

            def link(instruction):
                links[0] += 1
                instruction.then_inc(s["pool_chain"], 1)
                pool.wait_ge(s["pool_chain"], links[0])

            def load(dst, src):
                loads[0] += 1
                pool.dma_start(dst, src).then_inc(s["bfly_loaded"], 16)
                pool.wait_ge(s["bfly_loaded"], 16 * loads[0])

            def butterfly(src, dst_last, other, temps, weights, w_sb, rows_, stages, transposed):
                bufs = [src, other]


                def load_weights(n):
                    pool.dma_start(w_sb[n % 2], weights[stages[n], :, :, :].rearrange("(a k) i j -> a (k i j)", a=1)
                                   .to_broadcast([P, 4 * (HID // 2)])).then_inc(bfly_weights[n % 2], 16)
                load_weights(0)
                for n, stage in enumerate(stages):
                    if n + 1 < len(stages):
                        load_weights(n + 1)
                    weight_loads[n % 2] += 1
                    pool.wait_ge(bfly_weights[n % 2], 16 * weight_loads[n % 2])
                    st = 2 ** stage
                    nb = HID // (2 * st)
                    i, o = bufs[n % 2], dst_last if n == len(stages) - 1 else bufs[(n + 1) % 2]

                    def half(buf, which):
                        return buf.rearrange("p (r n h s) -> p r n h s", r=rows_, h=2, s=st)[:, :, :, which, :]

                    def weight(a, b):
                        c = 2 * b + a if transposed else 2 * a + b
                        w = w_sb[n % 2].rearrange("p (r n s c) -> p r n s c", r=1, s=st, c=4)[:, :, :, :, c]
                        return w.to_broadcast([P, rows_, nb, st]) if rows_ > 1 else w

                    def temp(k):
                        return temps[k].rearrange("p (r n s) -> p r n s", r=rows_, s=st)
                    for a in range(2):
                        tt(temp(0), half(i, 0), weight(a, 0), ALU.mult)
                        link(tt(temp(1), half(i, 1), weight(a, 1), ALU.mult))
                        link(tt(half(o, a), temp(0), temp(1), ALU.add))

            for no, (kind, l, sub) in enumerate(phases):
                z = at[no]
                if kind == "stats":
                    pool.wait_ge(s["mean_var_done"], STATS[no] + 1)
                    link(nc.gpsimd.tensor_scalar(var_eps[:, :], mean_var[:, :].rearrange("p (t c) -> p t c", c=2)[:, :, 1],
                                                 EPS, None, ALU.add))
                    link(tt(rstd[:, :], var_eps[:, :], minus_half[:, :], ALU.pow))
                    if l == 1 and sub == 0:
                        link(nc.gpsimd.tensor_copy(down_T[:, :], region_c[:, 4096:4096 + HID]))
                elif kind == "routed" and l == 0:
                    load(region_c[:, 0:HID], d["L2_ffn_W_conT"])
                    result = region_c[:, 4096:4096 + HID]
                    butterfly(region_c[:, 0:HID], result, result, [region_c[:, 1024:1280], region_c[:, 1280:1536]],
                              d["L2_ffn_down_weights"], [region_c[:, 1536:2560], region_c[:, 2560:3584]], 1, list(range(STAGES))[::-1], True)
                elif kind == "attention" and l == 1:
                    a, b2, bias = region_a[:, 3584:4608], region_a[:, 4608:5632], region_a[:, 5632:6144]
                    load(a[:, 0:HID], d["L2_ffn_W_exp"])
                    load(a[:, HID:2 * HID], rows("L2_ffn_b_exp").to_broadcast([P, HID]))
                    load(bias, rows("L2_ffn_up_bias").to_broadcast([P, HID]))
                    butterfly(a, up_fold, b2, [region_a[:, 2560:3072], region_a[:, 3072:3584]], d["L2_ffn_up_weights"],
                              [region_a[:, 512:1536], region_a[:, 1536:2560]], 2, list(range(STAGES)), False)
                    link(tt(up_fold[:, HID:], up_fold[:, HID:], bias, ALU.add))
                elif kind == "attention" and l == 2:
                    def body(i):
                        for k in range(2):
                            t = 2 * i + k
                            if not (isinstance(t, int) and t < 2):
                                pool.wait_ge(s["scores_prep"], z["scores_prep"] + 2 * (t - 1))
                            nc.gpsimd.tensor_copy(mask2_tile[k][:, :], mask2[:, ds(t * SK, SK)]).then_inc(s["mask2_copied"], 1)
                    pairs(pool, TILES // 2, body)
                elif (kind == "shared" and sub == 0) or (kind == "routed" and l == 3):
                    pool.wait_ge(s["slots_zeroed"], 16)
                    for c in range(2 if l == 3 else 1):
                        for t in range(TILES):
                            pool.indirect_dma_start(sorted_in, bass.IndirectOffsetOnAxis(ap=pos[c][:, t:t + 1], axis=0),
                                                    xn_all[:, t * D:(t + 1) * D], None).then_inc(s["scattered"], 16)
                elif (kind == "shared" and sub == 1) or (kind == "combine" and l == 3):
                    for c in range(2 if l == 3 else 1):
                        buf = keys if c else xn_all
                        for t in range(TILES):
                            pool.indirect_dma_start(buf[:, t * D:(t + 1) * D], None, sorted_out[l],
                                                    bass.IndirectOffsetOnAxis(ap=pos[c][:, t:t + 1], axis=0)).then_inc(s["gathered"], 16)
                phase_end(pool, no + 1)


def kernel(**inputs):
    import numpy as _np
    import concourse.bacc as _bacc
    from concourse import mybir as _mybir
    from concourse.bass_utils import run_bass_kernel_spmd as _run

    a = {k: _np.asarray(v) for k, v in inputs.items()}
    T = lambda m: _np.ascontiguousarray(_np.swapaxes(m, -1, -2))
    keep = {"g_xattn", "g_ffn"}
    g = {k: a[k] for k in a if k in keep or (k.startswith("L") and k not in (
        "L1_xattn_Wq", "L1_xattn_Wk", "L1_xattn_Wv", "L1_xattn_Wo", "L1_xattn_rel_bias", "L2_xattn_wK_w", "L2_xattn_wV_w",
        "L2_xattn_wOut_w", "L2_ffn_W_con", "L3_xattn_Wq", "L3_xattn_Wkv", "L3_xattn_Wout"))}
    g["x"] = a["x"].reshape(TOKENS, D)
    g["ctxT"] = T(a["ctx_1024"].reshape(BK, D))
    g["ctxT_backwards"] = T(a["ctx_1024"][:, ::-1].reshape(BK, D))
    for n in ("Wq", "Wk", "Wv", "Wo"):
        g[f"L1_xattn_{n}T"] = T(a[f"L1_xattn_{n}"])
    g["rel_T"] = T(a["L1_xattn_rel_bias"])
    g["L2_xattn_WkT"], g["L2_xattn_WvT"] = T(a["L2_xattn_wK_w"]), T(a["L2_xattn_wV_w"])
    g["L2_xattn_WoT"] = T(a["L2_xattn_wOut_w"])
    g["L2_ffn_W_conT"] = T(a["L2_ffn_W_con"])
    halves = _np.arange(D).reshape(8, 2, 8)[:, ::-1, :].reshape(D)
    wk3, wv3 = a["L3_xattn_Wkv"][:D], a["L3_xattn_Wkv"][D:]
    g["L3_xattn_WqT"], g["L3_xattn_WqT_swapped"] = T(a["L3_xattn_Wq"]), T(a["L3_xattn_Wq"][halves])
    g["L3_xattn_WkT"], g["L3_xattn_WkT_swapped"] = T(wk3), T(wk3[halves])
    g["L3_xattn_WvT"], g["L3_xattn_WoT"] = T(wv3), T(a["L3_xattn_Wout"])
    g["mask1"] = _np.ascontiguousarray(a["mask_Bx1x1xS2_bk0"].reshape(B, SK)[:, ::-1]).reshape(1, BK)
    g["mask2"] = a["mask_BxSxS2_bf0"].reshape(TOKENS, SK)
    g.update(shape_constants())

    nc = _bacc.Bacc("TRN2", target_bir_lowering=False, num_devices=1)
    arrays, d = {}, {}
    for name, v in g.items():
        v = _np.ascontiguousarray(v)
        arrays[f"in_{name}"] = v
        d[name] = nc.dram_tensor(f"in_{name}", v.shape, _mybir.dt.from_np(v.dtype), kind="ExternalInput").ap()
    out = nc.dram_tensor("out_x", (TOKENS, D), _mybir.dt.float32, kind="ExternalOutput").ap()
    flamingo_kernel(nc, d, out)
    r = _run(nc, [arrays], core_ids=[0])
    return r.results[0]["out_x"].reshape(B, S, D)
```

```python
import numpy as np

import concourse.bass as bass
from concourse import mybir
from contextlib import ExitStack

P = 128
B, S, SK, D = 4, 512, 77, 128
TOKENS = B * S
TILES = TOKENS // P
QT = S // P
GROUPS = TILES // 4
BK = B * SK
HG = 8
UW = HG * SK
CHUNKS = tuple(min(c, UW - P) for c in range(0, UW, P))
NC = len(CHUNKS)
TW = NC * P
BANK = 512
EPS = 1e-5
BUCKETS = 32
DELTAS = S + SK - 1
CHOICE_TILES = {0: TILES + 8, 1: TILES + 8, 3: TILES + 16}
CHOICES = {0: 1, 1: 1, 3: 2}
ROUTED_TILES = {l: CHOICES[l] * n for l, n in CHOICE_TILES.items()}
CAPACITY = 320
STAGES = 9
HID = 512
BIG_ROW = -(2.0 ** 100)
MASKED_L1 = -1e9
MASKED_L2 = -1e4


def relative_buckets():
    rp = np.arange(DELTAS) - (S - 1)
    half = BUCKETS // 2
    exact = half // 2
    dist = np.abs(rp)
    ratio = np.log(np.maximum(dist, 1).astype(np.float32) / np.float32(exact)).astype(np.float32)
    large = exact + (ratio / np.float32(np.log(128 / exact)) * np.float32(half - exact)).astype(np.int32)
    large = np.minimum(large, half - 1)
    return (rp > 0) * half + np.where(dist < exact, dist, large)


def shape_constants():
    c = {}
    c["ident"] = np.eye(P, dtype=np.float32)
    for name, hd in (("heads8", 8), ("heads16", 16)):
        n = P // hd
        c[name] = (np.arange(P)[:, None] // hd == np.arange(n)[None, :]).astype(np.float32)
    row = np.arange(P)[:, None] + np.array(CHUNKS)[None, :]
    seen = np.array([0] + [c + P for c in CHUNKS[:-1]])[None, :]
    c["row_head"] = ((row[:, :, None] // SK == np.arange(HG)) & (row >= seen)[:, :, None]).astype(np.float32).reshape(P, NC * HG)
    half, chunk, h = np.ogrid[0:P, 0:8, 0:16]
    c["half_head"] = ((h == 2 * chunk + half // 64)).astype(np.float32).reshape(P, 8 * 16)
    c["earlier"] = (np.arange(P)[:, None] < np.arange(P)[None, :]).astype(np.float32)
    c["bucket_hot"] = (np.arange(BUCKETS)[:, None] == relative_buckets()[None, ::-1]).astype(np.float32)
    j = np.arange(0, 16, 2, dtype=np.float32)
    inv = (np.float32(1.0) / np.power(np.float32(10000.0), j / np.float32(16))).astype(np.float32)
    freq = np.arange(S, dtype=np.float32)[None, :] * inv[:, None]
    cos, sin = np.cos(freq).astype(np.float32), np.sin(freq).astype(np.float32)
    c["rope_cos"] = np.tile(np.concatenate([cos, cos]), (8, 1))
    c["rope_sin"] = np.tile(np.concatenate([-sin, sin]), (8, 1))
    for e in (8, 16):
        c[f"rev{e}"] = np.broadcast_to(np.arange(e, 0, -1, dtype=np.float32), (P, TILES, e)).reshape(P, TILES * e)
        c[f"step{e}"] = np.broadcast_to(np.arange(TILES, dtype=np.float32) * P, (P, e, TILES)).reshape(P, e * TILES)
        keep = np.ones((P, e, TILES), np.float32)
        keep[:, :, 0] = 0
        c[f"carry{e}"] = keep.reshape(P, e * TILES)
    c["digits"] = np.broadcast_to(np.tile(16.0 ** np.arange(4), ROUTED_TILES[3] // 4), (P, ROUTED_TILES[3]))
    n = ROUTED_TILES[0]
    c["slot8"] = np.broadcast_to(np.arange(n, dtype=np.float32)[None, :, None], (P, n, 8)).reshape(P, n * 8)
    n = CHOICE_TILES[3]
    c["slot16"] = np.broadcast_to(np.arange(n, dtype=np.float32)[None, :, None], (P, n, 16)).reshape(P, n * 16)
    return {k: np.ascontiguousarray(v, dtype=np.float32) for k, v in c.items()}


def flamingo_kernel(nc, d, out):
    f32, bf16, i32, u8 = mybir.dt.float32, mybir.dt.bfloat16, mybir.dt.int32, mybir.dt.uint8
    ALU, ACT, AX = mybir.AluOpType, mybir.ActivationFunctionType, mybir.AxisListType
    ds = bass.ds

    ctx = ExitStack()
    with ctx:
        ctx.enter_context(nc.allow_non_contiguous_dma(reason="small vectors and Toeplitz rows"))

        def sb(name, cols, dt=f32, parts=P):
            return ctx.enter_context(nc.sbuf_tensor(name, [parts, cols], dt))

        def sem(name):
            return ctx.enter_context(nc.semaphore(name))

        x = sb("x", TILES * D)
        xn_all = sb("xn_all", TILES * D)
        region_a = sb("region_a", 9 * 1024 + 9 * 512)
        region_b = sb("region_b", 9 * 704 + 9 * 384)
        region_c = sb("region_c", 4 * 16 * SK)
        keys = sb("keys", B * 16 * SK)
        ctxT = sb("ctxT", BK)
        kT = sb("kT", BK)
        ident = sb("ident", P)
        earlier = sb("earlier", P, bf16)
        ones_bf = sb("ones_bf", P, bf16)
        ones_row = sb("ones_row", P, parts=1)
        heads8 = sb("heads8", 16)
        heads16 = sb("heads16", 8)
        row_head = sb("row_head", NC * HG)
        half_head = sb("half_head", 8 * 16)
        wq = sb("wq", D)
        wk = sb("wk", D)
        wv = sb("wv", D)
        wo = sb("wo", D)
        wqs = sb("wqs", D)
        wks = sb("wks", D)
        cols = sb("cols", 4)
        colk2 = sb("colk2", 24)
        brow = sb("brow", 5 * D, parts=1)
        gates_in = sb("gates_in", 8)
        tanh_g = sb("tanh_g", 8)
        tile_bn = [sb(f"tile_bn{s}", 6) for s in range(2)]
        tile_mv = [sb(f"tile_mv{s}", 2) for s in range(2)]
        tile_var = [sb(f"tile_var{s}", 1) for s in range(2)]
        stats = sb("stats", TILES * 6)
        mean_var = sb("mean_var", TILES * 2)
        rstd = sb("rstd", TILES)
        var_eps = sb("var_eps", TILES)
        minus_half = sb("minus_half", TILES)
        ones16 = sb("ones16", 16)
        xin = [sb(f"xin{s}", D) for s in range(2)]
        xnT = [sb(f"xnT{s}", D) for s in range(2)]
        qT = [sb(f"qT{s}", D) for s in range(2)]
        row_max = [sb(f"row_max{s}", HG) for s in range(4)]
        row_sum = [sb(f"row_sum{s}", HG) for s in range(4)]
        row_inv = [sb(f"row_inv{s}", HG) for s in range(4)]
        probs = [sb(f"probs{s}", UW) for s in range(2)]
        probsT = [sb(f"probsT{s}", TW) for s in range(2)]
        out_inv = [sb(f"out_inv{s}", 16) for s in range(2)]
        out_n = [sb(f"out_n{s}", D) for s in range(2)]
        outT = sb("outT", D)
        bucket_hot = xn_all[0:BUCKETS, 0:DELTAS]
        rel_by_delta = xn_all[0:16, DELTAS:2 * DELTAS]
        rope_cos, rope_sin = xn_all[:, 0:S], xn_all[:, S:2 * S]
        rel_T = sb("rel_T", 16, parts=BUCKETS)
        mask1_raw = sb("mask1_raw", BK, u8, parts=1)
        mask1_row = sb("mask1_row", BK, bf16, parts=1)
        mask2 = sb("mask2", TILES * SK, u8)
        mask2_tile = [sb(f"mask2_tile{s}", SK, u8) for s in range(2)]
        up_col = sb("up_col", 4)
        masked2 = sb("masked2", 1)
        stepped = sb("stepped", 8)
        router_w = sb("router_w", 16)
        hid = [sb(f"hid{s}", HID) for s in range(2)]
        hidT = [sb(f"hidT{s}", HID) for s in range(2)]
        earlier_f = hid[1][:, 0:D]
        ropeA, ropeB = hid[0][:, 0:D], hid[1][:, 0:D]
        y_out = [sb(f"y_out{s}", D) for s in range(2)]
        NR = TILES * 16
        region_r = sb("region_r", 10 * NR)
        r = {n: region_r[:, k * NR:(k + 1) * NR] for k, n in enumerate(
            ("logit", "a", "b", "hot1", "hot2", "tot1", "tot2", "scan1", "scan2", "prob"))}
        r_bf = [sb(f"r_bf{k}", NR, bf16) for k in range(2)]
        rc = {n: sb(f"rc_{n}", NR) for n in ("rev", "step", "carry")}
        slot_no = sb("slot_no", CHOICE_TILES[3] * 16)
        r_m = {n: sb(f"rm_{n}", 16) for n in ("m1", "m2", "m3", "nt", "cum", "base", "w1", "w2", "sum", "pf", "kp", "sr")}
        pos = [sb(f"pos{k}", TILES, i32) for k in range(2)]
        expert_f = sb("expert_f", ROUTED_TILES[3])
        expert_of = sb("expert_of", ROUTED_TILES[0], i32)
        digits = sb("digits", ROUTED_TILES[3])
        tail = 9 * 1536 - 3 * HID
        up_fold = region_a[:, tail:tail + 2 * HID]
        down_fold = region_a[:, tail + 2 * HID:]
        zeros = y_out[0]
        q_bias = region_r[0:3, 0:B * 16 * SK // 2].bitcast(bf16)

        psum = ctx.enter_context(nc.psum_tensor("psum", [P, 8 * BANK], f32))

        def bank(n, a=0, b=BANK, parts=P):
            return psum[0:parts, n * BANK + a:n * BANK + b]

        sorted_in = [nc.dram_tensor(f"sorted_in{c}", (CHOICE_TILES[3] * P, D), f32).ap() for c in range(2)]
        sorted_out = {l: [nc.dram_tensor(f"sorted_out{l}_{c}", (n * P, D), f32).ap() for c in range(CHOICES[l])]
                      for l, n in CHOICE_TILES.items()}
        vw_dram = nc.dram_tensor("vw_dram", (B, 2, UW, D), f32).ap()
        rel_dram = nc.dram_tensor("rel_dram", (16, DELTAS), f32)

        s = {n: sem(n) for n in (
            "phase_done", "loaded_first", "loaded_second", "loaded_rest", "zeros_set", "slots_zeroed", "kv_psum", "kT_ready",
            "rel_stored", "bias_first", "bias_loaded", "reloaded", "xn_ready", "xnT_psum", "xnT_sbuf", "qT_psum",
            "qT_sbuf", "rope_step", "scores_psum", "scores_prep", "row_max_done", "scores_shifted", "probs_ready",
            "probs_inverted", "probs_scaled", "probsT_psum", "probsT_sbuf", "out_psum", "out_inverted", "out_scaled",
            "outT_psum", "outT_sbuf", "proj_psum", "x_new", "stats_done", "mask2_copied", "dve_chain", "pool_chain",
            "logits_psum", "rank_psum", "hots_ready", "pos_ready", "weights_ready", "scattered", "scattered_second", "up_psum",
            "act_ready", "hid_ready", "y_psum", "y_taken", "bfly_loaded", "stored",
            "v_taken", "down_moved", "repeated", "tables_loaded", "x_loaded", "experts_loaded", "rel_psum",
            "rel_evac", "kv_evac_v", "kv_evac_a", "vw_zeroed", "rstd_ready", "var_ready", "mean_var_done",
            "fold_psum", "q_bias_parts", "q_bias_loaded", "vw_stored", "vw_loaded", "gate_ready", "softmax_done",
            "combined")}
        xin_loaded = [sem(f"xin_loaded{k}") for k in range(2)]
        bfly_weights = [sem(f"bfly_weights{k}") for k in range(2)]
        gathered = [sem(f"gathered{g}") for g in range(GROUPS)]
        y_stored = [sem(f"y_stored{k}") for k in range(2)]

        def pairs(eng, n_pairs, body, first=1, last=1):
            for i in range(first):
                body(i)
            with eng.Fori(first, n_pairs - last) as i:
                body(i)
            for i in range(n_pairs - last, n_pairs):
                body(i)

        def exists(t, n):
            return 0 <= t < n if isinstance(t, int) else True

        ENGINES = 5

        def phase_end(eng, no):
            eng.drain().then_inc(s["phase_done"], 1)
            eng.wait_ge(s["phase_done"], ENGINES * no)

        ATT = {l: dict(layer=l, units=1 if l == 3 else 2) for l in range(4)}
        FFN = {0: dict(E=8, F=HID, act=ACT.Gelu), 1: dict(E=8, F=352, act=ACT.Silu),
               2: dict(E=0, F=HID, act=ACT.Gelu), 3: dict(E=16, F=128, act=ACT.Silu)}
        phases = [("load", 0, 0)]
        for l in range(4):
            phases.append(("keys", l, 0))
            phases.append(("attention", l, 0))
            if l == 1:
                phases.append(("stats", l, 1))
            if l == 2:
                phases.append(("router", l, 0))
                phases.append(("dense", l, 0))
            else:
                phases.append(("router", l, 0))
                if l < 2:
                    phases.append(("shared", l, 0))
                phases.append(("routed", l, 0))
                if l < 2:
                    phases.append(("shared", l, 1))
                if l == 3:
                    phases.append(("combine", l, 0))

        UNIT = {0: 1, 1: 1, 3: 4}

        def group_range(kind, part):
            if kind == "dense":
                return range(GROUPS)
            return range(0, 1) if kind == "router" else range(1, 2) if part == 0 else range(2, GROUPS)

        def chunks(F):
            return [(c, min(P, F - c)) for c in range(0, F, P)]

        totals, at = {k: 0 for k in s}, []
        totals |= {"xin_pairs": 0, "y_pairs": 0}
        for kind, l, part in phases:
            at.append(dict(totals))
            if kind == "attention":
                units = TILES * ATT[l]["units"]
                for k in ("xn_ready", "xnT_psum", "xnT_sbuf"):
                    totals[k] += TILES
                if l != 2:
                    for k in ("qT_psum", "qT_sbuf", "out_psum", "out_inverted", "out_scaled", "outT_psum", "outT_sbuf"):
                        totals[k] += TILES
                for k in ("proj_psum", "x_new"):
                    totals[k] += TILES
                if l != 1:
                    for k in ("mean_var_done", "rstd_ready", "stats_done"):
                        totals[k] += TILES
                for k in ("scores_psum", "row_max_done", "probs_ready", "probsT_psum", "probsT_sbuf"):
                    totals[k] += units
                if l < 2:
                    totals["scores_shifted"] += units
                if l in (1, 2):
                    totals["scores_prep"] += units
                if l == 1:
                    totals["row_max_done"] += units
                if l == 2:
                    for k in ("probs_inverted", "probs_scaled"):
                        totals[k] += units
                    totals["mask2_copied"] += TILES
                if l == 3:
                    totals["rope_step"] += 2 * TILES
            if kind == "router":
                totals["xn_ready"] += TILES
                totals["xnT_psum"] += GROUPS
                totals["xnT_sbuf"] += GROUPS
                if l != 2:
                    totals["logits_psum"] += TILES
            if kind in ("shared", "dense") or (kind == "router" and l < 2):
                groups = len(group_range(kind, part))
                jobs = groups * len(chunks(FFN[l]["F"]))
                for k in ("up_psum", "hid_ready") + (("act_ready",) if kind != "dense" else ()):
                    totals[k] += jobs
                for k in ("y_psum", "x_new"):
                    totals[k] += groups
            if kind == "stats" or (kind == "keys" and l != 3):
                totals["mean_var_done"] += 1
            if kind == "dense":
                for k in ("mean_var_done", "rstd_ready"):
                    totals[k] += TILES
                totals["stats_done"] += TILES
            if kind == "routed":
                n = ROUTED_TILES[l] // UNIT[l]
                for k in ("xnT_psum", "xnT_sbuf", "weights_ready", "up_psum", "act_ready", "hid_ready", "y_psum", "y_taken"):
                    totals[k] += n
                totals["xin_pairs"] += n // 2
                totals["y_pairs"] += n // 2
        scatters_before, n_scat = {}, 0
        for l in (0, 1, 3):
            scatters_before[l] = n_scat
            n_scat += TILES

        up_w = {0: region_a[:, 0:9 * 1024], 1: region_b[:, 0:9 * 704], 3: region_b[:, 0:16 * 256]}
        down_w = {0: region_a[:, 9 * 1024:9 * 1536], 1: region_b[:, 9 * 704:9 * 1088], 3: region_b[:, 4096:4096 + 16 * 128]}
        xnT_all = keys[:, 0:TILES * P]
        hidT_all = region_c[:, 0:4096]
        up_now = [region_r[:, k * 1024:(k + 1) * 1024] for k in range(2)]
        wide = [region_c[:, k * 512:(k + 1) * 512] for k in range(6)]
        ffn_in = {0: xin, 1: xin, 3: wide[0:2]}
        ffn_inT = {0: xnT, 1: xnT, 3: wide[2:4]}
        ffn_out = {0: y_out, 1: y_out, 3: wide[4:6]}
        extra = {0: region_c[:, 0:2 * UW], 1: region_a[:, 6656:6656 + 2 * UW], 2: region_c[:, 0:2 * UW]}
        P_SLOTS = {l: [probs[0][:, :], probs[1][:, :], e[:, 0:UW], e[:, UW:2 * UW]] for l, e in extra.items()}
        P_SLOTS[3] = P_SLOTS[0][0:2]
        r_bf_parts = hidT[0][:, 0:3 * BK // 2].bitcast(bf16)
        values = {0: region_b, 1: region_a[:, 8192:12288], 3: region_a}
        vw_keys = region_a[0:SK, 0:B * 16 * D]
        vw = region_b[:, 0:B * 2 * NC * D]
        repeated = region_r[:, 0:B * UW]
        wkT2, wvT2 = region_a[:, 8192:9216], region_a[:, 9216:10240]
        wq2, woT2 = region_a[:, 10240:11264], region_a[:, 11264:12288]
        kT2, vT2 = region_c[:, 0:8 * BK], region_c[:, 8 * BK:16 * BK]
        bias1 = region_c

        def rows(name):
            return d[name].rearrange("(a n) -> a n", a=1)

        def expert_loads(l, shared_names, names):
            F, E = FFN[l]["F"], FFN[l]["E"]
            n = E + bool(shared_names)
            up = up_w[l].rearrange("p (e w f) -> p e w f", e=n, w=2)
            down = down_w[l].rearrange("p (e c o) -> p e c o", e=n, o=D)
            loads = [(up[:, 0:E, w, :], d[names[w]].rearrange("e p f -> p e f")) for w in range(2)]
            for c, (c0, cn) in enumerate(chunks(F)):
                loads.append((down[0:cn, 0:E, c, :], d[names[2]][:, c0:c0 + cn, :].rearrange("e p o -> p e o")))
            if shared_names:
                loads += [(up[:, E, w, :], d[shared_names[w]]) for w in range(2)]
                for c, (c0, cn) in enumerate(chunks(F)):
                    loads.append((down[0:cn, E, c, :], d[shared_names[2]][c0:c0 + cn, :]))
            return loads

        first_loads = [
            (ctxT[:, :], d["ctxT"]), (heads8[:, :], d["heads8"]),
            (row_head[:, :], d["row_head"]), (wk[:, :], d["L0_xattn_Wk"]),
            (wv[:, :], d["L0_xattn_Wv"]), (wo[:, :], d["L0_xattn_Wo"]),
            (cols[:, 1:2], d["L0_xattn_bk"].rearrange("(p a) -> p a", a=1)),
            (cols[:, 2:3], d["L0_xattn_bv"].rearrange("(p a) -> p a", a=1)), (brow[0:1, 0:D], rows("L0_xattn_bo")),
            (rel_T[:, :], d["rel_T"]), (bucket_hot, d["bucket_hot"])]
        second_loads = [
            (earlier_f[:, :], d["earlier"]), (gates_in[:, 0:4], rows("g_xattn").to_broadcast([P, 4])),
            (gates_in[:, 4:8], rows("g_ffn").to_broadcast([P, 4])),
            (ident[:, :], d["ident"]), (wq[:, :], d["L0_xattn_Wq"]), (heads16[:, :], d["heads16"]),
            (cols[:, 0:1], d["L0_xattn_bq"].rearrange("(p a) -> p a", a=1))]
        x_loads = [(x[:, g * 512:(g + 1) * 512].rearrange("p (t e) -> p t e", e=D),
                    d["x"][g * 512:(g + 1) * 512, :].rearrange("(t p) e -> p t e", p=P)) for g in range(GROUPS)]
        rest_loads = expert_loads(0, ("L0_ffn_w1s", "L0_ffn_w2s", "L0_ffn_w3s"), ("L0_ffn_W1", "L0_ffn_W2", "L0_ffn_W3"))
        rest_loads += [
            (half_head[:, :], d["half_head"]),
            (mask1_raw[:, :], d["mask1"]),
            (mask2[:, :].rearrange("p (t k) -> p t k", k=SK), d["mask2"].rearrange("(t p) k -> p t k", p=P)),
            (brow[0:1, 2 * D:3 * D], rows("L2_xattn_wOut_b")), (brow[0:1, 3 * D:4 * D], rows("L2_ffn_b_con")),
            (brow[0:1, 4 * D:5 * D], rows("L2_ffn_down_bias")),
            (colk2[:, 0:8], d["L2_xattn_wQ_b"].rearrange("(c p) -> p c", p=P)),
            (colk2[:, 8:16], d["L2_xattn_wK_b"].rearrange("(c p) -> p c", p=P)),
            (colk2[:, 16:24], d["L2_xattn_wV_b"].rearrange("(c p) -> p c", p=P))]
        def tables(E):
            n = CHOICE_TILES[3 if E == 16 else 0]
            t = [(rc[k][:, 0:TILES * E], d[f"{k}{E}"]) for k in ("rev", "step", "carry")] + [(slot_no[:, 0:n * E], d[f"slot{E}"])]
            return t + ([(digits[:, :], d["digits"])] if E == 16 else [])

        early_loads = {
            0: [(ctxT[:, :], d["ctxT_backwards"]), (wk[:, :], d["L1_xattn_WkT"]), (wv[:, :], d["L1_xattn_WvT"]),
                (router_w[:, 0:8], d["L0_ffn_Wg"])] + tables(8),
            1: [(ctxT[:, :], d["ctxT"]), (router_w[:, 0:8], d["L1_ffn_router_DE"])],
            2: [(wk[:, :], d["L3_xattn_WkT"]), (wv[:, :], d["L3_xattn_WvT"]), (wks[:, :], d["L3_xattn_WkT_swapped"])],
            3: [(router_w[:, :], d["L3_ffn_router_w"])] + tables(16)}
        late_loads = {
            0: [(wq[:, :], d["L1_xattn_WqT"]), (wo[:, :], d["L1_xattn_WoT"])],
            1: [(wkT2, d["L2_xattn_WkT"]), (wvT2, d["L2_xattn_WvT"]),
                (wq2.rearrange("p (c e) -> p c e", e=D), d["L2_xattn_wQ_w"].rearrange("(c p) e -> p c e", p=P)),
                (woT2.rearrange("p (c e) -> p c e", e=D), d["L2_xattn_WoT"].rearrange("(c p) e -> p c e", p=P))],
            2: [(wq[:, :], d["L3_xattn_WqT"]), (wo[:, :], d["L3_xattn_WoT"]), (wqs[:, :], d["L3_xattn_WqT_swapped"])],
            3: []}
        next_experts = {
            0: expert_loads(1, ("L1_ffn_ws1_DF", "L1_ffn_ws3_DF", "L1_ffn_ws2_FD"),
                            ("L1_ffn_w1_eDF", "L1_ffn_w3_eDF", "L1_ffn_w2_eFD")),
            1: [], 2: expert_loads(3, None, ("L3_ffn_gate_w", "L3_ffn_up_w", "L3_ffn_down_w")), 3: []}

        VJ = B
        KV = {0: dict(kv_psum=0, kv_evac_v=0)}
        KV[1] = dict(kv_psum=1 + VJ, kv_evac_v=0)
        KV[2] = dict(kv_psum=2 * (1 + VJ), kv_evac_v=0)
        KV[3] = dict(kv_psum=2 * (1 + VJ) + 16 + 1 + 16 + B * 4, kv_evac_v=16 + 1 + B * 4)
        HOTS = {0: 0, 1: 1, 3: 2}

        def logits_at(l):
            return bank(4 if l < 2 else 0, 0, TILES * FFN[l]["E"])

        def ranks_at(l, c, whole):
            W = TILES * FFN[l]["E"]
            return bank(4, (1 + whole) * W, (2 + whole) * W) if l < 2 else bank(1 + 2 * c + whole, 0, W)

        V_TAKEN = {0: 0, 1: VJ, 3: 2 * VJ}
        REPEATED = {0: 0, 1: 1, 3: 2}
        down_T = region_a[:, 0:HID]

        block = ctx.enter_context(nc.Block())

        def experts_of(eng, l, t):
            E, U = FFN[l]["E"], UNIT[l]
            word = eng.value_load(expert_of[0:1, ds(t, 1)], min_val=0, max_val=E ** U - 1)
            return [(word // E ** i) % E if U > 1 else word for i in range(U)]

        def hidden_parts(l):
            cs, U = chunks(FFN[l]["F"]), UNIT[l]
            whole = U * sum(cn == P for _, cn in cs) * P
            return [(P, 0, whole)] + ([(cs[-1][1], whole, whole + P)] if cs[-1][1] < P else [])

        @block.sync
        def _(sp):
            for dst, src in first_loads:
                sp.dma_start(dst, src).then_inc(s["loaded_first"], 16)
            for dst, src in x_loads:
                sp.dma_start(dst, src).then_inc(s["x_loaded"], 16)
            for dst, src in second_loads:
                sp.dma_start(dst, src).then_inc(s["loaded_second"], 16)
            sp.wait_ge(s["zeros_set"], 1)
            for c in range(2):
                sp.dma_start(sorted_in[c].rearrange("(t p) e -> p t e", p=P),
                             zeros[:, :].rearrange("p (a e) -> p a e", a=1).to_broadcast([P, CHOICE_TILES[3], D]))\
                    .then_inc(s["slots_zeroed"], 16)

            reloads = experts = 0
            for no, (kind, l, sub) in enumerate(phases):
                z = at[no]
                if kind == "load":
                    sp.wait_ge(s["loaded_first"], 16 * len(first_loads))
                if kind == "keys" and l == 0:
                    for dst, src in rest_loads:
                        sp.dma_start(dst, src).then_inc(s["loaded_rest"], 16)
                    sp.wait_ge(s["x_loaded"], 16 * len(x_loads))
                    sp.wait_ge(s["rel_evac"], 2)
                    sp.dma_start(rel_dram.ap(), rel_by_delta).then_inc(s["rel_stored"], 16)
                if kind == "attention":
                    for dst, src in early_loads[l]:
                        sp.dma_start(dst, src).then_inc(s["reloaded"], 16)
                    reloads += len(early_loads[l])
                    sp.wait_ge(s["reloaded"], 16 * reloads)
                    if l == 0:
                        sp.wait_ge(s["loaded_rest"], 16 * len(rest_loads))
                    else:
                        sp.wait_ge(s["experts_loaded"], 16 * experts)
                if kind == "router":
                    for dst, src in late_loads[l]:
                        sp.dma_start(dst, src).then_inc(s["reloaded"], 16)
                    for dst, src in next_experts[l]:
                        sp.dma_start(dst, src).then_inc(s["experts_loaded"], 16)
                    reloads += len(late_loads[l])
                    experts += len(next_experts[l])
                if (kind == "shared" and sub == 1) or kind == "dense":
                    sp.wait_ge(s["reloaded"], 16 * reloads)
                if kind == "dense":
                    for dst, src in ((rope_cos, d["rope_cos"]), (rope_sin, d["rope_sin"])):
                        sp.dma_start(dst, src).then_inc(s["tables_loaded"], 16)
                    sp.wait_ge(s["tables_loaded"], 32)
                if kind == "keys" and l == 1:
                    sp.wait_ge(s["rel_stored"], 16)
                    for q in range(QT):
                        if q == QT - 1:
                            sp.wait_ge(s["down_moved"], 1)
                        src = bass.AP(rel_dram, q * P, [[1, P], [DELTAS, 16], [1, SK]])
                        sp.dma_start(bias1[:, q * 16 * SK:(q + 1) * 16 * SK].rearrange("p (h k) -> p h k", k=SK), src)\
                            .then_inc(s["bias_loaded" if q else "bias_first"], 16)
                    sp.wait_ge(s["bias_first"], 16)
                if kind == "keys" and l == 2:
                    sp.wait_ge(s["q_bias_parts"], 1)
                    for part in range(3):
                        for b in range(B):
                            at_b = part * BK + b * SK
                            sp.dma_start(q_bias[part:part + 1, b * 16 * SK:(b + 1) * 16 * SK].rearrange("p (h k) -> p h k", k=SK),
                                         r_bf_parts[0:16, at_b:at_b + SK]).then_inc(s["q_bias_loaded"], 16)
                    for b in range(B):
                        sp.wait_ge(s["kv_evac_v"], KV[2]["kv_evac_v"] + 17 + 4 * (b + 1))
                        sp.dma_start(vw_dram[b].rearrange("u (h k) e -> k u h e", k=SK),
                                     vw_keys.rearrange("p (b u h e) -> p b u h e", b=B, u=2, e=D)[:, b, :, :, :]).then_inc(s["vw_stored"], 16)
                    sp.wait_ge(s["vw_stored"], 16 * B)
                    sp.wait_ge(s["vw_zeroed"], 1)
                    vw5 = vw.rearrange("p (b u c e) -> p b u c e", b=B, u=2, e=D)
                    for b in range(B):
                        for u in range(2):
                            sp.dma_start(vw5[:, b, u, 0:NC - 1, :], vw_dram[b, u, 0:(NC - 1) * P, :].rearrange("(c p) e -> p c e", p=P))\
                                .then_inc(s["vw_loaded"], 16)
                        sp.dma_start(vw5[P - (UW - (NC - 1) * P):P, b, :, NC - 1, :], vw_dram[b, :, (NC - 1) * P:UW, :].rearrange("u p e -> p u e"))\
                            .then_inc(s["vw_loaded"], 16)
                    sp.wait_ge(s["q_bias_loaded"], 16 * 3 * B)
                if kind == "routed":
                    U = UNIT[l]
                    n = ROUTED_TILES[l] // U
                    if l == 0:
                        sp.wait_ge(s["slots_zeroed"], 32)
                    sp.wait_ge(s["scattered"], 16 * (scatters_before[l] + TILES))

                    def sorted_rows(choices, t):
                        second = len(choices) > 1 and not (isinstance(t, int) and t < n // 2)
                        t = t - n // 2 if second else t
                        return choices[int(second)][ds(t * (U * P), U * P), :].rearrange("(a p) e -> p a e", p=P)

                    def load(i, k):
                        sp.dma_start(ffn_in[l][k][:, :].rearrange("p (a e) -> p a e", e=D), sorted_rows(sorted_in[0:CHOICES[l]], 2 * i + k))\
                            .then_inc(xin_loaded[k], 16)

                    def store(t, k):
                        sp.wait_ge(s["y_taken"], z["y_taken"] + t + 1)
                        sp.dma_start(sorted_rows(sorted_out[l], t), ffn_out[l][k][:, :].rearrange("p (a e) -> p a e", e=D))\
                            .then_inc(y_stored[k], 16)

                    for k in range(2):
                        load(0, k)

                    def body(i):
                        for k in range(2):
                            t = 2 * i + k
                            if exists(t + 2, n):
                                if l == 3 and isinstance(i, int) and t + 2 == n // 2:
                                    sp.wait_ge(s["scattered_second"], 16 * TILES)
                                sp.wait_ge(s["xnT_psum"], z["xnT_psum"] + t + 1)
                                load(i + 1, k)
                            if exists(t - 2, n):
                                store(t - 2, k)
                    pairs(sp, n // 2, body, n // 4 + 1 if l == 3 else 1)
                    for k in range(2):
                        store(n - 2 + k, k)
                if kind == "combine":
                    for g in range(GROUPS):
                        sp.wait_ge(s["combined"], g + 1)
                        sp.dma_start(out[g * 512:(g + 1) * 512, :].rearrange("(t p) e -> p t e", p=P),
                                     x[:, g * 512:(g + 1) * 512].rearrange("p (t e) -> p t e", e=D)).then_inc(s["stored"], 16)
                phase_end(sp, no + 1)
            sp.wait_ge(s["stored"], 16 * GROUPS)

        def scores(k):
            two = psum[:, 2 * k * BANK:(2 * k + 2) * BANK].rearrange("p (a c) -> p a c", a=2)
            return two[:, :, 0:UW // 2].rearrange("p a (h k) -> p a h k", k=SK)

        def by_head(ap):
            return ap.rearrange("p (a h k) -> p a h k", a=2, k=SK)

        def over_keys(ap):
            return ap.rearrange("p (a h o) -> p a h o", a=2, o=1).to_broadcast([P, 2, HG // 2, SK])

        HD = {0: 8, 1: 8, 3: 16}
        TRANSPOSED = 4 * BANK
        OUT, MIX = 6, 7

        @block.tensor
        def _(pe):
            mm, tr = nc.tensor.matmul, nc.tensor.transpose

            def keys_phase(l, z):
                if l == 2:
                    return keys_phase2(z)
                mm(bank(0, 0, BK), wk[:, :], ctxT[:, :], start=True, stop=True).then_inc(s["kv_psum"], 1)
                if l == 3:
                    mm(bank(1, 0, BK), wks[:, :], ctxT[:, :], start=True, stop=True).then_inc(s["kv_psum"], 1)
                pe.wait_ge(s["repeated"], REPEATED[l] + 1)
                for b in range(B):
                    if b >= 2:
                        pe.wait_ge(s["v_taken"], V_TAKEN[l] + b - 1)
                    for c in range(NC):
                        o = 2 * BANK + (b % 2) * 2 * BANK + c * D
                        last = mm(psum[:, o:o + D], repeated[:, b * UW + CHUNKS[c]:b * UW + CHUNKS[c] + P], wv[:, :], start=True, stop=True)
                    last.then_inc(s["kv_psum"], 1)
                if l == 0:
                    mm(bank(1, 0, D, parts=1), cols[:, 2:3], wo[:, :], start=True, stop=False)
                    mm(bank(1, 0, D, parts=1), ones_row[0:1, 0:1], brow[0:1, 0:D], start=False, stop=True).then_inc(s["rel_psum"], 1)
                if l == 0:
                    mm(bank(6, 0, BANK, parts=16), rel_T[:, :], bucket_hot[:, 0:BANK], start=True, stop=True).then_inc(s["rel_psum"], 1)
                    mm(bank(7, 0, DELTAS - BANK, parts=16), rel_T[:, :], bucket_hot[:, BANK:DELTAS], start=True, stop=True)\
                        .then_inc(s["rel_psum"], 1)

            def keys_phase2(z):
                for j in range(16):
                    if j >= 8:
                        pe.wait_ge(s["kv_evac_v"], z["kv_evac_v"] + j - 8 + 1)
                    w, c = (wkT2, j) if j < 8 else (wvT2, j - 8)
                    mm(bank(j % 8, 0, BK), w[:, c * P:(c + 1) * P], ctxT[:, :], start=True, stop=True).then_inc(s["kv_psum"], 1)
                pe.wait_ge(s["kv_evac_v"], z["kv_evac_v"] + 17)
                for c in range(8):
                    last = mm(bank(0, 0, BK, parts=16), hid[1][:, c * 16:(c + 1) * 16], kT2[:, c * BK:(c + 1) * BK], start=c == 0, stop=c == 7)
                last.then_inc(s["kv_psum"], 1)
                pe.wait_ge(s["kv_evac_a"], 1)
                for j in range(B * 4):
                    if j >= 8:
                        pe.wait_ge(s["kv_evac_v"], z["kv_evac_v"] + 17 + j - 8 + 1)
                    b, g = j // 4, j % 4
                    for i in range(4):
                        h = 8 * (g // 2) + 2 * i + g % 2
                        rows_h = slice(64 * (h % 2), 64 * (h % 2) + 64)
                        last = mm(bank(j % 8, i * D, (i + 1) * D, parts=SK),
                                  vT2[rows_h, (h // 2) * BK + b * SK:(h // 2) * BK + (b + 1) * SK],
                                  woT2[rows_h, (h // 2) * P:(h // 2 + 1) * P], start=True, stop=True)
                    last.then_inc(s["kv_psum"], 1)
                for h in range(16):
                    rows_h = slice(64 * (h % 2), 64 * (h % 2) + 64)
                    k_h = kT2[rows_h, (h // 2) * BK:(h // 2 + 1) * BK]
                    if h >= 6:
                        pe.wait_ge(s["kv_evac_a"], h - 4)
                    else:
                        pe.wait_ge(s["kv_evac_v"], z["kv_evac_v"] + 17 + 10 + h + 1)
                    mm(bank(2 + h % 6, 0, BK), wq2[rows_h, (h // 2) * P:(h // 2 + 1) * P], k_h, start=True, stop=True)\
                        .then_inc(s["kv_psum"], 1)

            def attention_phase(l, z):
                units = ATT[l]["units"]

                def normalised(t, k):
                    pe.wait_ge(s["xn_ready"], z["xn_ready"] + t + 1)
                    tr(bank(MIX, 0, D), xin[k][:, :], ident[:, :]).then_inc(s["xnT_psum"], 1)

                def queries(t, k):
                    if l == 2:
                        return
                    pe.wait_ge(s["xnT_sbuf"], z["xnT_sbuf"] + t + 1)
                    last = mm(bank(MIX, D, 2 * D), wq[:, :], xnT[k][:, :], start=True, stop=True)
                    if l == 3:
                        last = mm(bank(MIX, 2 * D, 3 * D), wqs[:, :], xnT[k][:, :], start=True, stop=True)
                    last.then_inc(s["qT_psum"], 1)

                def score(t, h, k, kt, first_two):
                    u = t * units + h
                    if l == 2:
                        pe.wait_ge(s["xnT_sbuf"], z["xnT_sbuf"] + t + 1)
                    else:
                        pe.wait_ge(s["qT_sbuf"], z["qT_sbuf"] + t + 1)
                    if not first_two:
                        read = "probs_ready" if l >= 2 else "scores_shifted"
                        pe.wait_ge(s[read], z[read] + u - 1)
                    q = (xnT if l == 2 else qT)[kt]
                    b = t // QT
                    for half in range(2):
                        o = bank(2 * k + half, 0, UW // 2)
                        at_k = b * (units * UW) + h * UW + half * (UW // 2)
                        last = mm(o, q[:, :], keys[:, ds(at_k, UW // 2)], start=True, stop=l in (0, 3))
                        if l == 1:
                            last = mm(o, ones_bf[0:1, :], mask1_row[0:1, ds(b * SK, SK)].rearrange("p (a k) -> p a k", a=1)
                                      .to_broadcast([1, HG // 2, SK]), start=False, stop=True)
                        if l == 2:
                            last = mm(o, ones_bf[0:3, :], q_bias[:, ds(at_k, UW // 2)], start=False, stop=True)
                    last.then_inc(s["scores_psum"], 1)

                def transpose_probs(t, h, k, very_first):
                    u = t * units + h
                    ready = "probs_scaled" if l == 2 else "probs_ready"
                    pe.wait_ge(s[ready], z[ready] + u + 1)
                    if not very_first:
                        pe.wait_ge(s["probsT_sbuf"], z["probsT_sbuf"] + u)
                    for i, c in enumerate(CHUNKS):
                        last = tr(psum[:, TRANSPOSED + i * P:TRANSPOSED + (i + 1) * P], P_SLOTS[l][k][:, c:c + P], ident[:, :])
                    last.then_inc(s["probsT_psum"], 1)

                def attend(t, h, k, first_tile):
                    u = t * units + h
                    pe.wait_ge(s["probsT_sbuf"], z["probsT_sbuf"] + u + 1)
                    b = t // QT
                    if h == 0 and not first_tile:
                        if l == 2:
                            pe.wait_ge(s["x_new"], z["x_new"] + t)
                        else:
                            pe.wait_ge(s["out_scaled"], z["out_scaled"] + t)
                    if l == 2 and h == 0 and first_tile:
                        pe.wait_ge(s["vw_loaded"], 16 * 3 * B)
                    if l == 2 and h == 0:
                        mm(bank(OUT, 0, D), ones_row[0:1, :], brow[0:1, 2 * D:3 * D], start=True, stop=False)
                    for i in range(NC):
                        pT = probsT[k][:, i * P:(i + 1) * P]
                        if l == 2:
                            last = mm(bank(OUT, 0, D), pT, vw[:, ds(b * (2 * NC * D) + (h * NC + i) * D, D)],
                                      start=False, stop=h == 1 and i == NC - 1)
                        else:
                            w = HG * (HD[l] + 1)
                            last = mm(bank(OUT, h * w, (h + 1) * w), pT, values[l][:, ds(b * (units * NC * w) + (h * NC + i) * w, w)],
                                      start=i == 0, stop=i == NC - 1)
                    if h == units - 1:
                        last.then_inc(s["proj_psum" if l == 2 else "out_psum"], 1)

                def out_transpose(t, k):
                    pe.wait_ge(s["out_scaled"], z["out_scaled"] + t + 1)
                    tr(bank(MIX, 3 * D, 4 * D) if l == 3 else bank(MIX, 2 * D, 3 * D), out_n[k][:, :], ident[:, :]).then_inc(s["outT_psum"], 1)

                def project(t):
                    pe.wait_ge(s["outT_sbuf"], z["outT_sbuf"] + t + 1)
                    o = bank(OUT, 256, 256 + D) if l == 3 else bank(MIX, 0, D)
                    if l == 3:
                        pe.wait_ge(s["out_scaled"], z["out_scaled"] + (t + 2 if exists(t + 1, TILES) else t + 1))
                    if l == 0:
                        mm(o, ones_row[0:1, :], brow[0:1, D:2 * D], start=True, stop=False)
                    mm(o, outT[:, :], wo[:, :], start=l != 0, stop=True).then_inc(s["proj_psum"], 1)

                def new_x_read(t):
                    if l != 2 and exists(t, TILES):
                        pe.wait_ge(s["x_new"], z["x_new"] + t + 1)

                def queries_read(t):
                    if l != 2:
                        pe.wait_ge(s["qT_sbuf"], z["qT_sbuf"] + t + 1)

                for t in range(2):
                    normalised(t, t)
                    queries(t, t)
                    if l == 2:
                        pe.wait_ge(s["xnT_sbuf"], z["xnT_sbuf"] + t + 1)
                    queries_read(t)
                if l == 3:
                    normalised(2, 0)
                    score(0, 0, 0, 0, True)
                    score(1, 0, 1, 1, True)
                else:
                    score(0, 0, 0, 0, True)
                    score(0, 1, 1, 0, True)
                    score(1, 0, 0, 1, False)

                def body(i):
                    for k in range(2):
                        t = 2 * i + k
                        start = isinstance(t, int) and t == 0
                        if l == 3:
                            transpose_probs(t, 0, k, start)
                            if exists(t + 2, TILES):
                                queries(t + 2, k)
                            if exists(t - 1, TILES):
                                if exists(t - 3, TILES):
                                    new_x_read(t - 3)
                                attend(t - 1, 0, 1 - k, isinstance(t, int) and t == 1)
                            if exists(t - 2, TILES):
                                if exists(t + 2, TILES):
                                    queries_read(t + 2)
                                out_transpose(t - 2, k)
                            if exists(t + 2, TILES):
                                score(t + 2, 0, k, k, False)
                            if exists(t + 3, TILES):
                                if exists(t - 2, TILES):
                                    pe.wait_ge(s["outT_sbuf"], z["outT_sbuf"] + t - 1)
                                else:
                                    queries_read(t + 2)
                                normalised(t + 3, 1 - k)
                            if exists(t - 2, TILES):
                                project(t - 2)
                        else:
                            p = 2 * k
                            transpose_probs(t, 0, p, start)
                            if exists(t + 2, TILES):
                                if exists(t - 2, TILES):
                                    new_x_read(t - 2)
                                normalised(t + 2, k)
                            if exists(t - 1, TILES):
                                attend(t - 1, 1, 1, False)
                            if exists(t + 2, TILES):
                                queries(t + 2, k)
                            if exists(t + 1, TILES):
                                score(t + 1, 1, 1, 1 - k, False)
                            transpose_probs(t, 1, p + 1, False)
                            if l != 2 and exists(t - 1, TILES):
                                if exists(t + 2, TILES):
                                    queries_read(t + 2)
                                else:
                                    new_x_read(t - 2)
                                out_transpose(t - 1, 1 - k)
                            attend(t, 0, 0, start)
                            if l != 2 and exists(t - 1, TILES):
                                project(t - 1)
                            if exists(t + 2, TILES):
                                score(t + 2, 0, 0, k, False)
                pairs(pe, TILES // 2, body, 2, 2)
                last = TILES - 1
                if l == 3:
                    new_x_read(last - 2)
                    attend(last, 0, 1, False)
                    for t in (last - 1, last):
                        out_transpose(t, t % 2)
                        if t == last:
                            new_x_read(last - 1)
                        project(t)
                else:
                    attend(last, 1, 1, False)
                    if l != 2:
                        new_x_read(last - 1)
                        out_transpose(last, 1)
                        project(last)

            def router_phase(l, z):
                E = FFN[l]["E"]
                for g in range(GROUPS):
                    if g >= 2:
                        pe.wait_ge(s["xnT_sbuf"], z["xnT_sbuf"] + g - 1)
                    for i in range(4):
                        t = 4 * g + i
                        pe.wait_ge(s["xn_ready"], z["xn_ready"] + t + 1)
                        last = tr(bank(6 + g % 2, i * P, (i + 1) * P), xn_all[:, t * D:(t + 1) * D], ident[:, :])
                    last.then_inc(s["xnT_psum"], 1)
                if l == 2:
                    return
                for t in range(TILES):
                    pe.wait_ge(s["xnT_sbuf"], z["xnT_sbuf"] + t // 4 + 1)
                    mm(logits_at(l)[:, t * E:(t + 1) * E], xnT_all[:, t * P:(t + 1) * P], router_w[:, 0:E], start=True, stop=True)\
                        .then_inc(s["logits_psum"], 1)
                if l < 2:
                    up, down = shared_steps("router", 0, l, z)
                    up(0, 0)
                for c in range(CHOICES[l]):
                    pe.wait_ge(s["hots_ready"], HOTS[l] + c + 1)
                    mm(ranks_at(l, c, False), earlier[:, :], r_bf[c][:, 0:TILES * E], start=True, stop=True)
                    mm(ranks_at(l, c, True), ones_bf[:, :], r_bf[c][:, 0:TILES * E], start=True, stop=True)\
                        .then_inc(s["rank_psum"], 1)
                if l < 2:
                    for c in range(1, len(chunks(FFN[l]["F"]))):
                        up(0, c)
                    down(0)

            def shared_steps(kind, part, l, z):
                F, E = FFN[l]["F"], FFN[l]["E"]
                cs = chunks(F)
                C = len(cs)
                groups = group_range(kind, part)

                def up(g, c):
                    j = (g - groups[0]) * C + c
                    c0, cn = cs[c]
                    if j >= 2:
                        pe.wait_ge(s["hid_ready"], z["hid_ready"] + j - 1)
                    tokens = xnT_all[:, g * 512:(g + 1) * 512]
                    if kind == "dense":
                        last = mm(bank(j % 2), up_fold[:, c0:c0 + cn], tokens, start=True, stop=True)
                    else:
                        at_w = E * 2 * F + c0
                        mm(bank(j % 2, parts=cn), up_w[l][:, at_w:at_w + cn], tokens, start=True, stop=True)
                        last = mm(bank(2 + j % 2, parts=cn), up_w[l][:, at_w + F:at_w + F + cn], tokens, start=True, stop=True)
                    last.then_inc(s["up_psum"], 1)

                def down(g):
                    n = g - groups[0]
                    pe.wait_ge(s["hid_ready"], z["hid_ready"] + (n + 1) * C)
                    if n >= 2:
                        pe.wait_ge(s["x_new"], z["x_new"] + n - 1)
                    for i in range(4):
                        o = bank(6 + n % 2, i * D, (i + 1) * D)
                        if kind == "dense":
                            mm(o, ones_row[0:1, :], brow[0:1, 3 * D:4 * D], start=True, stop=False)
                        for c, (c0, cn) in enumerate(cs):
                            w = down_fold[:, c * D:(c + 1) * D] if kind == "dense" else \
                                down_w[l][0:cn, (E * C + c) * D:(E * C + c + 1) * D]
                            h = ((n % 2) * C + c) * 512 + i * P
                            last = mm(o, hidT_all[0:cn, h:h + P], w, start=c == 0 and kind != "dense", stop=c == C - 1)
                    last.then_inc(s["y_psum"], 1)

                return up, down

            def shared_phase(kind, part, l, z):
                up, down = shared_steps(kind, part, l, z)
                groups = group_range(kind, part)
                for g in groups:
                    for c in range(len(chunks(FFN[l]["F"]))):
                        up(g, c)
                        if c == 1 and g > groups[0]:
                            down(g - 1)
                down(groups[-1])

            def routed_phase(l, z):
                F, U = FFN[l]["F"], UNIT[l]
                n = ROUTED_TILES[l] // U
                C = len(chunks(F))
                x_in, x_T = ffn_in[l], ffn_inT[l]

                def normalised(t, k, first):
                    pe.wait_ge(xin_loaded[k], 16 * (z["xin_pairs"] + (t - k) // 2 + 1) if isinstance(t, int)
                               else 16 * (z["xin_pairs"] + 1) + (t - k) * 8)
                    if not first:
                        pe.wait_ge(s["xnT_sbuf"], z["xnT_sbuf"] + t)
                    for i in range(U):
                        last = tr(bank(7, i * D, (i + 1) * D), x_in[k][:, i * D:(i + 1) * D], ident[:, :])
                    last.then_inc(s["xnT_psum"], 1)

                def up(t, k, first_two):
                    pe.wait_ge(s["xnT_sbuf"], z["xnT_sbuf"] + t + 1)
                    pe.wait_ge(s["weights_ready"], z["weights_ready"] + t + 1)
                    if not first_two:
                        pe.wait_ge(s["hid_ready"], z["hid_ready"] + t - 1)
                    for i in range(U):
                        for w in range(2):
                            for c, (c0, cn) in enumerate(chunks(F)):
                                last = mm(bank(2 * w + k, (i * C + c) * P, (i * C + c + 1) * P, parts=cn),
                                          up_now[k][:, (2 * i + w) * F + c0:(2 * i + w) * F + c0 + cn], x_T[k][:, i * D:(i + 1) * D], start=True, stop=True)
                    last.then_inc(s["up_psum"], 1)

                def down(t, k, es, first):
                    pe.wait_ge(s["hid_ready"], z["hid_ready"] + t + 1)
                    if not first:
                        pe.wait_ge(s["y_taken"], z["y_taken"] + t)
                    for i, e in enumerate(es):
                        for c, (c0, cn) in enumerate(chunks(F)):
                            last = mm(bank(6, i * D, (i + 1) * D), hid[k][0:cn, (i * C + c) * P:(i * C + c + 1) * P],
                                      down_w[l][0:cn, ds(e * (C * D) + c * D, D)], start=c == 0, stop=c == C - 1)
                    last.then_inc(s["y_psum"], 1)

                normalised(0, 0, True)
                normalised(1, 1, False)
                up(0, 0, True)

                def body(i):
                    start = isinstance(i, int) and i == 0
                    for k in range(2):
                        t = 2 * i + k
                        es = experts_of(pe, l, t)
                        if exists(t + 2, n):
                            normalised(t + 2, k, False)
                        if exists(t + 1, n):
                            up(t + 1, 1 - k, start and k == 0)
                        down(t, k, es, start and k == 0)
                pairs(pe, n // 2, body)

            for no, (kind, l, sub) in enumerate(phases):
                z = at[no]
                if kind == "keys":
                    keys_phase(l, KV[l])
                elif kind == "attention":
                    attention_phase(l, z)
                elif kind == "router":
                    router_phase(l, z)
                elif kind in ("shared", "dense"):
                    shared_phase(kind, sub, l, z)
                elif kind == "routed":
                    routed_phase(l, z)
                elif kind == "stats":
                    for c in range(4):
                        tr(bank(0, c * P, (c + 1) * P), down_T[:, c * P:(c + 1) * P], ident[:, :])
                        last = tr(bank(1, c * P, (c + 1) * P), up_fold[:, HID + c * P:HID + (c + 1) * P], ident[:, :])
                    last.then_inc(s["fold_psum"], 1)
                phase_end(pe, no + 1)

        @block.scalar
        def _(act):
            run = nc.scalar.activation

            def keys_phase(l, z):
                if l == 2:
                    act.wait_ge(s["kv_psum"], z["kv_psum"] + 17)
                    run(hid[0][0:16, 0:BK], bank(0, 0, BK, parts=16), ACT.Copy, scale=0.125).then_inc(s["kv_evac_a"], 1)
                    for h in range(16):
                        act.wait_ge(s["kv_psum"], z["kv_psum"] + 33 + h + 1)
                        run(keys[:, :].rearrange("p (b h k) -> p b h k", b=B, k=SK)[:, :, h, :],
                            bank(2 + h % 6, 0, BK).rearrange("p (b k) -> p b k", k=SK), ACT.Copy, scale=0.125).then_inc(s["kv_evac_a"], 1)
                    return
                run(repeated.rearrange("p (b h k) -> p b h k", b=B, k=SK),
                    ctxT[:, :].rearrange("p (b h k) -> p b h k", b=B, h=1).to_broadcast([P, B, HG, SK]), ACT.Copy).then_inc(s["repeated"], 1)
                hd = HD[l]
                v = values[l][:, 0:B * ATT[l]["units"] * NC * HG * (hd + 1)].rearrange("p (b c h w) -> p b c h w", b=B, h=HG, w=hd + 1)
                for b in range(B):
                    run(v[:, b, :, :, hd].rearrange("p (u c) h -> p u c h", c=NC),
                        row_head[:, :].rearrange("p (u c h) -> p u c h", u=1, h=HG).to_broadcast([P, ATT[l]["units"], NC, HG]), ACT.Copy)
                act.wait_ge(s["kT_ready"], REPEATED[l] + 1)
                n, sel = (8, heads16) if l == 3 else (16, heads8)
                for h in range(n):
                    run(keys[:, 0:B * n * SK].rearrange("p (b h k) -> p b h k", b=B, k=SK)[:, B // 2:, h, :],
                        kT[:, B // 2 * SK:].rearrange("p (b k) -> p b k", k=SK), ACT.Copy, scale=sel[:, h:h + 1])
                if l == 0:
                    act.wait_ge(s["rel_psum"], 3)
                    act.wait_ge(s["loaded_second"], 16 * len(second_loads))
                    run(tanh_g[:, :], gates_in[:, :], ACT.Tanh)
                    run(brow[0:1, D:2 * D], bank(1, 0, D, parts=1), ACT.Copy)
                    run(rel_by_delta[:, 0:BANK], bank(6, 0, BANK, parts=16), ACT.Copy).then_inc(s["rel_evac"], 1)
                    run(rel_by_delta[:, BANK:DELTAS], bank(7, 0, DELTAS - BANK, parts=16), ACT.Copy).then_inc(s["rel_evac"], 1)

            def attention_phase(l, z):
                units = ATT[l]["units"]

                def normalised(t, k):
                    act.wait_ge(s["xnT_psum"], z["xnT_psum"] + t + 1)
                    run(xnT[k][:, :], bank(MIX, 0, D), ACT.Copy).then_inc(s["xnT_sbuf"], 1)

                def queries(t, k):
                    if l in (2, 3):
                        return
                    act.wait_ge(s["qT_psum"], z["qT_psum"] + t + 1)
                    if l == 0:
                        run(qT[k][:, :], bank(MIX, D, 2 * D), ACT.Identity, bias=cols[:, 0:1]).then_inc(s["qT_sbuf"], 1)
                    else:
                        run(qT[k][:, :], bank(MIX, D, 2 * D), ACT.Copy).then_inc(s["qT_sbuf"], 1)

                def exps(t, h, k):
                    if l < 2:
                        act.wait_ge(s["scores_shifted"], z["scores_shifted"] + t * units + h + 1)
                        run(P_SLOTS[l][k], P_SLOTS[l][k], ACT.Exp).then_inc(s["probs_ready"], 1)
                        return
                    act.wait_ge(s["row_max_done"], z["row_max_done"] + t * units + h + 1)
                    if not (isinstance(t, int) and t < 2):
                        act.wait_ge(s["probsT_psum"], z["probsT_psum"] + t * units + h - len(P_SLOTS[l]) + 1)
                    for i in range(HG):
                        sums = {"accum_out": row_sum[k][:, i:i + 1]} if l == 2 else {}
                        last = run(P_SLOTS[l][k][:, i * SK:(i + 1) * SK], bank(2 * (k % 2) + i // 4, (i % 4) * SK, (i % 4 + 1) * SK), ACT.Exp,
                                   bias=row_max[k][:, i:i + 1], **sums)
                    last.then_inc(s["probs_ready"], 1)

                def probs_copy(t, h, k):
                    act.wait_ge(s["probsT_psum"], z["probsT_psum"] + t * units + h + 1)
                    run(probsT[k][:, :], psum[:, TRANSPOSED:TRANSPOSED + TW], ACT.Copy).then_inc(s["probsT_sbuf"], 1)

                def out_copy(t):
                    act.wait_ge(s["outT_psum"], z["outT_psum"] + t + 1)
                    run(outT[:, :], bank(MIX, 3 * D, 4 * D) if l == 3 else bank(MIX, 2 * D, 3 * D), ACT.Copy).then_inc(s["outT_sbuf"], 1)

                for t in range(2):
                    normalised(t, t)
                    queries(t, t)
                if l == 3:
                    normalised(2, 0)
                exps(0, 0, 0)
                if l != 3:
                    exps(0, 1, 1)

                def body(i):
                    for k in range(2):
                        t = 2 * i + k
                        if l == 3:
                            probs_copy(t, 0, k)
                            if exists(t + 1, TILES):
                                exps(t + 1, 0, 1 - k)
                            if exists(t - 2, TILES):
                                out_copy(t - 2)
                            if exists(t + 3, TILES):
                                normalised(t + 3, 1 - k)
                        else:
                            probs_copy(t, 0, 0)
                            if exists(t + 2, TILES):
                                normalised(t + 2, k)
                            if exists(t + 1, TILES):
                                exps(t + 1, 0, 2 - 2 * k)
                            if exists(t + 2, TILES):
                                queries(t + 2, k)
                            probs_copy(t, 1, 1)
                            if l != 2 and exists(t - 1, TILES):
                                out_copy(t - 1)
                            if exists(t + 1, TILES):
                                exps(t + 1, 1, 3 - 2 * k)
                pairs(act, TILES // 2, body, 2, 2)
                if l == 3:
                    out_copy(TILES - 2)
                if l != 2:
                    out_copy(TILES - 1)

            def gate(l):
                act.wait_ge(s["hots_ready"], HOTS[l] + 1)
                run(r_m["kp"][:, :], r_m["m1"][:, :], ACT.Sigmoid).then_inc(s["gate_ready"], 1)

            def router_phase(l, z):
                for g in range(GROUPS):
                    act.wait_ge(s["xnT_psum"], z["xnT_psum"] + g + 1)
                    run(xnT_all[:, g * 512:(g + 1) * 512], bank(6 + g % 2), ACT.Copy).then_inc(s["xnT_sbuf"], 1)
                if l < 2:
                    for j, (c0, cn) in enumerate(chunks(FFN[l]["F"])):
                        if j == 0 and l == 1:
                            gate(l)
                        act.wait_ge(s["up_psum"], z["up_psum"] + j + 1)
                        if j >= 2:
                            act.wait_ge(s["hid_ready"], z["hid_ready"] + j - 1)
                        run(hidT_all[0:cn, j * 512:(j + 1) * 512], bank(j % 2, parts=cn), FFN[l]["act"])
                        run(hid[j % 2][0:cn, :], bank(2 + j % 2, parts=cn), ACT.Copy).then_inc(s["act_ready"], 1)
                if l == 3:
                    act.wait_ge(s["softmax_done"], 1)
                    run(r["prob"], r["prob"], ACT.Exp).then_inc(s["softmax_done"], 1)

            def shared_phase(kind, part, l, z):
                cs = chunks(FFN[l]["F"])
                C = len(cs)
                groups = group_range(kind, part)
                for g in groups:
                    for c, (c0, cn) in enumerate(cs):
                        n = g - groups[0]
                        j = n * C + c
                        h = ((n % 2) * C + c) * 512
                        act.wait_ge(s["up_psum"], z["up_psum"] + j + 1)
                        bias = {"bias": up_col[:, c:c + 1]} if kind == "dense" else {}
                        run(hidT_all[0:cn, h:h + 512], bank(j % 2, parts=cn), FFN[l]["act"], **bias)\
                            .then_inc(s["hid_ready" if kind == "dense" else "act_ready"], 1)

            def routed_phase(l, z):
                F, U = FFN[l]["F"], UNIT[l]
                n = ROUTED_TILES[l] // U
                x_T, y = ffn_inT[l], ffn_out[l]

                def normalised(t, k):
                    act.wait_ge(s["xnT_psum"], z["xnT_psum"] + t + 1)
                    run(x_T[k][:, :], bank(7, 0, U * D), ACT.Copy).then_inc(s["xnT_sbuf"], 1)

                def activate(t, k):
                    act.wait_ge(s["up_psum"], z["up_psum"] + t + 1)
                    for parts, a, b in hidden_parts(l):
                        last = run(hid[k][0:parts, a:b], bank(k, a, b, parts=parts), FFN[l]["act"])
                    last.then_inc(s["act_ready"], 1)

                def take_y(t, k, first_two):
                    act.wait_ge(s["y_psum"], z["y_psum"] + t + 1)
                    if not first_two:
                        act.wait_ge(y_stored[k], 16 * (z["y_pairs"] + (t - k) // 2) if isinstance(t, int) else 16 * z["y_pairs"] + (t - k) * 8)
                    run(y[k][:, :], bank(6, 0, U * D), ACT.Copy).then_inc(s["y_taken"], 1)

                normalised(0, 0)
                normalised(1, 1)
                activate(0, 0)

                def body(i):
                    for k in range(2):
                        t = 2 * i + k
                        if exists(t + 2, n):
                            normalised(t + 2, k)
                        if exists(t + 1, n):
                            activate(t + 1, 1 - k)
                        take_y(t, k, isinstance(t, int) and t < 2)
                pairs(act, n // 2, body)

            for no, (kind, l, sub) in enumerate(phases):
                z = at[no]
                if kind == "keys":
                    keys_phase(l, KV[l])
                elif kind == "attention":
                    attention_phase(l, z)
                elif kind == "router":
                    router_phase(l, z)
                elif kind in ("shared", "dense"):
                    shared_phase(kind, sub, l, z)
                elif kind == "routed":
                    routed_phase(l, z)
                elif kind == "stats":
                    act.wait_ge(s["fold_psum"], 1)
                    run(down_fold[:, :], bank(0), ACT.Copy)
                    run(up_col[:, :], bank(1).rearrange("p (c e) -> p c e", e=P)[:, :, 0], ACT.Copy)
                phase_end(act, no + 1)

        @block.vector
        def _(dve):
            tt, copy = nc.vector.tensor_tensor, nc.vector.tensor_copy
            links = [0]

            def link(instruction):
                links[0] += 1
                instruction.then_inc(s["dve_chain"], 1)
                dve.wait_ge(s["dve_chain"], links[0])

            def x_tile(t):
                return x[:, ds(t * D, D)]

            def normalise(t, k, out_tile=None):
                return nc.vector.tensor_scalar(xin[k][:, :] if out_tile is None else out_tile, x_tile(t),
                                               mean_var[:, ds(2 * t, 1)], rstd[:, ds(t, 1)], ALU.subtract, ALU.mult)

            def step_over(place):
                nc.vector.memset(stepped[:, place:place + 1], 0.0)

            def tile_stats(t, k, n):
                if not (isinstance(n, int) and n < 2):
                    dve.wait_ge(s["rstd_ready"], n - 1)
                step_over(2 * k)
                nc.vector.bn_stats(tile_bn[k][:, :], x_tile(t)).then_inc(s["stats_done"], 1)
                dve.wait_ge(s["stats_done"], n + 1)
                step_over(2 * k + 1)
                nc.vector.bn_aggr(tile_mv[k][:, :], tile_bn[k][:, :]).then_inc(s["mean_var_done"], 1)

            def update_x(t, k, y, gate, z):
                nc.vector.scalar_tensor_tensor(x_tile(t), y, tanh_g[:, gate:gate + 1], x_tile(t), ALU.mult, ALU.add)\
                    .then_inc(s["x_new"], 1)
                dve.wait_ge(s["x_new"], z["x_new"] + t + 1)
                if gate == 1:
                    nc.vector.bn_stats(stats[:, ds(6 * t, 6)], x_tile(t))
                else:
                    tile_stats(t, k, z["stats_done"] + t)

            def all_stats():
                for t in range(TILES):
                    last = nc.vector.bn_stats(stats[:, 6 * t:6 * t + 6], x[:, t * D:(t + 1) * D])
                return last

            def stats_phase(l, sub):
                if l == 0:
                    dve.wait_ge(s["x_loaded"], 16 * len(x_loads))
                    link(all_stats())
                for t in range(TILES):
                    last = nc.vector.bn_aggr(mean_var[:, 2 * t:2 * t + 2], stats[:, 6 * t:6 * t + 6])
                last.then_inc(s["mean_var_done"], 1)

            def keys_phase(l, z):
                if l == 2:
                    for j in range(16):
                        dve.wait_ge(s["kv_psum"], z["kv_psum"] + j + 1)
                        dst = (kT2 if j < 8 else vT2)[:, (j % 8) * BK:(j % 8 + 1) * BK]
                        nc.vector.tensor_scalar(dst, bank(j % 8, 0, BK), colk2[:, 8 + j:9 + j], None, ALU.add)\
                            .then_inc(s["kv_evac_v"], 1)
                    tt(hid[1][:, 0:128].rearrange("p (c h) -> p c h", h=16), half_head[:, :].rearrange("p (c h) -> p c h", h=16),
                       colk2[:, 0:8].rearrange("p (c h) -> p c h", h=1).to_broadcast([P, 8, 16]), ALU.mult).then_inc(s["kv_evac_v"], 1)
                    nc.vector.memset(vw[0:CHUNKS[-2] + P - CHUNKS[-1], :].rearrange("p (b c e) -> p b c e", c=NC, e=D)[:, :, NC - 1, :], 0.0)\
                        .then_inc(s["vw_zeroed"], 1)
                    dve.wait_ge(s["kv_evac_a"], 1)
                    rest = hid[0][0:16, 0:BK]
                    for part in range(3):
                        to = r_bf_parts[0:16, part * BK:(part + 1) * BK]
                        link(copy(to, rest))
                        if part < 2:
                            link(tt(rest, rest, to, ALU.subtract))
                    nc.vector.memset(stepped[:, 0:1], 0.0).then_inc(s["q_bias_parts"], 1)
                    for j in range(B * 4):
                        dve.wait_ge(s["kv_psum"], z["kv_psum"] + 17 + j + 1)
                        b, g = j // 4, j % 4
                        copy(vw_keys.rearrange("p (b f i h e) -> p b f i h e", b=B, f=2, h=2, e=D)[:, b, g // 2, :, g % 2, :],
                             bank(j % 8, parts=SK).rearrange("p (i e) -> p i e", e=D)).then_inc(s["kv_evac_v"], 1)
                    return
                if l == 1:
                    nc.vector.tensor_scalar(mask1_row[0:1, :], mask1_raw[0:1, :], 0.0, BIG_ROW, ALU.is_equal, ALU.mult)
                dve.wait_ge(s["kv_psum"], z["kv_psum"] + (2 if l == 3 else 1))
                if l == 0:
                    dve.wait_ge(s["loaded_second"], 16 * len(second_loads))
                    copy(earlier[:, :], earlier_f[:, :])
                    link(nc.vector.tensor_scalar(kT[:, :], bank(0, 0, BK), cols[:, 1:2], float(8.0 ** -0.5), ALU.add, ALU.mult))
                elif l == 1:
                    link(copy(kT[:, :], bank(0, 0, BK)))
                else:
                    rot = hid[0][:, 0:BK].rearrange("p (b k) -> p b k", k=SK)
                    k3 = kT[:, :].rearrange("p (b k) -> p b k", k=SK)
                    for table, n, o in ((rope_cos, 0, k3), (rope_sin, 1, rot)):
                        c = table[:, 0:SK].rearrange("p (b k) -> p b k", b=1).to_broadcast([P, B, SK])
                        last = tt(o, bank(n, 0, BK).rearrange("p (b k) -> p b k", k=SK), c, ALU.mult)
                    link(last)
                    link(tt(kT[:, :], kT[:, :], hid[0][:, 0:BK], ALU.add))
                    link(nc.vector.tensor_scalar(kT[:, :], kT[:, :], 0.25, None, ALU.mult))
                nc.vector.memset(stepped[:, 0:1], 0.0).then_inc(s["kT_ready"], 1)
                n, sel = (8, heads16) if l == 3 else (16, heads8)

                def key_blocks(b):
                    tt(keys[:, b * n * SK:(b + 1) * n * SK].rearrange("p (h k) -> p h k", k=SK),
                       kT[:, b * SK:(b + 1) * SK].rearrange("p (h k) -> p h k", h=1).to_broadcast([P, n, SK]),
                       sel[:, :].rearrange("p (h k) -> p h k", k=1).to_broadcast([P, n, SK]), ALU.mult)
                units, hd = ATT[l]["units"], HD[l]
                w = hd + 1
                v = values[l][:, 0:B * units * NC * HG * w].rearrange("p (b u c h w) -> p b u c h w", b=B, u=units, c=NC, w=w)
                for b in range(B):
                    if b % 2 == 0:
                        key_blocks(b // 2)
                    dve.wait_ge(s["kv_psum"], z["kv_psum"] + (2 if l == 3 else 1) + b + 1)
                    o = 2 * BANK + (b % 2) * 2 * BANK
                    from_v = psum[:, o:o + NC * D].rearrange("p (c u h w) -> p u c h w", c=NC, u=units, w=hd)
                    for u in range(units):
                        last = tt(v[:, b, u, :, :, 0:hd], from_v[:, u], row_head[:, :].rearrange("p (c h w) -> p c h w", c=NC, w=1)
                                  .to_broadcast([P, NC, HG, hd]), ALU.mult)
                    last.then_inc(s["v_taken"], 1)

            def attention_phase(l, z):
                units = ATT[l]["units"]

                def normalised(t, k, first_two):
                    if not first_two:
                        dve.wait_ge(s["xnT_psum"], z["xnT_psum"] + t - 1)
                    normalise(t, k).then_inc(s["xn_ready"], 1)

                def shift(t, h, p, first_ones):
                    u = t * units + h
                    k = p % 2
                    place = P_SLOTS[l][p]
                    dve.wait_ge(s["scores_psum"], z["scores_psum"] + u + 1)
                    src = scores(k)
                    if l == 2:
                        if h == 0:
                            dve.wait_ge(s["mask2_copied"], z["mask2_copied"] + t + 1)
                        m = mask2_tile[p // 2][:, :].rearrange("p (a h k) -> p a h k", a=1, h=1).to_broadcast([P, 2, HG // 2, SK])
                        c = masked2[:, :].rearrange("p (a h k) -> p a h k", a=1, h=1).to_broadcast([P, 2, HG // 2, SK])
                        step_over(4 + p)
                        nc.vector.copy_predicated(src, m, c).then_inc(s["scores_prep"], 1)
                        dve.wait_ge(s["scores_prep"], z["scores_prep"] + u + 1)
                    if l >= 2:
                        nc.vector.tensor_reduce(row_max[p][:, :].rearrange("p (a h) -> p a h", a=2), src, AX.X, ALU.max, negate=True)\
                            .then_inc(s["row_max_done"], 1)
                        return
                    if not first_ones:
                        dve.wait_ge(s["probsT_psum"], z["probsT_psum"] + u - len(P_SLOTS[l]) + 1)
                    if l == 1:
                        if isinstance(t, int) and t == 1 and h == 0:
                            dve.wait_ge(s["bias_loaded"], 16 * (QT - 1))
                        tt(by_head(place), src, by_head(bias1[:, ds((t % QT) * (2 * UW) + h * UW, UW)]), ALU.add)\
                            .then_inc(s["scores_prep"], 1)
                        dve.wait_ge(s["scores_prep"], z["scores_prep"] + u + 1)
                        src = by_head(place)
                    nc.vector.reduce_max(row_max[p][:, :].rearrange("p (a h) -> p a h", a=2), src, AX.X).then_inc(s["row_max_done"], 1)
                    if l == 1:
                        dve.wait_ge(s["row_max_done"], z["row_max_done"] + 2 * u + 1)
                        nc.vector.tensor_scalar(row_max[p][:, :], row_max[p][:, :], MASKED_L1, None, ALU.max).then_inc(s["row_max_done"], 1)
                        dve.wait_ge(s["row_max_done"], z["row_max_done"] + 2 * u + 2)
                        p3 = place.rearrange("p (h k) -> p h k", k=SK)
                        nc.vector.scalar_tensor_tensor(p3, p3, MASKED_L1, row_max[p][:, :].rearrange("p (h k) -> p h k", k=1)
                                                       .to_broadcast([P, HG, SK]), ALU.max, ALU.subtract).then_inc(s["scores_shifted"], 1)
                    else:
                        dve.wait_ge(s["row_max_done"], z["row_max_done"] + u + 1)
                        tt(by_head(place), src, over_keys(row_max[p][:, :]), ALU.subtract).then_inc(s["scores_shifted"], 1)

                def invert_sums(t, h, p):
                    u = t * units + h
                    dve.wait_ge(s["probs_ready"], z["probs_ready"] + u + 1)
                    nc.vector.reciprocal(row_inv[p][:, :], row_sum[p][:, :]).then_inc(s["probs_inverted"], 1)

                def rotate(t, k):
                    dve.wait_ge(s["qT_psum"], z["qT_psum"] + t + 1)
                    at_q = ds((t % QT) * P, P)
                    tt(ropeA, bank(MIX, D, 2 * D), rope_cos[:, at_q], ALU.mult).then_inc(s["rope_step"], 1)
                    tt(ropeB, bank(MIX, 2 * D, 3 * D), rope_sin[:, at_q], ALU.mult).then_inc(s["rope_step"], 1)
                    dve.wait_ge(s["rope_step"], z["rope_step"] + 2 * t + 2)
                    tt(qT[k][:, :], ropeA, ropeB, ALU.add).then_inc(s["qT_sbuf"], 1)

                def scale_out(t, k):
                    if l == 2:
                        return
                    w = HD[l] + 1
                    o = bank(OUT, 0, units * HG * w).rearrange("p (h w) -> p h w", w=w)
                    dve.wait_ge(s["out_psum"], z["out_psum"] + t + 1)
                    inv = out_inv[k][:, 0:units * HG].rearrange("p (h o) -> p h o", o=1)
                    nc.vector.reciprocal(inv, o[:, :, w - 1:w]).then_inc(s["out_inverted"], 1)
                    dve.wait_ge(s["out_inverted"], z["out_inverted"] + t + 1)
                    tt(out_n[k][:, :].rearrange("p (h w) -> p h w", w=w - 1), o[:, :, 0:w - 1],
                       inv.to_broadcast([P, units * HG, w - 1]), ALU.mult).then_inc(s["out_scaled"], 1)

                def new_x(t, k):
                    dve.wait_ge(s["proj_psum"], z["proj_psum"] + t + 1)
                    y = bank(OUT, 256, 256 + D) if l == 3 else bank(OUT if l == 2 else MIX, 0, D)
                    update_x(t, k, y, l, z)

                for t in range(2):
                    normalised(t, t, True)
                    if l == 3:
                        rotate(t, t)
                normalised(2, 0, False)
                shift(0, 0, 0, True)
                if l != 3:
                    shift(0, 1, 1, True)
                if l == 2:
                    invert_sums(0, 0, 0)

                def body(i):
                    for k in range(2):
                        t = 2 * i + k
                        early = isinstance(t, int)
                        if l == 3:
                            if exists(t + 1, TILES):
                                shift(t + 1, 0, 1 - k, early and t == 0)
                            if exists(t - 3, TILES):
                                new_x(t - 3, 1 - k)
                            if exists(t + 2, TILES):
                                rotate(t + 2, k)
                            if exists(t - 1, TILES):
                                scale_out(t - 1, 1 - k)
                            if exists(t + 3, TILES):
                                normalised(t + 3, 1 - k, False)
                        else:
                            if l != 2 and exists(t - 2, TILES):
                                new_x(t - 2, k)
                            if exists(t + 1, TILES):
                                shift(t + 1, 0, 2 - 2 * k, early and t == 0)
                            if l == 2:
                                invert_sums(t, 1, 2 * k + 1)
                            if exists(t - 1, TILES):
                                scale_out(t - 1, 1 - k)
                                if l == 2:
                                    new_x(t - 1, 1 - k)
                            if exists(t + 3, TILES):
                                normalised(t + 3, 1 - k, False)
                            if exists(t + 1, TILES):
                                shift(t + 1, 1, 3 - 2 * k, early and t == 0)
                                if l == 2:
                                    invert_sums(t + 1, 0, 2 - 2 * k)
                pairs(dve, TILES // 2, body, 2, 2)
                if l == 3:
                    new_x(TILES - 3, 1)
                elif l != 2:
                    new_x(TILES - 2, 0)
                scale_out(TILES - 1, 1)
                if l == 3:
                    new_x(TILES - 2, 0)
                new_x(TILES - 1, 1)

            def first_best(values_, hot, E):
                v = values_[:, 0:TILES * E].rearrange("p (t e) -> p t e", e=E)
                a = r["a"][:, 0:TILES * E]
                a3 = a.rearrange("p (t e) -> p t e", e=E)
                top = r_m["m3"][:, :].rearrange("p (t e) -> p t e", e=1).to_broadcast([P, TILES, E])
                link(nc.vector.reduce_max(r_m["m3"][:, :], v, AX.X))
                link(tt(a3, v, top, ALU.is_equal))
                link(tt(a, a, rc["rev"][:, 0:TILES * E], ALU.mult))
                link(nc.vector.reduce_max(r_m["m2"][:, :], a3, AX.X))
                link(tt(hot[:, 0:TILES * E].rearrange("p (t e) -> p t e", e=E), a3,
                        r_m["m2"][:, :].rearrange("p (t e) -> p t e", e=1).to_broadcast([P, TILES, E]), ALU.is_equal))

            def router_phase(l, z):
                E = FFN[l]["E"]
                W = TILES * E

                def te(ap):
                    return ap[:, 0:W].rearrange("p (t e) -> p t e", e=E)

                def et(ap):
                    return ap[:, 0:W].rearrange("p (e t) -> p e t", t=TILES)

                def t_by_e(ap):
                    return ap[:, 0:W].rearrange("p (e t) -> p t e", t=TILES)

                for t in range(TILES):
                    normalise(t, 0, xn_all[:, t * D:(t + 1) * D]).then_inc(s["xn_ready"], 1)
                if l == 2:
                    tt(brow[0:1, 3 * D:4 * D], brow[0:1, 3 * D:4 * D], brow[0:1, 4 * D:5 * D], ALU.add)
                    return
                dve.wait_ge(s["logits_psum"], z["logits_psum"] + TILES)
                link(copy(r["logit"][:, 0:W], logits_at(l)))
                first_best(r["logit"], r["hot1"], E)
                link(copy(r_m["m1"][:, :], r_m["m3"][:, :]))
                copy(r_bf[0][:, 0:W], r["hot1"][:, 0:W]).then_inc(s["hots_ready"], 1)
                if l == 3:
                    tt(te(r["prob"]), te(r["logit"]), r_m["m1"][:, :].rearrange("p (t e) -> p t e", e=1)
                       .to_broadcast([P, TILES, E]), ALU.subtract).then_inc(s["softmax_done"], 1)
                if l == 1:
                    dve.wait_ge(s["gate_ready"], 1)
                    rows3 = xn_all[:, :].rearrange("p (t e) -> p t e", e=D)
                    link(tt(rows3, rows3, r_m["kp"][:, :].rearrange("p (t e) -> p t e", e=1).to_broadcast([P, TILES, D]), ALU.mult))
                for c in range(CHOICES[l]):
                    hot, tot, scan = r[f"hot{c + 1}"], r[f"tot{c + 1}"], r[f"scan{c + 1}"]
                    if c == 1:
                        link(nc.vector.scalar_tensor_tensor(r["b"][:, 0:W], r["hot1"][:, 0:W], -3e38, r["logit"][:, 0:W], ALU.mult, ALU.add))
                        first_best(r["b"], hot, E)
                        copy(r_bf[1][:, 0:W], hot[:, 0:W]).then_inc(s["hots_ready"], 1)
                    dve.wait_ge(s["rank_psum"], HOTS[l] + c + 1)
                    link(copy(et(tot), ranks_at(l, c, True).rearrange("p (t e) -> p e t", e=E)))
                    link(nc.vector.tensor_tensor_scan(scan[:, 0:W], rc["carry"][:, 0:W], tot[:, 0:W], 0.0, ALU.mult, ALU.add))
                    link(tt(tot[:, 0:W], scan[:, 0:W], tot[:, 0:W], ALU.subtract))
                    link(tt(et(r["a"]), et(scan)[:, :, TILES - 1:TILES].to_broadcast([P, E, TILES]), et(rc["step"]), ALU.is_gt))
                    link(nc.vector.reduce_sum(r_m["nt"][:, 0:E], et(r["a"]), AX.X))
                    link(nc.vector.tensor_tensor_scan(r_m["cum"][:, 0:E], ones16[:, 0:E], r_m["nt"][:, 0:E], 0.0, ALU.mult, ALU.add))
                    link(tt(r_m["base"][:, 0:E], r_m["cum"][:, 0:E], r_m["nt"][:, 0:E], ALU.subtract))
                    link(nc.vector.tensor_scalar(r_m["base"][:, 0:E], r_m["base"][:, 0:E], float(P), None, ALU.mult))
                    link(tt(te(r["a"]), ranks_at(l, c, False).rearrange("p (t e) -> p t e", e=E), t_by_e(tot), ALU.add))
                    link(tt(r["a"][:, 0:W], r["a"][:, 0:W], hot[:, 0:W], ALU.mult))
                    link(nc.vector.reduce_sum(r_m["sr"][:, :], te(r["a"]), AX.X))
                    link(tt(te(r["a"]), te(hot), r_m["base"][:, 0:E].rearrange("p (t e) -> p t e", t=1).to_broadcast([P, TILES, E]), ALU.mult))
                    link(nc.vector.reduce_sum(r_m["pf"][:, :], te(r["a"]), AX.X))
                    link(tt(r_m["pf"][:, :], r_m["pf"][:, :], r_m["sr"][:, :], ALU.add))
                    copy(pos[c][:, :], r_m["pf"][:, :]).then_inc(s["pos_ready"], 1)
                    n = CHOICE_TILES[l]
                    of_choice = expert_f[:, c * n:(c + 1) * n]
                    over = psum[:, 5 * BANK:5 * BANK + n * E].rearrange("p (n e) -> p n e", e=E)
                    link(tt(over, r_m["cum"][:, 0:E].rearrange("p (n e) -> p n e", n=1).to_broadcast([P, n, E]),
                            slot_no[:, 0:n * E].rearrange("p (n e) -> p n e", e=E), ALU.is_le))
                    link(nc.vector.reduce_sum(of_choice, over, AX.X))
                    link(nc.vector.tensor_scalar(of_choice, of_choice, float(E - 1), None, ALU.min))
                    if l == 3:
                        w = r_m[f"w{c + 1}"]
                        link(nc.vector.tensor_scalar(r_m["kp"][:, :], r_m["sr"][:, :], float(CAPACITY), None, ALU.is_lt))
                        if c == 0:
                            dve.wait_ge(s["softmax_done"], 2)
                            link(nc.vector.reduce_sum(r_m["sum"][:, :], te(r["prob"]), AX.X))
                            link(nc.vector.reciprocal(r_m["sum"][:, :], r_m["sum"][:, :]))
                        link(tt(r["b"][:, 0:W], r["prob"][:, 0:W], hot[:, 0:W], ALU.mult))
                        link(nc.vector.reduce_sum(w[:, :], te(r["b"]), AX.X))
                        link(tt(w[:, :], w[:, :], r_m["sum"][:, :], ALU.mult))
                        link(tt(w[:, :], w[:, :], r_m["kp"][:, :], ALU.mult))
                n = ROUTED_TILES[l]
                if UNIT[l] > 1:
                    link(tt(expert_f[:, 0:n], expert_f[:, 0:n], digits[:, 0:n], ALU.mult))
                    n = n // UNIT[l]
                    link(nc.vector.reduce_sum(expert_f[:, 0:n], expert_f[:, :].rearrange("p (n u) -> p n u", u=UNIT[l]), AX.X))
                link(copy(expert_of[:, 0:n], expert_f[:, 0:n]))
                if l < 2:
                    C = len(chunks(FFN[l]["F"]))
                    cn = chunks(FFN[l]["F"])[-1][1]
                    dve.wait_ge(s["act_ready"], z["act_ready"] + C)
                    h = hidT_all[0:cn, (C - 1) * 512:C * 512]
                    tt(h, h, hid[(C - 1) % 2][0:cn, :], ALU.mult).then_inc(s["hid_ready"], 1)
                    dve.wait_ge(s["y_psum"], z["y_psum"] + 1)
                    x_group = x[:, 0:512]
                    nc.vector.scalar_tensor_tensor(x_group, bank(6), tanh_g[:, 4 + l:5 + l], x_group, ALU.mult, ALU.add)\
                        .then_inc(s["x_new"], 1)

            def shared_phase(kind, part, l, z):
                cs = chunks(FFN[l]["F"])
                C = len(cs)
                groups = group_range(kind, part)

                def new_x(g):
                    n = g - groups[0]
                    dve.wait_ge(s["y_psum"], z["y_psum"] + n + 1)
                    x_group = x[:, g * 512:(g + 1) * 512]
                    nc.vector.scalar_tensor_tensor(x_group, bank(6 + n % 2), tanh_g[:, 4 + l:5 + l], x_group, ALU.mult, ALU.add)\
                        .then_inc(s["x_new"], 1)
                    if kind == "dense":
                        dve.wait_ge(s["x_new"], z["x_new"] + n + 1)
                        for t in range(4 * g, 4 * g + 4):
                            tile_stats(t, t % 2, z["stats_done"] + t)

                def add_routed(g):
                    dve.wait_ge(gathered[g], 64 * (l + 1))
                    if g in groups:
                        dve.wait_ge(s["x_new"], z["x_new"] + g - groups[0] + 1)
                    cols_g = slice(g * 512, (g + 1) * 512)
                    link(nc.vector.scalar_tensor_tensor(x[:, cols_g], xn_all[:, cols_g], tanh_g[:, 4 + l:5 + l], x[:, cols_g], ALU.mult, ALU.add))
                    for t in range(4 * g, 4 * g + 4):
                        nc.vector.bn_stats(stats[:, 6 * t:6 * t + 6], x[:, t * D:(t + 1) * D])

                for g in groups:
                    for c, (c0, cn) in enumerate(cs):
                        n = g - groups[0]
                        j = n * C + c
                        h = ((n % 2) * C + c) * 512
                        if kind != "dense":
                            dve.wait_ge(s["act_ready"], z["act_ready"] + j + 1)
                            tt(hidT_all[0:cn, h:h + 512], hidT_all[0:cn, h:h + 512], bank(2 + j % 2, parts=cn), ALU.mult)\
                                .then_inc(s["hid_ready"], 1)
                        if c == 2 and n >= 1:
                            new_x(g - 1)
                        if kind == "shared" and part == 1 and n == 1 and c < 2:
                            add_routed(c)
                new_x(groups[-1])
                if kind == "shared" and part == 1:
                    for g in range(2, GROUPS):
                        add_routed(g)

            def routed_phase(l, z):
                n = ROUTED_TILES[l] // UNIT[l]

                def gate(t, k):
                    dve.wait_ge(s["act_ready"], z["act_ready"] + t + 1)
                    for parts, a, b in hidden_parts(l):
                        last = tt(hid[k][0:parts, a:b], hid[k][0:parts, a:b], bank(2 + k, a, b, parts=parts), ALU.mult)
                    last.then_inc(s["hid_ready"], 1)

                def weights(t, k):
                    W = 2 * FFN[l]["F"]
                    for i, e in enumerate(experts_of(dve, l, t)):
                        last = copy(up_now[k][:, i * W:(i + 1) * W], up_w[l][:, ds(e * W, W)])
                    last.then_inc(s["weights_ready"], 1)

                weights(0, 0)
                weights(1, 1)

                def body(i):
                    for k in range(2):
                        t = 2 * i + k
                        gate(t, k)
                        if exists(t + 2, n):
                            weights(t + 2, k)
                pairs(dve, n // 2, body)

            def combine_phase(l):
                for g in range(GROUPS):
                    cols_g = slice(g * 512, (g + 1) * 512)
                    dve.wait_ge(gathered[g], 64 * 4)
                    for buf, w in ((xn_all, "w1"), (keys, "w2")):
                        y3 = buf[:, cols_g].rearrange("p (t e) -> p t e", e=D)
                        link(tt(y3, y3, r_m[w][:, 4 * g:4 * g + 4].rearrange("p (t e) -> p t e", e=1).to_broadcast([P, 4, D]), ALU.mult))
                        last = nc.vector.scalar_tensor_tensor(x[:, cols_g], buf[:, cols_g], tanh_g[:, 4 + l:5 + l], x[:, cols_g], ALU.mult, ALU.add)
                        if buf is xn_all:
                            link(last)
                    last.then_inc(s["combined"], 1)

            for no, (kind, l, sub) in enumerate(phases):
                z = at[no]
                if kind == "load":
                    nc.vector.memset(zeros[:, :], 0.0).then_inc(s["zeros_set"], 1)
                    nc.vector.memset(ones_bf[:, :], 1.0)
                    nc.vector.memset(ones_row[:, :], 1.0)
                    nc.vector.memset(ones16[:, :], 1.0)
                    nc.vector.memset(minus_half[:, :], -0.5)
                    nc.vector.memset(masked2[:, :], MASKED_L2)
                elif kind == "stats":
                    stats_phase(l, sub)
                elif kind == "keys":
                    if l != 3:
                        stats_phase(l, sub)
                    keys_phase(l, KV[l])
                elif kind == "attention":
                    attention_phase(l, z)
                elif kind == "router":
                    router_phase(l, z)
                elif kind in ("shared", "dense"):
                    shared_phase(kind, sub, l, z)
                elif kind == "routed":
                    routed_phase(l, z)
                elif kind == "combine":
                    combine_phase(l)
                phase_end(dve, no + 1)

        @block.gpsimd
        def _(pool):
            tt = nc.gpsimd.tensor_tensor
            links = [0]
            loads, weight_loads = [0], [0, 0]

            def link(instruction):
                links[0] += 1
                instruction.then_inc(s["pool_chain"], 1)
                pool.wait_ge(s["pool_chain"], links[0])

            def load(dst, src):
                loads[0] += 1
                pool.dma_start(dst, src).then_inc(s["bfly_loaded"], 16)
                pool.wait_ge(s["bfly_loaded"], 16 * loads[0])

            def butterfly(src, dst_last, other, temps, weights, w_sb, rows_, stages, transposed):
                bufs = [src, other]

                def load_weights(n):
                    pool.dma_start(w_sb[n % 2], weights[stages[n], :, :, :].rearrange("(a k) i j -> a (k i j)", a=1)
                                   .to_broadcast([P, 4 * (HID // 2)])).then_inc(bfly_weights[n % 2], 16)
                load_weights(0)
                for n, stage in enumerate(stages):
                    if n + 1 < len(stages):
                        load_weights(n + 1)
                    weight_loads[n % 2] += 1
                    pool.wait_ge(bfly_weights[n % 2], 16 * weight_loads[n % 2])
                    st = 2 ** stage
                    nb = HID // (2 * st)
                    i, o = bufs[n % 2], dst_last if n == len(stages) - 1 else bufs[(n + 1) % 2]

                    def half(buf, which):
                        return buf.rearrange("p (r n h s) -> p r n h s", r=rows_, h=2, s=st)[:, :, :, which, :]

                    def weight(a, b):
                        c = 2 * b + a if transposed else 2 * a + b
                        w = w_sb[n % 2].rearrange("p (r n s c) -> p r n s c", r=1, s=st, c=4)[:, :, :, :, c]
                        return w.to_broadcast([P, rows_, nb, st]) if rows_ > 1 else w

                    def temp(k):
                        return temps[k].rearrange("p (r n s) -> p r n s", r=rows_, s=st)
                    for a in range(2):
                        tt(temp(0), half(i, 0), weight(a, 0), ALU.mult)
                        link(tt(temp(1), half(i, 1), weight(a, 1), ALU.mult))
                        link(tt(half(o, a), temp(0), temp(1), ALU.add))

            def gather(l, c, stored_pairs):
                for k in range(2):
                    pool.wait_ge(y_stored[k], 16 * stored_pairs)
                for t in range(TILES):
                    pool.indirect_dma_start((keys if c else xn_all)[:, t * D:(t + 1) * D], None, sorted_out[l][c],
                                            bass.IndirectOffsetOnAxis(ap=pos[c][:, t:t + 1], axis=0)).then_inc(gathered[t // 4], 16)

            def tile_rstd(t, k, z):
                pool.wait_ge(s["mean_var_done"], z["mean_var_done"] + t + 1)
                nc.gpsimd.tensor_copy(mean_var[:, ds(2 * t, 1)], tile_mv[k][:, 0:1])
                nc.gpsimd.tensor_scalar(tile_var[k][:, :], tile_mv[k][:, 1:2], EPS, None, ALU.add).then_inc(s["var_ready"], 1)
                pool.wait_ge(s["var_ready"], z["rstd_ready"] + t + 1)
                tt(rstd[:, ds(t, 1)], tile_var[k][:, :], minus_half[:, 0:1], ALU.pow).then_inc(s["rstd_ready"], 1)

            for no, (kind, l, sub) in enumerate(phases):
                z = at[no]
                if kind == "keys" and l == 1:
                    nc.gpsimd.tensor_copy(down_T[:, :], region_c[:, 4096:4096 + HID]).then_inc(s["down_moved"], 1)
                if kind == "stats" or (kind == "keys" and l != 3):
                    pool.wait_ge(s["mean_var_done"], z["mean_var_done"] + 1)
                    link(nc.gpsimd.tensor_scalar(var_eps[:, :], mean_var[:, :].rearrange("p (t c) -> p t c", c=2)[:, :, 1],
                                                 EPS, None, ALU.add))
                    link(tt(rstd[:, :], var_eps[:, :], minus_half[:, :], ALU.pow))
                elif kind == "routed" and l == 0:
                    load(region_c[:, 0:HID], d["L2_ffn_W_conT"])
                    result = region_c[:, 4096:4096 + HID]
                    butterfly(region_c[:, 0:HID], result, result, [region_c[:, 1024:1280], region_c[:, 1280:1536]],
                              d["L2_ffn_down_weights"], [region_c[:, 1536:2560], region_c[:, 2560:3584]], 1, list(range(STAGES))[::-1], True)
                elif kind == "attention" and l == 1:
                    a, b2, bias = region_a[:, 3584:4608], region_a[:, 4608:5632], region_a[:, 5632:6144]
                    load(a[:, 0:HID], d["L2_ffn_W_exp"])
                    load(a[:, HID:2 * HID], rows("L2_ffn_b_exp").to_broadcast([P, HID]))
                    load(bias, rows("L2_ffn_up_bias").to_broadcast([P, HID]))
                    butterfly(a, up_fold, b2, [region_a[:, 2560:3072], region_a[:, 3072:3584]], d["L2_ffn_up_weights"],
                              [region_a[:, 512:1536], region_a[:, 1536:2560]], 2, list(range(STAGES)), False)
                    link(tt(up_fold[:, HID:], up_fold[:, HID:], bias, ALU.add))
                elif kind == "dense" or (kind == "attention" and l in (0, 3)):
                    def body(i):
                        for k in range(2):
                            tile_rstd(2 * i + k, k, z)
                    pairs(pool, TILES // 2, body)
                elif kind == "attention" and l == 2:
                    def mask_copy(t, k):
                        if not (isinstance(t, int) and t < 2):
                            pool.wait_ge(s["scores_prep"], z["scores_prep"] + 2 * (t - 1))
                        nc.gpsimd.tensor_copy(mask2_tile[k][:, :], mask2[:, ds(t * SK, SK)]).then_inc(s["mask2_copied"], 1)

                    def scale_probs(t, h, p):
                        pool.wait_ge(s["probs_inverted"], z["probs_inverted"] + 2 * t + h + 1)
                        p3 = P_SLOTS[2][p].rearrange("p (h k) -> p h k", k=SK)
                        tt(p3, p3, row_inv[p][:, :].rearrange("p (h k) -> p h k", k=1).to_broadcast([P, HG, SK]), ALU.mult)\
                            .then_inc(s["probs_scaled"], 1)

                    mask_copy(0, 0)
                    mask_copy(1, 1)
                    scale_probs(0, 0, 0)

                    def body(i):
                        for k in range(2):
                            t = 2 * i + k
                            if exists(t + 2, TILES):
                                mask_copy(t + 2, k)
                            scale_probs(t, 1, 2 * k + 1)
                            if exists(t - 2, TILES):
                                tile_rstd(t - 2, k, z)
                            if exists(t + 1, TILES):
                                scale_probs(t + 1, 0, 2 - 2 * k)
                    pairs(pool, TILES // 2, body)
                    for t in range(TILES - 2, TILES):
                        tile_rstd(t, t % 2, z)
                elif kind == "router" and l < 2:
                    for j, (c0, cn) in enumerate(chunks(FFN[l]["F"])[:-1]):
                        pool.wait_ge(s["act_ready"], z["act_ready"] + j + 1)
                        h = hidT_all[0:cn, j * 512:(j + 1) * 512]
                        tt(h, h, hid[j % 2][0:cn, :], ALU.mult).then_inc(s["hid_ready"], 1)
                elif (kind == "shared" and sub == 0) or (kind == "routed" and l == 3):
                    pool.wait_ge(s["slots_zeroed"], 32)
                    for c in range(CHOICES[l]):
                        pool.wait_ge(s["pos_ready"], HOTS[l] + c + 1)
                        for t in range(TILES):
                            pool.indirect_dma_start(sorted_in[c], bass.IndirectOffsetOnAxis(ap=pos[c][:, t:t + 1], axis=0),
                                                    xn_all[:, t * D:(t + 1) * D], None).then_inc(s["scattered_second" if c else "scattered"], 16)
                    pool.wait_ge(s["phase_done"], ENGINES * no)
                    if l == 3:
                        pool.wait_ge(s["scattered_second"], 16 * TILES)
                        gather(l, 0, z["y_pairs"] + CHOICE_TILES[3] // UNIT[3] // 2)
                elif kind == "shared" and sub == 1:
                    gather(l, 0, z["y_pairs"])
                elif kind == "combine":
                    gather(l, 1, z["y_pairs"])
                if kind == "router" and l != 2:
                    pool.drain().then_inc(s["phase_done"], 1)
                else:
                    phase_end(pool, no + 1)


def kernel(**inputs):
    import numpy as _np
    import concourse.bacc as _bacc
    from concourse import mybir as _mybir
    from concourse.bass_utils import run_bass_kernel_spmd as _run

    a = {k: _np.asarray(v) for k, v in inputs.items()}
    T = lambda m: _np.ascontiguousarray(_np.swapaxes(m, -1, -2))
    keep = {"g_xattn", "g_ffn"}
    g = {k: a[k] for k in a if k in keep or (k.startswith("L") and k not in (
        "L1_xattn_Wq", "L1_xattn_Wk", "L1_xattn_Wv", "L1_xattn_Wo", "L1_xattn_rel_bias", "L2_xattn_wK_w", "L2_xattn_wV_w",
        "L2_xattn_wOut_w", "L2_ffn_W_con", "L3_xattn_Wq", "L3_xattn_Wkv", "L3_xattn_Wout"))}
    g["x"] = a["x"].reshape(TOKENS, D)
    g["ctxT"] = T(a["ctx_1024"].reshape(BK, D))
    g["ctxT_backwards"] = T(a["ctx_1024"][:, ::-1].reshape(BK, D))
    for n in ("Wq", "Wk", "Wv", "Wo"):
        g[f"L1_xattn_{n}T"] = T(a[f"L1_xattn_{n}"])
    g["rel_T"] = T(a["L1_xattn_rel_bias"])
    g["L2_xattn_WkT"], g["L2_xattn_WvT"] = T(a["L2_xattn_wK_w"]), T(a["L2_xattn_wV_w"])
    g["L2_xattn_WoT"] = T(a["L2_xattn_wOut_w"])
    g["L2_ffn_W_conT"] = T(a["L2_ffn_W_con"])
    halves = _np.arange(D).reshape(8, 2, 8)[:, ::-1, :].reshape(D)
    wk3, wv3 = a["L3_xattn_Wkv"][:D], a["L3_xattn_Wkv"][D:]
    g["L3_xattn_WqT"], g["L3_xattn_WqT_swapped"] = T(a["L3_xattn_Wq"]), T(a["L3_xattn_Wq"][halves])
    g["L3_xattn_WkT"], g["L3_xattn_WkT_swapped"] = T(wk3), T(wk3[halves])
    g["L3_xattn_WvT"], g["L3_xattn_WoT"] = T(wv3), T(a["L3_xattn_Wout"])
    g["mask1"] = _np.ascontiguousarray(a["mask_Bx1x1xS2_bk0"].reshape(B, SK)[:, ::-1]).reshape(1, BK)
    g["mask2"] = a["mask_BxSxS2_bf0"].reshape(TOKENS, SK)
    g.update(shape_constants())

    nc = _bacc.Bacc("TRN2", target_bir_lowering=False, num_devices=1)
    arrays, d = {}, {}
    for name, v in g.items():
        v = _np.ascontiguousarray(v)
        arrays[f"in_{name}"] = v
        d[name] = nc.dram_tensor(f"in_{name}", v.shape, _mybir.dt.from_np(v.dtype), kind="ExternalInput").ap()
    out = nc.dram_tensor("out_x", (TOKENS, D), _mybir.dt.float32, kind="ExternalOutput").ap()
    flamingo_kernel(nc, d, out)
    r = _run(nc, [arrays], core_ids=[0])
    return r.results[0]["out_x"].reshape(B, S, D)
```
